# Optimizing a Trainium2 kernel written in Bass

```python
import numpy as np
import jax
import jax.numpy as jnp

def _softmax(x, axis=-1):
    return jax.nn.softmax(x, axis=axis)

def _gelu(x):
    return jax.nn.gelu(x, approximate=True)

def _silu(x):
    return jax.nn.silu(x)

def _sigmoid(x):
    return jax.nn.sigmoid(x)

def _layernorm(x, axis=-1, eps=1e-05):
    m = jnp.mean(x, axis=axis, keepdims=True)
    v = jnp.var(x, axis=axis, keepdims=True)
    return (x - m) / jnp.sqrt(v + eps)

def _scatter_add(tgt, idx, src, axis=0):
    return tgt.at[idx].add(src)

def _segment_sum(src, seg, n):
    return jax.ops.segment_sum(src, seg, n)
kernel_name = 'mk_xattn_ffn_d4_seqx_r8_50a1dc'

def setup_inputs(seed: int=0):
    np.random.seed(seed)
    _w = jnp.asarray

    def _rec_inputs():
        import jax
        import jax.numpy as jnp
        _rk = jax.random.key(seed)
        x = -0.0002928 + 1 * jax.random.normal(jax.random.fold_in(_rk, 1), (8, 256, 128), jnp.float32)
        _lenS = 256 - jax.random.randint(jax.random.fold_in(_rk, 7), (8,), 0, max(1, 256 // 4) + 1, jnp.int32)
        _lenS2 = 256 - jax.random.randint(jax.random.fold_in(_rk, 8), (8,), 0, max(1, 256 // 4) + 1, jnp.int32)
        _ctx_1024P = jax.random.normal(jax.random.fold_in(_rk, 11), (8, 16, 128), jnp.float32)
        _ctx_1024c = jax.random.dirichlet(jax.random.fold_in(_rk, 511), 0.3 * jnp.ones((16,), jnp.float32), (8, 256))
        _ctx_1024t = jnp.einsum('bsk,bkd->bsd', _ctx_1024c, _ctx_1024P)
        _ctx_1024t = _ctx_1024t * jax.lax.rsqrt(jnp.mean(jnp.square(_ctx_1024t)) + 1e-12) * 0.953939
        ctx_1024 = -1.39393e-06 + 0.999914 * (_ctx_1024t + 0.3 * jax.random.normal(jax.random.fold_in(_rk, 611), (8, 256, 128), jnp.float32))
        _validS = jnp.arange(256)[None, :] < _lenS[:, None]
        _validS2 = jnp.arange(256)[None, :] < _lenS2[:, None]
        _causal = jnp.tril(jnp.ones((256, 256), dtype=bool))
        mask_1x1xSxS2_ik0 = jnp.where(jnp.broadcast_to(_validS2[0:1, None, None, :], (1, 1, 256, 256)), 0, 1).astype(jnp.int32)
        mask_BxS2_bk0 = jnp.logical_not(jnp.broadcast_to(_validS2[:, :], (8, 256)))
        return (x, ctx_1024, mask_1x1xSxS2_ik0, mask_BxS2_bk0)
    x, ctx_1024, mask_1x1xSxS2_ik0, mask_BxS2_bk0 = _rec_inputs()

    def _L0_xattn_setup():
        import math
        import jax, jax.numpy as jnp
        import numpy as np
        B, S, H, NH = (2, 256, 128, 4)
        DH = H // NH

        def _mlstm_parallel(qh, kh, vh, ig, fg, eps=1e-06):
            b, nh, s, dh = qh.shape
            log_f = jax.nn.log_sigmoid(fg)
            pcs = jnp.pad(jnp.cumsum(log_f, axis=-1), ((0, 0), (0, 0), (1, 0)))
            mat = pcs[..., :, None] - pcs[..., None, :]
            ltr = jnp.tril(jnp.ones((s, s), dtype=bool))
            log_fg_matrix = jnp.where(ltr, mat[..., 1:, 1:], -jnp.inf)
            log_D = log_fg_matrix + ig[..., None, :]
            max_log_D = jnp.max(log_D, axis=-1, keepdims=True)
            D = jnp.exp(log_D - max_log_D)
            qk = jnp.einsum('bhsd,bhtd->bhst', qh, kh) / math.sqrt(dh)
            C = qk * D
            normalizer = jnp.maximum(jnp.abs(C.sum(axis=-1, keepdims=True)), jnp.exp(-max_log_D))
            Cn = C / (normalizer + eps)
            return jnp.einsum('bhst,bhtd->bhsd', Cn, vh)
        key = jax.random.key(seed)
        ks = jax.random.split(key, 8)
        gate_std = 1.0 / math.sqrt(3 * H)
        return {'q': jax.random.normal(ks[0], (B, S, H), jnp.float32), 'k': jax.random.normal(ks[1], (B, S, H), jnp.float32), 'v': jax.random.normal(ks[2], (B, S, H), jnp.float32), 'w_igate': jax.random.normal(ks[3], (NH, 3 * H), jnp.float32) * gate_std, 'b_igate': jax.random.normal(ks[4], (NH,), jnp.float32) * 0.1, 'w_fgate': jax.random.normal(ks[5], (NH, 3 * H), jnp.float32) * gate_std, 'b_fgate': jnp.linspace(3.4, 6.0, NH, dtype=jnp.float32), 'ln_weight': jnp.zeros((H,), jnp.float32)}
    _L0_xattn_all = _L0_xattn_setup()
    _L0_xattn_in = {k: v for k, v in _L0_xattn_all.items() if k in ('w_igate', 'b_igate', 'w_fgate', 'b_fgate', 'ln_weight')}
    del _L0_xattn_all

    def _L0_ffn_setup():
        import jax, jax.numpy as jnp
        import numpy as np
        D_MODEL = 128
        D_FF = 512
        NUM_EXPERTS = 8
        key = jax.random.key(seed)
        ks = jax.random.split(key, 8)
        scale_in = 1.0 / np.sqrt(D_MODEL)
        scale_ff = 1.0 / np.sqrt(D_FF)
        x = jax.random.normal(ks[0], (4, 256, D_MODEL), dtype=jnp.float32)
        gate_w = jax.random.uniform(ks[1], (NUM_EXPERTS, D_MODEL), jnp.float32, -scale_in, scale_in)
        gate_b = jax.random.uniform(ks[2], (NUM_EXPERTS,), jnp.float32, -scale_in, scale_in)
        expert_bias = jnp.zeros((NUM_EXPERTS,), dtype=jnp.float32)
        w1 = jax.random.uniform(ks[3], (NUM_EXPERTS, D_MODEL, D_FF), jnp.float32, -scale_in, scale_in)
        b1 = jax.random.uniform(ks[4], (NUM_EXPERTS, D_FF), jnp.float32, -scale_in, scale_in)
        w2 = jax.random.uniform(ks[5], (NUM_EXPERTS, D_FF, D_MODEL), jnp.float32, -scale_ff, scale_ff)
        b2 = jax.random.uniform(ks[6], (NUM_EXPERTS, D_MODEL), jnp.float32, -scale_ff, scale_ff)
        return {'x': x, 'gate_w': gate_w, 'gate_b': gate_b, 'expert_bias': expert_bias, 'w1': w1, 'b1': b1, 'w2': w2, 'b2': b2}
    _L0_ffn_all = _L0_ffn_setup()
    _L0_ffn_in = {k: v for k, v in _L0_ffn_all.items() if k in ('gate_w', 'gate_b', 'expert_bias', 'w1', 'b1', 'w2', 'b2')}
    del _L0_ffn_all

    def _L1_xattn_setup():
        import jax, jax.numpy as jnp
        import numpy as np
        B, S, D, H = (2, 256, 128, 16)
        DK = D // H

        def _split_heads(x):
            b, s, _ = x.shape
            return x.reshape(b, s, H, DK).transpose(0, 2, 1, 3)
        key = jax.random.key(seed)
        ks = jax.random.split(key, 7)
        q = jax.random.normal(ks[0], (B, S, D), dtype=jnp.float32)
        k = jax.random.normal(ks[1], (B, S, D), dtype=jnp.float32)
        v = jax.random.normal(ks[2], (B, S, D), dtype=jnp.float32)
        mask = jnp.tril(jnp.ones((S, S), dtype=jnp.int32))[None, None, :, :]
        scale = 1.0 / np.sqrt(DK)
        W_q = jax.random.normal(ks[3], (D, D), dtype=jnp.float32) * 0.02
        W_k = jax.random.normal(ks[4], (D, D), dtype=jnp.float32) * 0.02
        W_v = jax.random.normal(ks[5], (D, D), dtype=jnp.float32) * 0.02
        W_o = jax.random.normal(ks[6], (D, D), dtype=jnp.float32) * 0.02
        return {'q': q, 'k': k, 'v': v, 'mask': mask, 'W_q': W_q, 'W_k': W_k, 'W_v': W_v, 'W_o': W_o}
    _L1_xattn_all = _L1_xattn_setup()
    _L1_xattn_in = {k: v for k, v in _L1_xattn_all.items() if k in ('W_q', 'W_k', 'W_v', 'W_o')}
    del _L1_xattn_all

    def _L1_ffn_setup():
        import jax, jax.numpy as jnp
        import numpy as np
        B, S, DIM, FFN, E = (4, 256, 128, 512, 8)
        key = jax.random.key(seed)
        k0, k1, k2, k3 = jax.random.split(key, 4)
        scale = 0.02
        return {'hidden_states': jax.random.normal(k0, (B, S, DIM), jnp.float32), 'router_w': jax.random.normal(k1, (DIM, E), jnp.float32) * scale, 'router_b': jnp.zeros((E,), jnp.float32), 'w1': jax.random.normal(k2, (E, DIM, 2 * FFN), jnp.float32) * scale, 'w2': jax.random.normal(k3, (E, FFN, DIM), jnp.float32) * scale}
    _L1_ffn_all = _L1_ffn_setup()
    _L1_ffn_in = {k: v for k, v in _L1_ffn_all.items() if k in ('router_w', 'router_b', 'w1', 'w2')}
    del _L1_ffn_all

    def _L2_xattn_setup():
        import jax, jax.numpy as jnp
        import numpy as np
        D_MODEL = 128
        NUM_HEADS = 16
        HEAD_DIM = D_MODEL // NUM_HEADS
        key = jax.random.key(seed)
        ks = jax.random.split(key, 11)
        N, S = (4, 256)
        s = 1.0 / np.sqrt(D_MODEL)
        return {'query': jax.random.normal(ks[0], (N, S, D_MODEL), jnp.float32), 'key': jax.random.normal(ks[1], (N, S, D_MODEL), jnp.float32), 'value': jax.random.normal(ks[2], (N, S, D_MODEL), jnp.float32), 'Wq': jax.random.normal(ks[3], (D_MODEL, D_MODEL), jnp.float32) * s, 'bq': jnp.zeros((D_MODEL,), jnp.float32), 'Wk': jax.random.normal(ks[4], (D_MODEL, D_MODEL), jnp.float32) * s, 'bk': jnp.zeros((D_MODEL,), jnp.float32), 'Wv': jax.random.normal(ks[5], (D_MODEL, D_MODEL), jnp.float32) * s, 'bv': jnp.zeros((D_MODEL,), jnp.float32), 'Wo': jax.random.normal(ks[6], (D_MODEL, D_MODEL), jnp.float32) * s, 'bo': jnp.zeros((D_MODEL,), jnp.float32)}
    _L2_xattn_all = _L2_xattn_setup()
    _L2_xattn_in = {k: v for k, v in _L2_xattn_all.items() if k in ('Wq', 'bq', 'Wk', 'bk', 'Wv', 'bv', 'Wo', 'bo')}
    del _L2_xattn_all

    def _L2_ffn_setup():
        import jax, jax.numpy as jnp
        import numpy as np
        HID = 128
        INTER = 512
        RDIM = 128
        HEADS = 4
        NUM_EXPERTS = 2048
        NUM_KEYS = 128
        TOPK = 8
        B, T = (2, 256)
        key = jax.random.key(seed)
        ks = jax.random.split(key, 8)
        s = lambda fan_in: 1.0 / np.sqrt(fan_in)
        return {'hidden_states': jax.random.normal(ks[0], (B, T, HID), jnp.float32), 'Wq': jax.random.normal(ks[1], (HEADS * RDIM, HID), jnp.float32) * s(HID), 'keys': jax.random.normal(ks[2], (HEADS, NUM_KEYS, 2, RDIM // 2), jnp.float32) * s(RDIM // 2), 'down_embed': jax.random.normal(ks[3], (NUM_EXPERTS, HID), jnp.float32) * 0.02, 'up_embed': jax.random.normal(ks[4], (NUM_EXPERTS, HID), jnp.float32) * 0.02, 'Wg': jax.random.normal(ks[5], (INTER, HID), jnp.float32) * s(HID), 'Wu': jax.random.normal(ks[6], (INTER, HID), jnp.float32) * s(HID), 'Wd': jax.random.normal(ks[7], (HID, INTER), jnp.float32) * s(INTER)}
    _L2_ffn_all = _L2_ffn_setup()
    _L2_ffn_in = {k: v for k, v in _L2_ffn_all.items() if k in ('Wq', 'keys', 'down_embed', 'up_embed', 'Wg', 'Wu', 'Wd')}
    del _L2_ffn_all

    def _L3_xattn_setup():
        import jax, jax.numpy as jnp
        import numpy as np
        B, LQ, LKV = (8, 128, 256)
        QDIM, KDIM, HID = (128, 128, 128)
        key = jax.random.key(seed)
        ks = jax.random.split(key, 12)
        s = lambda d: 1.0 / np.sqrt(d)
        return {'query': jax.random.normal(ks[0], (B, LQ, QDIM), jnp.float32), 'key_value': jax.random.normal(ks[1], (B, LKV, KDIM), jnp.float32), 'key_mask': jax.random.randint(ks[2], (B, LKV), 0, 2).astype(bool), 'Wq': jax.random.uniform(ks[3], (QDIM, HID), jnp.float32, -s(QDIM), s(QDIM)), 'bq': jax.random.uniform(ks[4], (HID,), jnp.float32, -s(QDIM), s(QDIM)), 'Wk': jax.random.uniform(ks[5], (KDIM, HID), jnp.float32, -s(KDIM), s(KDIM)), 'bk': jax.random.uniform(ks[6], (HID,), jnp.float32, -s(KDIM), s(KDIM)), 'Wv': jax.random.uniform(ks[7], (KDIM, HID), jnp.float32, -s(KDIM), s(KDIM)), 'bv': jax.random.uniform(ks[8], (HID,), jnp.float32, -s(KDIM), s(KDIM)), 'Wo': jax.random.uniform(ks[9], (HID, QDIM), jnp.float32, -s(HID), s(HID)), 'bo': jax.random.uniform(ks[10], (QDIM,), jnp.float32, -s(HID), s(HID))}
    _L3_xattn_all = _L3_xattn_setup()
    _L3_xattn_in = {k: v for k, v in _L3_xattn_all.items() if k in ('Wq', 'bq', 'Wk', 'bk', 'Wv', 'bv', 'Wo', 'bo')}
    del _L3_xattn_all

    def _L3_ffn_setup():
        import jax, jax.numpy as jnp
        import numpy as np
        D = 128
        H = 256
        E = 8
        K = 2
        B, T = (4, 256)
        key = jax.random.key(seed)
        ks = jax.random.split(key, 7)
        s = 0.02
        return {'x': jax.random.normal(ks[0], (B, T, D), dtype=jnp.float32), 'W1': jax.random.normal(ks[1], (E, D, 2 * H), dtype=jnp.float32) * s, 'b1': jnp.zeros((E, 2 * H), dtype=jnp.float32), 'W2': jax.random.normal(ks[2], (E, H, D), dtype=jnp.float32) * s, 'b2': jnp.zeros((E, D), dtype=jnp.float32), 'Wr': jax.random.normal(ks[3], (D, E), dtype=jnp.float32) * s, 'br': jnp.zeros((E,), dtype=jnp.float32)}
    _L3_ffn_all = _L3_ffn_setup()
    _L3_ffn_in = {k: v for k, v in _L3_ffn_all.items() if k in ('W1', 'b1', 'W2', 'b2', 'Wr', 'br')}
    del _L3_ffn_all
    return {'x': x, 'ctx_1024': ctx_1024, 'mask_1x1xSxS2_ik0': mask_1x1xSxS2_ik0, 'mask_BxS2_bk0': mask_BxS2_bk0, 'L0_xattn_w_igate': _L0_xattn_in['w_igate'], 'L0_xattn_b_igate': _L0_xattn_in['b_igate'], 'L0_xattn_w_fgate': _L0_xattn_in['w_fgate'], 'L0_xattn_b_fgate': _L0_xattn_in['b_fgate'], 'L0_xattn_ln_weight': _L0_xattn_in['ln_weight'], 'L0_ffn_gate_w': _L0_ffn_in['gate_w'], 'L0_ffn_gate_b': _L0_ffn_in['gate_b'], 'L0_ffn_expert_bias': _L0_ffn_in['expert_bias'], 'L0_ffn_w1': _L0_ffn_in['w1'], 'L0_ffn_b1': _L0_ffn_in['b1'], 'L0_ffn_w2': _L0_ffn_in['w2'], 'L0_ffn_b2': _L0_ffn_in['b2'], 'L1_xattn_W_q': _L1_xattn_in['W_q'], 'L1_xattn_W_k': _L1_xattn_in['W_k'], 'L1_xattn_W_v': _L1_xattn_in['W_v'], 'L1_xattn_W_o': _L1_xattn_in['W_o'], 'L1_ffn_router_w': _L1_ffn_in['router_w'], 'L1_ffn_router_b': _L1_ffn_in['router_b'], 'L1_ffn_w1': _L1_ffn_in['w1'], 'L1_ffn_w2': _L1_ffn_in['w2'], 'L2_xattn_Wq': _L2_xattn_in['Wq'], 'L2_xattn_bq': _L2_xattn_in['bq'], 'L2_xattn_Wk': _L2_xattn_in['Wk'], 'L2_xattn_bk': _L2_xattn_in['bk'], 'L2_xattn_Wv': _L2_xattn_in['Wv'], 'L2_xattn_bv': _L2_xattn_in['bv'], 'L2_xattn_Wo': _L2_xattn_in['Wo'], 'L2_xattn_bo': _L2_xattn_in['bo'], 'L2_ffn_Wq': _L2_ffn_in['Wq'], 'L2_ffn_keys': _L2_ffn_in['keys'], 'L2_ffn_down_embed': _L2_ffn_in['down_embed'], 'L2_ffn_up_embed': _L2_ffn_in['up_embed'], 'L2_ffn_Wg': _L2_ffn_in['Wg'], 'L2_ffn_Wu': _L2_ffn_in['Wu'], 'L2_ffn_Wd': _L2_ffn_in['Wd'], 'L3_xattn_Wq': _L3_xattn_in['Wq'], 'L3_xattn_bq': _L3_xattn_in['bq'], 'L3_xattn_Wk': _L3_xattn_in['Wk'], 'L3_xattn_bk': _L3_xattn_in['bk'], 'L3_xattn_Wv': _L3_xattn_in['Wv'], 'L3_xattn_bv': _L3_xattn_in['bv'], 'L3_xattn_Wo': _L3_xattn_in['Wo'], 'L3_xattn_bo': _L3_xattn_in['bo'], 'L3_ffn_W1': _L3_ffn_in['W1'], 'L3_ffn_b1': _L3_ffn_in['b1'], 'L3_ffn_W2': _L3_ffn_in['W2'], 'L3_ffn_b2': _L3_ffn_in['b2'], 'L3_ffn_Wr': _L3_ffn_in['Wr'], 'L3_ffn_br': _L3_ffn_in['br']}

def reference(x, ctx_1024, mask_1x1xSxS2_ik0, mask_BxS2_bk0, L0_xattn_w_igate, L0_xattn_b_igate, L0_xattn_w_fgate, L0_xattn_b_fgate, L0_xattn_ln_weight, L0_ffn_gate_w, L0_ffn_gate_b, L0_ffn_expert_bias, L0_ffn_w1, L0_ffn_b1, L0_ffn_w2, L0_ffn_b2, L1_xattn_W_q, L1_xattn_W_k, L1_xattn_W_v, L1_xattn_W_o, L1_ffn_router_w, L1_ffn_router_b, L1_ffn_w1, L1_ffn_w2, L2_xattn_Wq, L2_xattn_bq, L2_xattn_Wk, L2_xattn_bk, L2_xattn_Wv, L2_xattn_bv, L2_xattn_Wo, L2_xattn_bo, L2_ffn_Wq, L2_ffn_keys, L2_ffn_down_embed, L2_ffn_up_embed, L2_ffn_Wg, L2_ffn_Wu, L2_ffn_Wd, L3_xattn_Wq, L3_xattn_bq, L3_xattn_Wk, L3_xattn_bk, L3_xattn_Wv, L3_xattn_bv, L3_xattn_Wo, L3_xattn_bo, L3_ffn_W1, L3_ffn_b1, L3_ffn_W2, L3_ffn_b2, L3_ffn_Wr, L3_ffn_br):
    import jax
    import jax.numpy as jnp

    def _L0_xattn_ref(q, k, v, w_igate, b_igate, w_fgate, b_fgate, ln_weight):
        import math
        import jax, jax.numpy as jnp
        import numpy as np
        B, S, H, NH = (2, 256, 128, 4)
        DH = H // NH

        def _mlstm_parallel(qh, kh, vh, ig, fg, eps=1e-06):
            b, nh, s, dh = qh.shape
            log_f = jax.nn.log_sigmoid(fg)
            pcs = jnp.pad(jnp.cumsum(log_f, axis=-1), ((0, 0), (0, 0), (1, 0)))
            mat = pcs[..., :, None] - pcs[..., None, :]
            ltr = jnp.tril(jnp.ones((s, s), dtype=bool))
            log_fg_matrix = jnp.where(ltr, mat[..., 1:, 1:], -jnp.inf)
            log_D = log_fg_matrix + ig[..., None, :]
            max_log_D = jnp.max(log_D, axis=-1, keepdims=True)
            D = jnp.exp(log_D - max_log_D)
            qk = jnp.einsum('bhsd,bhtd->bhst', qh, kh) / math.sqrt(dh)
            C = qk * D
            normalizer = jnp.maximum(jnp.abs(C.sum(axis=-1, keepdims=True)), jnp.exp(-max_log_D))
            Cn = C / (normalizer + eps)
            return jnp.einsum('bhst,bhtd->bhsd', Cn, vh)
        b, s, h = q.shape
        nh = b_igate.shape[0]
        dh = h // nh
        gin = jnp.concatenate([q, k, v], axis=-1)
        ig = jnp.einsum('bsd,hd->bhs', gin, w_igate) + b_igate[None, :, None]
        fg = jnp.einsum('bsd,hd->bhs', gin, w_fgate) + b_fgate[None, :, None]
        qh = q.reshape(b, s, nh, dh).transpose(0, 2, 1, 3)
        kh = k.reshape(b, s, nh, dh).transpose(0, 2, 1, 3)
        vh = v.reshape(b, s, nh, dh).transpose(0, 2, 1, 3)
        hst = _mlstm_parallel(qh, kh, vh, ig, fg)
        mean = hst.mean(axis=-1, keepdims=True)
        var = hst.var(axis=-1, keepdims=True)
        hn = (hst - mean) / jnp.sqrt(var + 1e-05)
        scale = (1.0 + ln_weight).reshape(nh, dh)
        hn = hn * scale[None, :, None, :]
        return hn.transpose(0, 2, 1, 3).reshape(b, s, h)

    def _L0_ffn_ref(x, gate_w, gate_b, expert_bias, w1, b1, w2, b2):
        import jax, jax.numpy as jnp
        import numpy as np
        D_MODEL = 128
        D_FF = 512
        NUM_EXPERTS = 8
        gate_logits = jnp.einsum('bsd,ed->bse', x, gate_w) + gate_b + expert_bias
        top_idx = jnp.argmax(gate_logits, axis=-1)
        out = jnp.zeros_like(x)
        for e in range(NUM_EXPERTS):
            mask = (top_idx == e)[..., None].astype(x.dtype)
            h = jax.nn.relu(jnp.einsum('bsd,df->bsf', x, w1[e]) + b1[e])
            y = jnp.einsum('bsf,fd->bsd', h, w2[e]) + b2[e]
            out = out + mask * y
        return out

    def _L1_xattn_ref(q, k, v, mask, W_q, W_k, W_v, W_o):
        import jax, jax.numpy as jnp
        import numpy as np
        B, S, D, H = (2, 256, 128, 16)
        DK = D // H

        def _split_heads(x):
            b, s, _ = x.shape
            return x.reshape(b, s, H, DK).transpose(0, 2, 1, 3)
        qh = _split_heads(q @ W_q.T)
        kh = _split_heads(k @ W_k.T)
        vh = _split_heads(v @ W_v.T)
        scores = jnp.einsum('bhqd,bhkd->bhqk', qh, kh) / np.sqrt(DK)
        scores = jnp.where(mask == 0, jnp.float32(-1000000000.0), scores)
        attn = jax.nn.softmax(scores, axis=-1)
        out = jnp.einsum('bhqk,bhkd->bhqd', attn, vh)
        out = out.transpose(0, 2, 1, 3).reshape(q.shape[0], q.shape[1], D)
        return out @ W_o.T

    def _L1_ffn_ref(hidden_states, router_w, router_b, w1, w2):
        import jax, jax.numpy as jnp
        import numpy as np
        B, S, DIM, FFN, E = (4, 256, 128, 512, 8)
        b, s, d = hidden_states.shape
        x = hidden_states.reshape(-1, d)
        logits = x @ router_w + router_b
        route = jax.nn.softmax(logits, axis=1)
        max_prob = jnp.max(route, axis=1, keepdims=True)
        max_ind = jnp.argmax(route, axis=1)
        out = jnp.zeros_like(x)
        num_experts = w1.shape[0]
        for e in range(num_experts):
            h = x @ w1[e]
            a, g = jnp.split(h, 2, axis=1)
            y = jax.nn.silu(a) * g @ w2[e]
            out = jnp.where((max_ind == e)[:, None], y, out)
        out = out * max_prob
        return out.reshape(b, s, d)

    def _L2_xattn_ref(query, key, value, Wq, bq, Wk, bk, Wv, bv, Wo, bo):
        import jax, jax.numpy as jnp
        import numpy as np
        D_MODEL = 128
        NUM_HEADS = 16
        HEAD_DIM = D_MODEL // NUM_HEADS
        N, Q, _ = query.shape
        K = key.shape[1]
        q = (query @ Wq.T + bq).reshape(N, Q, NUM_HEADS, HEAD_DIM)
        k = (key @ Wk.T + bk).reshape(N, K, NUM_HEADS, HEAD_DIM)
        v = (value @ Wv.T + bv).reshape(N, K, NUM_HEADS, HEAD_DIM)
        scores = jnp.einsum('nqhd,nkhd->nhqk', q, k)
        attn = jax.nn.softmax(scores, axis=3)
        out = jnp.einsum('nhqk,nkhd->nqhd', attn, v).reshape(N, Q, D_MODEL)
        return out @ Wo.T + bo

    def _L2_ffn_ref(hidden_states, Wq, keys, down_embed, up_embed, Wg, Wu, Wd):
        import jax, jax.numpy as jnp
        import numpy as np
        HID = 128
        INTER = 512
        RDIM = 128
        HEADS = 4
        NUM_EXPERTS = 2048
        NUM_KEYS = 128
        TOPK = 8
        B, T = (2, 256)
        b, t, _ = hidden_states.shape
        q = hidden_states @ Wq.T
        q = q.reshape(b, t, 2, HEADS, RDIM // 2)
        q = jnp.transpose(q, (2, 0, 1, 3, 4))
        sim = jnp.einsum('pbthn,hkpn->pbthk', q, keys)
        sx, ix = jax.lax.top_k(sim[0], TOPK)
        sy, iy = jax.lax.top_k(sim[1], TOPK)
        all_scores = (sx[..., :, None] + sy[..., None, :]).reshape(b, t, HEADS, TOPK * TOPK)
        all_indices = (ix[..., :, None] * NUM_KEYS + iy[..., None, :]).reshape(b, t, HEADS, TOPK * TOPK)
        scores, pk = jax.lax.top_k(all_scores, TOPK)
        indices = jnp.take_along_axis(all_indices, pk, axis=-1)
        down = down_embed[indices]
        up = up_embed[indices]
        w = jnp.einsum('btd,bthkd->bthk', hidden_states, down)
        w = jax.nn.silu(w) * jax.nn.softmax(scores, axis=-1)
        experts_states = jnp.einsum('bthk,bthkd->btd', w, up)
        mlp = jax.nn.silu(hidden_states @ Wg.T) * (hidden_states @ Wu.T) @ Wd.T
        return mlp + experts_states

    def _L3_xattn_ref(query, key_value, key_mask, Wq, bq, Wk, bk, Wv, bv, Wo, bo):
        import jax, jax.numpy as jnp
        import numpy as np
        B, LQ, LKV = (8, 128, 256)
        QDIM, KDIM, HID = (128, 128, 128)
        Q = query @ Wq + bq
        K = key_value @ Wk + bk
        V = key_value @ Wv + bv
        hid = Q.shape[-1]
        scores = jnp.einsum('bqh,bkh->bqk', Q, K) / jnp.sqrt(jnp.float32(hid))
        scores = jnp.where(key_mask[:, None, :], scores, jnp.float32(-1000000000.0))
        attn = jax.nn.softmax(scores, axis=-1)
        context = jnp.einsum('bqk,bkh->bqh', attn, V)
        return context @ Wo + bo

    def _L3_ffn_ref(x, W1, b1, W2, b2, Wr, br):
        import jax, jax.numpy as jnp
        import numpy as np
        D = 128
        H = 256
        E = 8
        K = 2
        B, T = (4, 256)
        Bb, Tt, Dd = x.shape
        xf = x.reshape(-1, Dd)
        logits = xf @ Wr + br
        topk_val, topk_idx = jax.lax.top_k(logits, K)
        scores = jax.nn.softmax(topk_val, axis=-1)
        h = jnp.einsum('nd,edh->enh', xf, W1) + b1[:, None, :]
        a, g = jnp.split(h, 2, axis=-1)
        act = jax.nn.silu(a) * g
        out_e = jnp.einsum('enh,ehd->end', act, W2) + b2[:, None, :]
        out_ne = out_e.transpose(1, 0, 2)
        gathered = jnp.take_along_axis(out_ne, topk_idx[:, :, None], axis=1)
        out = jnp.sum(gathered * scores[:, :, None], axis=1)
        return out.reshape(Bb, Tt, Dd)
    x = x + _L0_xattn_ref(_layernorm(x, axis=-1), ctx_1024, ctx_1024, L0_xattn_w_igate, L0_xattn_b_igate, L0_xattn_w_fgate, L0_xattn_b_fgate, L0_xattn_ln_weight)
    x = x + _L0_ffn_ref(_layernorm(x, axis=-1), L0_ffn_gate_w, L0_ffn_gate_b, L0_ffn_expert_bias, L0_ffn_w1, L0_ffn_b1, L0_ffn_w2, L0_ffn_b2)
    x = x + _L1_xattn_ref(_layernorm(x, axis=-1), ctx_1024, ctx_1024, mask_1x1xSxS2_ik0, L1_xattn_W_q, L1_xattn_W_k, L1_xattn_W_v, L1_xattn_W_o)
    x = x + _L1_ffn_ref(_layernorm(x, axis=-1), L1_ffn_router_w, L1_ffn_router_b, L1_ffn_w1, L1_ffn_w2)
    x = x + _L2_xattn_ref(_layernorm(x, axis=-1), ctx_1024, ctx_1024, L2_xattn_Wq, L2_xattn_bq, L2_xattn_Wk, L2_xattn_bk, L2_xattn_Wv, L2_xattn_bv, L2_xattn_Wo, L2_xattn_bo)
    x = x + _L2_ffn_ref(_layernorm(x, axis=-1), L2_ffn_Wq, L2_ffn_keys, L2_ffn_down_embed, L2_ffn_up_embed, L2_ffn_Wg, L2_ffn_Wu, L2_ffn_Wd)
    x = x + _L3_xattn_ref(_layernorm(x, axis=-1), ctx_1024, mask_BxS2_bk0, L3_xattn_Wq, L3_xattn_bq, L3_xattn_Wk, L3_xattn_bk, L3_xattn_Wv, L3_xattn_bv, L3_xattn_Wo, L3_xattn_bo)
    x = x + _L3_ffn_ref(_layernorm(x, axis=-1), L3_ffn_W1, L3_ffn_b1, L3_ffn_W2, L3_ffn_b2, L3_ffn_Wr, L3_ffn_br)
    return x

_drawn_inputs = setup_inputs


def setup_inputs(seed=0):
    import zlib

    import numpy as np

    out = dict(_drawn_inputs(seed))
    spreads = {'L0_xattn_ln_weight': (0.0, 0.1),
     'L0_ffn_expert_bias': (0.0, 0.1),
     'L1_ffn_router_b': (0.0, 0.8),
     'L2_xattn_bq': (0.0, 0.1),
     'L2_xattn_bk': (0.0, 2.0),
     'L2_xattn_bv': (0.0, 0.1),
     'L2_xattn_bo': (0.0, 0.1),
     'L3_ffn_b1': (0.0, 0.8),
     'L3_ffn_b2': (0.0, 0.8),
     'L3_ffn_br': (0.0, 0.351)}
    factors = {'L0_xattn_b_igate': 53.265,
     'L0_ffn_b1': 4.346,
     'L0_ffn_b2': 3.434,
     'L1_xattn_W_q': 8.0,
     'L1_xattn_W_k': 8.0,
     'L1_xattn_W_v': 3.368,
     'L1_xattn_W_o': 3.471,
     'L1_ffn_router_w': 8.0,
     'L1_ffn_w1': 8.0,
     'L1_ffn_w2': 8.0,
     'L2_ffn_Wq': 8.0,
     'L2_ffn_keys': 8.0,
     'L2_ffn_down_embed': 8.0,
     'L2_ffn_up_embed': 8.0,
     'L3_xattn_Wq': 4.132,
     'L3_xattn_bq': 8.0,
     'L3_xattn_Wk': 4.147,
     'L3_xattn_bk': 64.0,
     'L3_xattn_bv': 3.265,
     'L3_ffn_W1': 8.0,
     'L3_ffn_W2': 8.0}
    for name, (base, spread) in spreads.items():
        noise = np.random.default_rng([zlib.crc32(name.encode()), seed]).standard_normal(out[name].shape)
        drawn = base * np.exp(spread * noise) if base else spread * noise
        out[name] = jnp.asarray(drawn.astype(out[name].dtype))
    for name, factor in factors.items():
        out[name] = (out[name] * factor).astype(out[name].dtype)
    return out
```

```python
import numpy as np

import concourse.bass as bass
import concourse.mybir as mybir

F32 = mybir.dt.float32
F32R = mybir.dt.float32r
BF16 = mybir.dt.bfloat16
I32 = mybir.dt.int32
U32 = mybir.dt.uint32
U8 = mybir.dt.uint8
ALU = mybir.AluOpType
ACT = mybir.ActivationFunctionType
AX = mybir.AxisListType

P = 128
D = 128
B = 8
S = 256
TB = S // P
NT = B * TB
LN_EPS = 1e-5


class Memory:

    carried = None
    used = []
    scattered = None
    gathered = []
    rounds = 0

    def __init__(self, nc, stack, prefix):
        self.nc, self.stack, self.prefix = nc, stack, prefix

    def sbuf(self, name, shape, dtype=F32):
        return self.stack.enter_context(self.nc.sbuf_tensor(f"{self.prefix}_{name}", shape, dtype))

    def psum(self, name, shape, dtype=F32):
        return self.stack.enter_context(self.nc.psum_tensor(f"{self.prefix}_{name}", shape, dtype))

    def sem(self, name):
        sem = self.stack.enter_context(self.nc.semaphore(f"{self.prefix}_{name}"))
        Memory.used.append(sem)
        return sem


def apart(engine):
    engine.sem_inc(Memory.carried, 1)


def clear_semaphores(nc):
    with nc.Block() as block:
        @block.gpsimd
        def _(pool):
            for sem in Memory.used:
                pool.sem_clear(sem)
    Memory.used = []


class Steps:

    def __init__(self, engine, sem, turn=0, per_turn=0):
        self.engine, self.sem, self.base, self.n, self.per_turn = engine, sem, turn * per_turn, 0, per_turn

    def step(self, instruction):
        instruction.then_inc(self.sem, 1)
        self.n += 1

    def settle(self):
        self.engine.wait_ge(self.sem, self.base + self.n)

    def link(self, instruction):
        self.step(instruction)
        self.settle()

    def close(self):
        assert not self.per_turn or self.n == self.per_turn, (self.n, self.per_turn)


class NormBuffers:

    def __init__(self, mem):
        self.stats = mem.sbuf("ln_stats", [P, TB, 6])
        self.mean_var = mem.sbuf("ln_mean_var", [P, TB, 2])
        self.var_eps = mem.sbuf("ln_var_eps", [P, TB])
        self.rstd = mem.sbuf("ln_rstd", [P, TB])
        self.power = mem.sbuf("ln_power", [P, TB])
        self.power_set = mem.sem("ln_power_set")
        self.moments_ready = mem.sem("ln_moments_ready")
        self.rstd_ready = mem.sem("ln_rstd_ready")
        self.ready = mem.sem("ln_ready")

NORM_STEPS = 4


def norm_vector(nc, dve, steps, nb, x, b, out):
    for t in range(TB):
        steps.step(nc.vector.bn_stats(nb.stats[:, t, :], x[:, bass.ds(b * TB + t, 1), :]))
    steps.settle()
    apart(dve)
    steps.step(nc.vector.bn_aggr(nb.mean_var[:, 0, :], nb.stats[:, 0, :]))
    nc.vector.bn_aggr(nb.mean_var[:, 1, :], nb.stats[:, 1, :]).then_inc(nb.moments_ready, 1)
    dve.wait_ge(nb.rstd_ready, b * 2 + 2)
    steps.step(nc.vector.tensor_scalar(out=out[:, 0, :], in0=x[:, bass.ds(b * TB, 1), :],
                                       scalar1=nb.mean_var[:, 0, 0:1], scalar2=nb.rstd[:, 0:1],
                                       op0=ALU.subtract, op1=ALU.mult))
    nc.vector.tensor_scalar(out=out[:, 1, :], in0=x[:, bass.ds(b * TB + 1, 1), :],
                            scalar1=nb.mean_var[:, 1, 0:1], scalar2=nb.rstd[:, 1:2],
                            op0=ALU.subtract, op1=ALU.mult).then_inc(nb.ready, 1)
    dve.wait_ge(nb.ready, b + 1)


def norm_power_set(nc, pool, nb):
    nc.gpsimd.memset(nb.power[:], -0.5).then_inc(nb.power_set, 1)
    pool.wait_ge(nb.power_set, 1)


def norm_gpsimd(nc, pool, nb, b):
    pool.wait_ge(nb.moments_ready, b + 1)
    apart(pool)
    nc.gpsimd.tensor_scalar(out=nb.var_eps[:], in0=nb.mean_var[:, :, 1], scalar1=LN_EPS, scalar2=None,
                            op0=ALU.add).then_inc(nb.rstd_ready, 1)
    pool.wait_ge(nb.rstd_ready, b * 2 + 1)
    nc.gpsimd.tensor_tensor(nb.rstd[:], nb.var_eps[:], nb.power[:], ALU.pow).then_inc(nb.rstd_ready, 1)



MH = 4
MD = D // MH
BH = MH * B
MSCALE = 1.0 / MD ** 0.5


def mlstm_gates(nc, a, x, ident, xn_t, cols):
    g_col, e_col, neg_g_row = cols
    from contextlib import ExitStack
    with ExitStack() as stack:
        mem = Memory(nc, stack, "m0")
        nb = NormBuffers(mem)
        xn = mem.sbuf("xn", [P, 2, TB, D])
        ctx_t = mem.sbuf("ctx_t", [P, B, S])
        w_gates = mem.sbuf("w_gates", [P, 3, 36])
        b_gates = mem.sbuf("b_gates", [BH, 2])
        gates = mem.sbuf("gates", [36, B, S])
        i_rows = mem.sbuf("i_rows", [BH, S])
        f_rows = mem.sbuf("f_rows", [BH, S])
        abs_f = mem.sbuf("abs_f", [BH, S])
        exp_f = mem.sbuf("exp_f", [BH, S])
        ln_f = mem.sbuf("ln_f", [BH, S])
        log_f = mem.sbuf("log_f", [BH, S])
        ones = mem.sbuf("ones", [BH, S])
        f_sum = mem.sbuf("f_sum", [BH, S])
        g_rows = mem.sbuf("g_rows", [BH, S])
        g_max = mem.sbuf("g_max", [BH, S])
        neg_g = mem.sbuf("neg_g", [BH, S])
        top = mem.sbuf("top", [BH, S])
        t_ps = mem.psum("t_ps", [P, 2, 512])
        gate_ps = mem.psum("gate_ps", [36, 2, 512])
        col_ps = mem.psum("col_ps", [P, 512])

        const_in = mem.sem("const_in")
        transposed = mem.sem("transposed")
        xn_t_ready = mem.sem("xn_t_ready")
        projected = mem.sem("projected")
        gates_ready = mem.sem("gates_ready")
        rows_in = mem.sem("rows_in")
        steps_done = mem.sem("steps_done")
        row_steps = mem.sem("row_steps")
        abs_ready = mem.sem("abs_ready")
        exp_ready = mem.sem("exp_ready")
        log_ready = mem.sem("log_ready")
        scans_ready = mem.sem("scans_ready")
        cols_ready = mem.sem("cols_ready")
        cols_out = mem.sem("cols_out")
        row_out = mem.sem("row_out")
        block = stack.enter_context(nc.Block())

        @block.sync
        def _(sync):
            sync.dma_start(w_gates[:], a["w_gates"]).then_inc(const_in, 16)
            sync.dma_start(b_gates[:], a["b_gates"]).then_inc(const_in, 16)
            sync.dma_start(ctx_t[:], a["ctx_t"]).then_inc(const_in, 16)
            sync.wait_ge(gates_ready, B + 2)
            for h in range(MH):
                for rows, at in ((f_rows, 32 + h), (i_rows, h)):
                    sync.dma_start(rows[h * B:(h + 1) * B, :], gates[at:at + 1, :, :]).then_inc(rows_in, 16)
            sync.wait_ge(scans_ready, 2)
            sync.dma_start(neg_g_row[0:1, :].rearrange("o (r s) -> o r s", s=S),
                           neg_g[:, :]).then_inc(row_out, 16)
            sync.wait_ge(row_out, 16)

        @block.gpsimd
        def _(pool):
            norm_power_set(nc, pool, nb)
            with pool.Fori(0, B) as b:
                norm_gpsimd(nc, pool, nb, b)

        @block.vector
        def _(dve):
            nc.vector.memset(ones[:], 1.0).then_inc(row_steps, 1)
            with dve.Fori(0, B // 2) as i:
                for j in range(2):
                    b = i * 2 + j
                    steps = Steps(dve, steps_done, b, NORM_STEPS)
                    dve.wait_ge(transposed, b + 1)
                    norm_vector(nc, dve, steps, nb, x, b, xn[:, j])
                    steps.close()
            dve.wait_ge(rows_in, 2 * MH * 16)
            rows = Steps(dve, row_steps)
            rows.n = 1
            rows.link(nc.vector.tensor_scalar(out=f_rows[:], in0=f_rows[:], scalar1=b_gates[:, 1:2],
                                              scalar2=None, op0=ALU.add))
            nc.vector.scalar_tensor_tensor(out=abs_f[:], in0=f_rows[:], scalar=-1.0, in1=f_rows[:],
                                           op0=ALU.mult, op1=ALU.max).then_inc(abs_ready, 1)
            dve.wait_ge(log_ready, 1)
            rows.link(nc.vector.scalar_tensor_tensor(out=log_f[:], in0=f_rows[:], scalar=0.0, in1=ln_f[:],
                                                     op0=ALU.min, op1=ALU.subtract))
            rows.link(nc.vector.tensor_tensor_scan(f_sum[:], ones[:], log_f[:], 0.0, ALU.mult, ALU.add))
            rows.link(nc.vector.scalar_tensor_tensor(out=g_rows[:], in0=i_rows[:], scalar=b_gates[:, 0:1],
                                                     in1=f_sum[:], op0=ALU.add, op1=ALU.subtract))
            rows.link(nc.vector.tensor_tensor_scan(g_max[:], g_rows[:], g_rows[:], -3e38, ALU.max, ALU.max))
            nc.vector.tensor_tensor(top[:], f_sum[:], g_max[:], ALU.add).then_inc(scans_ready, 1)
            nc.vector.tensor_scalar(out=neg_g[:], in0=g_max[:], scalar1=-1.0, scalar2=None,
                                    op0=ALU.mult).then_inc(scans_ready, 1)

        @block.tensor
        def _(pe):
            pe.wait_ge(const_in, 48)
            pe.sem_inc(transposed, 2)
            with pe.Fori(0, B // 2) as i:
                for j in range(2):
                    b = i * 2 + j
                    pe.wait_ge(nb.ready, b + 1)
                    pe.wait_ge(xn_t_ready, b + 1)
                    for t in range(TB):
                        last = nc.tensor.transpose(t_ps[:, j, t * P:(t + 1) * P], xn[:, j, t, :], ident[:])
                    last.then_inc(transposed, 1)
                    pe.wait_ge(gates_ready, b + 1)
                    pe.wait_ge(xn_t_ready, b + 3)
                    nc.tensor.matmul(gate_ps[:, j, 0:S], w_gates[:, 0, :], xn_t[:, bass.ds(b * S, S)],
                                     start=True, stop=False)
                    nc.tensor.matmul(gate_ps[:, j, 0:S], w_gates[:, 1, :], ctx_t[:, bass.ds(b, 1), :],
                                     start=False, stop=False)
                    nc.tensor.matmul(gate_ps[:, j, 0:S], w_gates[:, 2, :], ctx_t[:, bass.ds(b, 1), :],
                                     start=False, stop=True).then_inc(projected, 1)
            pe.wait_ge(scans_ready, 1)
            for n, rows in enumerate((g_rows, top)):
                for t in range(TB):
                    last = nc.tensor.transpose(col_ps[:, (n * TB + t) * BH:(n * TB + t + 1) * BH],
                                               rows[:, t * P:(t + 1) * P], ident[0:BH, 0:BH])
            last.then_inc(cols_ready, 1)

        @block.scalar
        def _(act):
            act.sem_inc(xn_t_ready, 2)
            act.sem_inc(gates_ready, 2)
            with act.Fori(0, B // 2) as i:
                for j in range(2):
                    b = i * 2 + j
                    act.wait_ge(transposed, b + 3)
                    nc.scalar.activation(xn_t[:, bass.ds(b * S, S)], t_ps[:, j, 0:S], ACT.Copy).then_inc(xn_t_ready, 1)
                    act.wait_ge(projected, b + 1)
                    nc.scalar.activation(gates[:, bass.ds(b, 1), :], gate_ps[:, j, 0:S], ACT.Copy).then_inc(gates_ready, 1)
            act.wait_ge(abs_ready, 1)
            nc.scalar.activation(exp_f[:], abs_f[:], ACT.Exp, scale=-1.0).then_inc(exp_ready, 1)
            act.wait_ge(exp_ready, 1)
            nc.scalar.activation(ln_f[:], exp_f[:], ACT.Ln, bias=1.0).then_inc(log_ready, 1)
            act.wait_ge(cols_ready, 1)
            nc.scalar.activation(g_col[:].rearrange("p t r -> p (t r)"), col_ps[:, 0:TB * BH],
                                 ACT.Copy).then_inc(cols_out, 1)
            nc.scalar.activation(e_col[:].rearrange("p t r -> p (t r)"), col_ps[:, TB * BH:2 * TB * BH],
                                 ACT.Exp, scale=-1.0).then_inc(cols_out, 1)
            act.wait_ge(cols_out, 2)


def mlstm_attention(nc, a, x, xn_t, cols):
    g_col, e_col, neg_g_row = cols
    W = S + P
    from contextlib import ExitStack
    with ExitStack() as stack:
        mem = Memory(nc, stack, "m1")
        ctx_t = mem.sbuf("ctx_t", [P, 2, S])
        q_t = mem.sbuf("q_t", [P, 2, S])
        v_one = mem.sbuf("v_one", [P, 2, TB, MH, MD + 1])
        causal = mem.sbuf("causal", [P, S])
        ln_scale = mem.sbuf("ln_scale", [P, D])
        ones = mem.sbuf("ones", [1, P])
        g_now = mem.sbuf("g_now", [P, 2, TB, MH])
        e_now = mem.sbuf("e_now", [P, TB, MH])
        d_arg = mem.sbuf("d_arg", [P, 2, MH, W])
        d_exp = mem.sbuf("d_exp", [P, 2, MH, W])
        c = mem.sbuf("c", [P, 2, MH, W])
        den = mem.sbuf("den", [P, TB * MH, 1])
        h = mem.sbuf("h", [P, TB * MH, MD])
        sq = mem.sbuf("sq", [P, TB * MH, MD])
        mean = mem.sbuf("mean", [P, TB * MH])
        var = mem.sbuf("var", [P, TB * MH])
        rstd = mem.sbuf("rstd", [P, TB * MH])
        power = mem.sbuf("power", [P, TB * MH])
        g_ps = mem.psum("g_ps", [P, MH * S])
        s_ps = mem.psum("s_ps", [P, MH, 512])
        o_ps = mem.psum("o_ps", [P, TB * MH, MD + 1])

        const_in = mem.sem("const_in")
        ones_set = mem.sem("ones_set")
        ctx_in = [mem.sem(f"ctx_in_{j}") for j in range(2)]
        q_ready = mem.sem("q_ready")
        g_spread = mem.sem("g_spread")
        g_read = mem.sem("g_read")
        d_ready = mem.sem("d_ready")
        scores_ready = mem.sem("scores_ready")
        c_ready = mem.sem("c_ready")
        out_ready = mem.sem("out_ready")
        out_read = mem.sem("out_read")
        var_ready = mem.sem("var_ready")
        rstd_ready = mem.sem("rstd_ready")
        steps_done = mem.sem("steps_done")
        block = stack.enter_context(nc.Block())

        @block.sync
        def _(sync):
            sync.dma_start(causal[:], a["causal"]).then_inc(const_in, 16)
            sync.dma_start(ln_scale[:], a["ln_scale"]).then_inc(const_in, 16)
            sync.wait_ge(ones_set, 2)
            with sync.Fori(0, B // 2) as i:
                for j in range(2):
                    b = i * 2 + j
                    sync.wait_ge(out_ready, b + 1)
                    sync.dma_start(ctx_t[:, j, :], a["ctx_t"][:, bass.ds(b, 1), :]).then_inc(ctx_in[j], 16)
                    for t in range(TB):
                        sync.dma_start(v_one[:, j, t, :, 0:MD],
                                       a["ctx_n"][:, bass.ds(b * TB + t, 1), :].rearrange("p t (h d) -> p (t h) d", d=MD)).then_inc(ctx_in[j], 16)

        @block.gpsimd
        def _(pool):
            nc.gpsimd.memset(power[:], -0.5).then_inc(rstd_ready, 1)
            with pool.Fori(0, B // 2) as i:
                for j in range(2):
                    b = i * 2 + j
                    pool.wait_ge(out_ready, b + 1)
                    apart(pool)
                    nc.gpsimd.tensor_copy(q_t[:, j, :], xn_t[:, bass.ds(b * S, S)]).then_inc(q_ready, 1)
                    pool.wait_ge(var_ready, b + 1)
                    pool.wait_ge(rstd_ready, b + 1)
                    nc.gpsimd.tensor_tensor(rstd[:], var[:], power[:], ALU.pow).then_inc(rstd_ready, 1)

        @block.vector
        def _(dve):
            nc.vector.memset(v_one[:], 1.0).then_inc(ones_set, 1)
            nc.vector.memset(ones[:], 1.0).then_inc(ones_set, 1)
            dve.wait_ge(const_in, 32)
            nc.vector.tensor_scalar(out=ln_scale[:], in0=ln_scale[:], scalar1=1.0, scalar2=None,
                                    op0=ALU.add).then_inc(ones_set, 1)
            dve.wait_ge(ones_set, 3)
            dve.sem_inc(g_read, 1)
            dve.sem_inc(c_ready, 1)
            dve.sem_inc(out_read, 1)
            with dve.Fori(0, B // 2) as i:
                for j in range(2):
                    b = i * 2 + j
                    steps = Steps(dve, steps_done, b, 9 + 12)
                    steps.step(nc.vector.tensor_copy(g_now[:, j], g_col[:].rearrange("p t (h b) -> p t h b", b=B)[:, :, :, bass.ds(b, 1)]))
                    steps.link(nc.vector.tensor_copy(e_now[:], e_col[:].rearrange("p t (h b) -> p t h b", b=B)[:, :, :, bass.ds(b, 1)]))
                    dve.wait_ge(g_spread, b + 1)
                    for n in range(MH):
                        steps.step(nc.vector.scalar_tensor_tensor(
                            out=d_arg[:, j, n, 0:S], in0=g_ps[:, n * S:(n + 1) * S],
                            scalar=g_now[:, j, 0, n:n + 1], in1=causal[:], op0=ALU.add, op1=ALU.min))
                        later = nc.vector.scalar_tensor_tensor(
                            out=d_arg[:, j, n, S:W], in0=g_ps[:, n * S + P:(n + 1) * S],
                            scalar=g_now[:, j, 1, n:n + 1], in1=causal[:, 0:P], op0=ALU.add, op1=ALU.min)
                        if n < MH - 1:
                            steps.step(later)
                    later.then_inc(g_read, 1)
                    dve.wait_ge(scores_ready, b + 1)
                    dve.wait_ge(d_ready, b + 1)
                    nc.vector.scalar_tensor_tensor(out=c[:, j], in0=s_ps[:, :, 0:W], scalar=MSCALE, in1=d_exp[:, j],
                                                   op0=ALU.mult, op1=ALU.mult).then_inc(c_ready, 1)
                    dve.wait_ge(out_ready, b + 3)
                    steps.link(nc.vector.scalar_tensor_tensor(
                        out=den[:, :, 0], in0=o_ps[:, :, MD], scalar=-1.0,
                        in1=e_now[:].rearrange("p t h -> p (t h)"), op0=ALU.mult, op1=ALU.max))
                    steps.link(nc.vector.tensor_tensor(den[:, :, 0], o_ps[:, :, MD], den[:, :, 0], ALU.max))
                    steps.link(nc.vector.tensor_scalar(out=den[:], in0=den[:], scalar1=1e-6, scalar2=None, op0=ALU.add))
                    steps.link(nc.vector.reciprocal(den[:], den[:]))
                    nc.vector.tensor_tensor(h[:], o_ps[:, :, 0:MD], den[:].to_broadcast([P, TB * MH, MD]),
                                            ALU.mult).then_inc(out_read, 1)
                    dve.wait_ge(out_read, b + 2)
                    steps.link(nc.vector.tensor_reduce(mean[:], h[:], AX.X, ALU.add))
                    steps.link(nc.vector.tensor_scalar(out=mean[:], in0=mean[:], scalar1=1.0 / MD, scalar2=None, op0=ALU.mult))
                    steps.link(nc.vector.tensor_tensor(h[:], h[:], mean[:].unsqueeze(2).to_broadcast([P, TB * MH, MD]), ALU.subtract))
                    steps.link(nc.vector.tensor_tensor(sq[:], h[:], h[:], ALU.mult))
                    steps.link(nc.vector.tensor_reduce(var[:], sq[:], AX.X, ALU.add))
                    nc.vector.tensor_scalar(out=var[:], in0=var[:], scalar1=1.0 / MD, scalar2=LN_EPS,
                                            op0=ALU.mult, op1=ALU.add).then_inc(var_ready, 1)
                    dve.wait_ge(rstd_ready, b + 2)
                    steps.link(nc.vector.tensor_tensor(h[:], h[:], rstd[:].unsqueeze(2).to_broadcast([P, TB * MH, MD]), ALU.mult))
                    flat = h[:].rearrange("p (t h) d -> p t (h d)", t=TB)
                    steps.link(nc.vector.tensor_tensor(flat, flat, ln_scale[:].unsqueeze(1).to_broadcast([P, TB, D]), ALU.mult))
                    steps.link(nc.vector.tensor_tensor(x[:, bass.ds(b * TB, TB), :], x[:, bass.ds(b * TB, TB), :], flat, ALU.add))
                    steps.close()

        @block.tensor
        def _(pe):
            pe.wait_ge(ones_set, 3)
            pe.sem_inc(out_ready, 2)
            with pe.Fori(0, B // 2) as i:
                for j in range(2):
                    b = i * 2 + j
                    pe.wait_ge(g_read, b + 1)
                    for n in range(MH):
                        last = nc.tensor.matmul(g_ps[:, n * S:(n + 1) * S], ones[:],
                                                neg_g_row[0:1, bass.ds(b * S + n * (B * S), S)],
                                                start=True, stop=True)
                    last.then_inc(g_spread, 1)
                    pe.wait_ge(ctx_in[j], i * 48 + 48)
                    pe.wait_ge(q_ready, b + 1)
                    pe.wait_ge(c_ready, b + 1)
                    for n in range(MH):
                        rows = slice(n * MD, (n + 1) * MD)
                        nc.tensor.matmul(s_ps[:, n, 0:S], ctx_t[rows, j, 0:P], q_t[rows, j, :], start=True, stop=True)
                        last = nc.tensor.matmul(s_ps[:, n, S:W], ctx_t[rows, j, P:S], q_t[rows, j, P:S],
                                                start=True, stop=True)
                    last.then_inc(scores_ready, 1)
                    pe.wait_ge(c_ready, b + 2)
                    pe.wait_ge(out_read, b + 1)
                    for n in range(MH):
                        nc.tensor.matmul(o_ps[:, n, :], c[:, j, n, 0:P], v_one[:, j, 0, n, :], start=True, stop=True)
                        nc.tensor.matmul(o_ps[:, MH + n, :], c[:, j, n, P:S], v_one[:, j, 0, n, :], start=True, stop=False)
                        last = nc.tensor.matmul(o_ps[:, MH + n, :], c[:, j, n, S:W], v_one[:, j, 1, n, :],
                                                start=False, stop=True)
                    last.then_inc(out_ready, 1)

        @block.scalar
        def _(act):
            with act.Fori(0, B // 2) as i:
                for j in range(2):
                    b = i * 2 + j
                    act.wait_ge(g_read, b + 2)
                    nc.scalar.activation(d_exp[:, j].rearrange("p h w -> p (h w)"),
                                         d_arg[:, j].rearrange("p h w -> p (h w)"), ACT.Exp).then_inc(d_ready, 1)



E = 8


class Mixture:

    def __init__(self, name, k, h, gated, bias):
        self.name, self.k, self.h, self.gated, self.bias = name, k, h, gated, bias
        self.wide = 2 * h if gated else h
        tiles = k * NT + E - 1
        self.tiles = tiles + tiles % 2
        self.second_bias = name == "f0"
        self.top_probability = name == "f1"


MIX0 = Mixture("f0", 1, 512, False, True)
MIX1 = Mixture("f1", 1, 512, True, False)
MIX3 = Mixture("f3", 2, 256, True, True)
MOST_SLOTS = MIX3.tiles * P


def mixture_route(nc, a, x, ident, mix, hold, slots_x):
    from contextlib import ExitStack
    K = mix.k
    with ExitStack() as stack:
        mem = Memory(nc, stack, mix.name + "r")
        nb = NormBuffers(mem)
        xn = mem.sbuf("xn", [P, NT, D])
        xn_now = mem.sbuf("xn_now", [P, 2, TB, D])
        xn_t = mem.sbuf("xn_t", [P, 2, S])
        router = mem.sbuf("router", [P, E])
        router_b = mem.sbuf("router_b", [P, 2, E])
        before = mem.sbuf("before", [P, P])
        ones = mem.sbuf("ones", [P, P])
        iota_e = mem.sbuf("iota_e", [P, E])
        iota_s = mem.sbuf("iota_s", [P, mix.tiles])
        keep = mem.sbuf("keep", [P, E, NT])
        tile_starts = mem.sbuf("tile_starts", [P, NT])
        logits = mem.sbuf("logits", [P, NT, E])
        top = mem.sbuf("top", [P, NT, E])
        top_at = mem.sbuf("top_at", [P, NT, E], U32)
        at = mem.sbuf("at", [P, K, NT])
        chosen = mem.sbuf("chosen", [P, K, NT, E])
        both = mem.sbuf("both", [P, NT, E])
        count = mem.sbuf("count", [P, E, NT])
        cum = mem.sbuf("cum", [P, E, NT])
        over = mem.sbuf("over", [P, E, NT])
        n_tiles = mem.sbuf("n_tiles", [P, E])
        ends = mem.sbuf("ends", [P, E])
        base = mem.sbuf("base", [P, E])
        offset = mem.sbuf("offset", [P, E, NT])
        place = mem.sbuf("place", [P, NT, E])
        picked = mem.sbuf("picked", [P, K, NT, E])
        slot = mem.sbuf("slot", [P, K, NT])
        past = mem.sbuf("past", [P, mix.tiles, E])
        expert = mem.sbuf("expert", [P, mix.tiles])
        gap = mem.sbuf("gap", [P, NT, E])
        exp_gap = mem.sbuf("exp_gap", [P, NT, E])
        total = mem.sbuf("total", [P, NT])
        t_ps = mem.psum("t_ps", [P, 2, 512])
        l_ps = mem.psum("l_ps", [P, 2, 512])
        c_ps = mem.psum("c_ps", [P, 2, 512])

        const_in = mem.sem("const_in")
        transposed = mem.sem("transposed")
        xn_t_ready = mem.sem("xn_t_ready")
        logits_done = mem.sem("logits_done")
        logits_ready = mem.sem("logits_ready")
        steps_done = mem.sem("steps_done")
        route_steps = mem.sem("route_steps")
        both_ready = mem.sem("both_ready")
        counted = mem.sem("counted")
        slots_ready = mem.sem("slots_ready")
        gap_ready = mem.sem("gap_ready")
        exp_ready = mem.sem("exp_ready")
        block = stack.enter_context(nc.Block())

        @block.sync
        def _(sync):
            for t, n in ((router, mix.name + "_router"), (router_b, mix.name + "_router_b"), (before, "before"),
                         (iota_e, "iota_e"), (iota_s, mix.name + "_iota_s"), (keep, "keep"), (tile_starts, "tile_starts")):
                sync.dma_start(t[:], a[n]).then_inc(const_in, 16)
            for t, n in hold.loads:
                sync.dma_start(t, n).then_inc(hold.loaded, 16)

        @block.gpsimd
        def _(pool):
            norm_power_set(nc, pool, nb)
            with pool.Fori(0, B) as b:
                norm_gpsimd(nc, pool, nb, b)
            pool.wait_ge(slots_ready, 1)
            for k in range(K):
                for t in range(NT):
                    nc.gpsimd.indirect_dma_start(
                        out=slots_x[:, :], out_offset=bass.IndirectOffsetOnAxis(ap=hold.slot[:, k, t:t + 1], axis=0),
                        in_=xn[:, t, :], in_offset=None).then_inc(Memory.scattered, 16)
            pool.wait_ge(Memory.scattered, (Memory.rounds + K) * NT * 16)

        @block.tensor
        def _(pe):
            pe.wait_ge(const_in, 7 * 16)
            pe.sem_inc(transposed, 2)
            pe.sem_inc(logits_done, 2)
            with pe.Fori(0, B // 2) as i:
                for j in range(2):
                    b = i * 2 + j
                    pe.wait_ge(nb.ready, b + 1)
                    pe.wait_ge(xn_t_ready, b + 1)
                    for t in range(TB):
                        last = nc.tensor.transpose(t_ps[:, j, t * P:(t + 1) * P], xn_now[:, j, t, :], ident[:])
                    last.then_inc(transposed, 1)
                    pe.wait_ge(logits_ready, b + 1)
                    pe.wait_ge(xn_t_ready, b + 3)
                    for t in range(TB):
                        last = nc.tensor.matmul(l_ps[:, j, t * E:(t + 1) * E], xn_t[:, j, t * P:(t + 1) * P], router[:],
                                                start=True, stop=True)
                    last.then_inc(logits_done, 1)
            pe.wait_ge(both_ready, 1)
            nc.tensor.matmul(c_ps[:, 0, 0:NT * E], before[:], both[:].rearrange("p t e -> p (t e)"), start=True, stop=True)
            nc.tensor.matmul(c_ps[:, 1, 0:NT * E], ones[:], both[:].rearrange("p t e -> p (t e)"),
                             start=True, stop=True).then_inc(counted, 1)

        @block.scalar
        def _(act):
            act.sem_inc(xn_t_ready, 2)
            with act.Fori(0, B // 2) as i:
                for j in range(2):
                    b = i * 2 + j
                    act.wait_ge(transposed, b + 3)
                    act.wait_ge(logits_done, b + 1)
                    nc.scalar.activation(xn_t[:, j, :], t_ps[:, j, 0:S], ACT.Copy).then_inc(xn_t_ready, 1)
            if K == 2 or mix.top_probability:
                act.wait_ge(gap_ready, 1)
                nc.scalar.activation(exp_gap[:], gap[:], ACT.Exp).then_inc(exp_ready, 1)

        @block.vector
        def _(dve):
            nc.vector.memset(ones[:], 1.0).then_inc(route_steps, 1)
            dve.wait_ge(const_in, 7 * 16)
            dve.sem_inc(logits_ready, 2)
            with dve.Fori(0, B // 2) as i:
                for j in range(2):
                    b = i * 2 + j
                    steps = Steps(dve, steps_done, b, NORM_STEPS + 1 + mix.second_bias)
                    dve.wait_ge(transposed, b + 1)
                    norm_vector(nc, dve, steps, nb, x, b, xn_now[:, j])
                    steps.step(nc.vector.tensor_copy(xn[:, bass.ds(b * TB, TB), :], xn_now[:, j]))
                    dve.wait_ge(logits_done, b + 3)
                    add = nc.vector.tensor_tensor(logits[:, bass.ds(b * TB, TB), :],
                                                  l_ps[:, j, 0:TB * E].rearrange("p (t e) -> p t e", e=E),
                                                  router_b[:, 0:1, :].to_broadcast([P, TB, E]), ALU.add)
                    if mix.second_bias:
                        steps.link(add)
                        add = nc.vector.tensor_tensor(logits[:, bass.ds(b * TB, TB), :], logits[:, bass.ds(b * TB, TB), :],
                                                      router_b[:, 1:2, :].to_broadcast([P, TB, E]), ALU.add)
                    add.then_inc(logits_ready, 1)
                    steps.close()
            dve.wait_ge(logits_ready, B + 2)
            r = Steps(dve, route_steps)
            r.n = 1
            for t in range(NT):
                r.step(nc.vector.max(top[:, t, :], logits[:, t, :]))
            r.settle()
            for t in range(NT):
                r.step(nc.vector.max_index(top_at[:, t, :], top[:, t, :], logits[:, t, :]))
            r.settle()
            wide = [P, NT, E]
            for k in range(K):
                r.link(nc.vector.tensor_copy(at[:, k, :], top_at[:, :, k]))
                r.link(nc.vector.tensor_tensor(chosen[:, k], iota_e[:].unsqueeze(1).to_broadcast(wide),
                                               at[:, k, :].unsqueeze(2).to_broadcast(wide), ALU.is_equal))
            if K == 2:
                nc.vector.tensor_tensor(both[:], chosen[:, 0], chosen[:, 1], ALU.add).then_inc(both_ready, 1)
            else:
                nc.vector.tensor_copy(both[:], chosen[:, 0]).then_inc(both_ready, 1)
            if mix.top_probability:
                nc.vector.tensor_tensor(gap[:], logits[:], top[:, :, 0:1].to_broadcast(wide),
                                        ALU.subtract).then_inc(gap_ready, 1)
                dve.wait_ge(exp_ready, 1)
                r.link(nc.vector.tensor_reduce(total[:], exp_gap[:], AX.X, ALU.add))
                r.link(nc.vector.reciprocal(hold.score[:, 0, :], total[:]))
            if K == 2:
                nc.vector.tensor_tensor(gap[:], top[:], top[:, :, 0:1].to_broadcast(wide),
                                        ALU.subtract).then_inc(gap_ready, 1)
                dve.wait_ge(exp_ready, 1)
                r.link(nc.vector.tensor_tensor(total[:], exp_gap[:, :, 0], exp_gap[:, :, 1], ALU.add))
                r.link(nc.vector.reciprocal(total[:], total[:]))
                for k in range(K):
                    r.link(nc.vector.tensor_tensor(hold.score[:, k, :], exp_gap[:, :, k], total[:], ALU.mult))
            dve.wait_ge(counted, 1)
            r.link(nc.vector.tensor_copy(count[:], c_ps[:, 1, 0:NT * E].rearrange("p (t e) -> p e t", e=E)))
            r.link(nc.vector.tensor_tensor_scan(cum[:].rearrange("p e t -> p (e t)"), keep[:].rearrange("p e t -> p (e t)"),
                                                count[:].rearrange("p e t -> p (e t)"), 0.0, ALU.mult, ALU.add))
            by_e = [P, E, NT]
            r.link(nc.vector.tensor_tensor(over[:], cum[:, :, NT - 1:NT].to_broadcast(by_e),
                                           tile_starts[:].unsqueeze(1).to_broadcast(by_e), ALU.is_gt))
            r.link(nc.vector.tensor_reduce(n_tiles[:], over[:], AX.X, ALU.add))
            r.link(nc.vector.tensor_tensor_scan(ends[:], ones[:, 0:E], n_tiles[:], 0.0, ALU.mult, ALU.add))
            r.link(nc.vector.tensor_tensor(base[:], ends[:], n_tiles[:], ALU.subtract))
            r.link(nc.vector.tensor_tensor(offset[:], cum[:], count[:], ALU.subtract))
            r.link(nc.vector.scalar_tensor_tensor(out=offset[:], in0=base[:].unsqueeze(2).to_broadcast(by_e), scalar=float(P),
                                                  in1=offset[:], op0=ALU.mult, op1=ALU.add))
            r.link(nc.vector.tensor_tensor(place[:], c_ps[:, 0, 0:NT * E].rearrange("p (t e) -> p t e", e=E),
                                           offset[:].rearrange("p e t -> p t e"), ALU.add))
            for k in range(K):
                r.link(nc.vector.tensor_tensor(picked[:, k], chosen[:, k], place[:], ALU.mult))
                r.link(nc.vector.tensor_reduce(slot[:, k, :], picked[:, k], AX.X, ALU.add))
            nc.vector.tensor_copy(hold.slot[:], slot[:]).then_inc(slots_ready, 1)
            by_s = [P, mix.tiles, E]
            r.link(nc.vector.tensor_tensor(past[:], iota_s[:].unsqueeze(2).to_broadcast(by_s),
                                           ends[:].unsqueeze(1).to_broadcast(by_s), ALU.is_ge))
            r.link(nc.vector.tensor_reduce(expert[:], past[:], AX.X, ALU.add))
            r.link(nc.vector.tensor_scalar(out=hold.expert[:], in0=expert[:], scalar1=float(E - 1), scalar2=None, op0=ALU.min))


def mixture_experts(nc, a, ident, mix, hold, slots_x, slots_y):
    from contextlib import ExitStack
    H, W, NS, HC = mix.h, mix.wide, mix.tiles, mix.h // P
    with ExitStack() as stack:
        mem = Memory(nc, stack, mix.name + "e")
        xs = mem.sbuf("xs", [P, 2, D])
        xs_t = mem.sbuf("xs_t", [P, 2, P])
        wide = mem.sbuf("wide", [P, 2, W])
        gate = mem.sbuf("gate", [P, 2, H])
        hidden = mem.sbuf("hidden", [P, 2, H])
        hidden_t = mem.sbuf("hidden_t", [P, 2, HC, P])
        ys = mem.sbuf("ys", [P, 2, D])
        xt_ps = mem.psum("xt_ps", [P, 512])
        h_ps = mem.psum("h_ps", [P, 2, max(W, 512)])
        ht_ps = mem.psum("ht_ps", [P, 512])
        y_ps = mem.psum("y_ps", [P, 512])

        row_in = [mem.sem(f"row_in_{j}") for j in range(2)]
        row_out = [mem.sem(f"row_out_{j}") for j in range(2)]
        xt_done = mem.sem("xt_done")
        xt_ready = mem.sem("xt_ready")
        h_done = mem.sem("h_done")
        wide_ready = mem.sem("wide_ready")
        gate_ready = mem.sem("gate_ready")
        hidden_ready = mem.sem("hidden_ready")
        ht_done = mem.sem("ht_done")
        ht_ready = mem.sem("ht_ready")
        y_done = mem.sem("y_done")
        y_ready = mem.sem("y_ready")
        block = stack.enter_context(nc.Block())

        def half(t, j):
            return t // 2 if isinstance(t, int) else (t - j) // 2

        def turns(engine, turn, lag):
            for t in range(2):
                turn(t, t % 2, "first")
            with engine.Fori(1, NS // 2) as i:
                for j in range(2):
                    turn(i * 2 + j, j, "middle")
            for t in range(NS, NS + lag):
                turn(t, t % 2, "last")

        def of(t, lag, where):
            return where == "middle" or (where == "first" and t >= lag) or (where == "last" and t - lag < NS)

        @block.sync
        def _(sync):
            def turn(t, j, where):
                if of(t, 0, where):
                    sync.wait_ge(xt_done, t + 1)
                    sync.dma_start(xs[:, j, :], slots_x[bass.ds(t * P, P), :]).then_inc(row_in[j], 16)
                if of(t, 3, where):
                    store(t - 3, 1 - j)

            def store(s, j):
                sync.wait_ge(y_ready, s + 2)
                sync.dma_start(slots_y[bass.ds(s * P, P), :], ys[:, j, :]).then_inc(row_out[j], 16)

            for j in range(2):
                sync.sem_inc(row_out[j], 16)
            for t in range(4):
                turn(t, t % 2, "first")
            with sync.Fori(2, NS // 2) as i:
                for j in range(2):
                    turn(i * 2 + j, j, "middle")
            for t in range(NS, NS + 3):
                turn(t, t % 2, "last")
            for j in range(2):
                sync.wait_ge(row_out[j], NS // 2 * 16 + 16)

        @block.tensor
        def _(pe):
            pe.wait_ge(hold.loaded, len(hold.loads) * 16)
            pe.sem_inc(xt_done, 2)
            pe.sem_inc(h_done, 2)
            pe.sem_inc(y_done, 2)

            def turn(t, j, where):
                if of(t, 0, where):
                    e = pe.value_load(hold.expert[0:1, bass.ds(t, 1)], min_val=0, max_val=E - 1)
                    pe.wait_ge(row_in[j], half(t, j) * 16 + 16)
                    pe.wait_ge(xt_ready, t + 1)
                    nc.tensor.transpose(xt_ps[:, 0:P], xs[:, j, :], ident[:]).then_inc(xt_done, 1)
                    pe.wait_ge(xt_ready, t + 2)
                    pe.wait_ge(hidden_ready, t + 1)
                    for c in range(0, W, 512):
                        last = nc.tensor.matmul(h_ps[:, j, c:c + 512], xs_t[:, j, :], hold.w1[:, bass.ds(e * W + c, 512)],
                                                start=True, stop=True)
                    last.then_inc(h_done, 1)
                if of(t, 1, where):
                    pe.wait_ge(hidden_ready, t + 2)
                    pe.wait_ge(ht_ready, t)
                    for c in range(HC):
                        last = nc.tensor.transpose(ht_ps[:, c * P:(c + 1) * P], hidden[:, 1 - j, c * P:(c + 1) * P], ident[:])
                    last.then_inc(ht_done, 1)
                if of(t, 2, where):
                    e = pe.value_load(hold.expert[0:1, bass.ds(t - 2, 1)], min_val=0, max_val=E - 1)
                    pe.wait_ge(ht_ready, t)
                    pe.wait_ge(y_ready, t - 1)
                    for c in range(HC):
                        last = nc.tensor.matmul(y_ps[:, 0:D], hidden_t[:, j, c, :], hold.w2[:, bass.ds(e * (HC * D) + c * D, D)],
                                                start=c == 0, stop=c == HC - 1)
                    last.then_inc(y_done, 1)

            turns(pe, turn, 2)

        @block.scalar
        def _(act):
            act.sem_inc(xt_ready, 1)
            act.sem_inc(ht_ready, 1)

            def turn(t, j, where):
                if of(t, 0, where):
                    act.wait_ge(xt_done, t + 3)
                    act.wait_ge(h_done, t + 1)
                    nc.scalar.activation(xs_t[:, j, :], xt_ps[:, 0:P], ACT.Copy).then_inc(xt_ready, 1)
                    if mix.gated:
                        if mix.bias:
                            act.wait_ge(wide_ready, t + 1)
                        else:
                            act.wait_ge(h_done, t + 3)
                        act.wait_ge(hidden_ready, t + 1)
                        nc.scalar.activation(gate[:, j, :], (wide if mix.bias else h_ps)[:, j, 0:H], ACT.Silu).then_inc(gate_ready, 1)
                if of(t, 1, where):
                    act.wait_ge(ht_done, t)
                    act.wait_ge(y_done, t)
                    nc.scalar.activation(hidden_t[:, 1 - j].rearrange("p c t -> p (c t)"), ht_ps[:, 0:H],
                                         ACT.Copy if mix.gated else ACT.Relu).then_inc(ht_ready, 1)

            turns(act, turn, 1)

        @block.vector
        def _(dve):
            dve.wait_ge(hold.loaded, len(hold.loads) * 16)
            dve.sem_inc(hidden_ready, 2)
            dve.sem_inc(y_ready, 1)

            def turn(t, j, where):
                if of(t, 0, where):
                    if mix.bias:
                        e = dve.value_load(hold.expert[0:1, bass.ds(t, 1)], min_val=0, max_val=E - 1)
                    dve.wait_ge(h_done, t + 3)
                    if where != "first":
                        dve.wait_ge(ht_done, t - 1)
                    if not mix.gated:
                        nc.vector.tensor_tensor(hidden[:, j, :], h_ps[:, j, 0:W], hold.b1[:, bass.ds(e * W, W)],
                                                ALU.add).then_inc(hidden_ready, 1)
                    else:
                        if mix.bias:
                            nc.vector.tensor_tensor(wide[:, j, :], h_ps[:, j, 0:W], hold.b1[:, bass.ds(e * W, W)],
                                                    ALU.add).then_inc(wide_ready, 1)
                        dve.wait_ge(gate_ready, t + 1)
                        nc.vector.tensor_tensor(hidden[:, j, :], gate[:, j, :], (wide if mix.bias else h_ps)[:, j, H:W],
                                                ALU.mult).then_inc(hidden_ready, 1)
                if of(t, 2, where):
                    if mix.bias:
                        e = dve.value_load(hold.expert[0:1, bass.ds(t - 2, 1)], min_val=0, max_val=E - 1)
                    dve.wait_ge(y_done, t + 1)
                    dve.wait_ge(row_out[j], half(t, j) * 16)
                    if mix.bias:
                        nc.vector.tensor_tensor(ys[:, j, :], y_ps[:, 0:D], hold.b2[:, bass.ds(e * D, D)], ALU.add).then_inc(y_ready, 1)
                    else:
                        nc.vector.tensor_copy(ys[:, j, :], y_ps[:, 0:D]).then_inc(y_ready, 1)

            turns(dve, turn, 2)


def mixture_gather(nc, x, mix, hold, slots_y):
    from contextlib import ExitStack
    with ExitStack() as stack:
        mem = Memory(nc, stack, mix.name + "g")
        back = mem.sbuf("back", [P, mix.k, NT, D])
        steps_done = mem.sem("steps_done")
        block = stack.enter_context(nc.Block())

        @block.gpsimd
        def _(pool):
            for t in range(NT):
                for k in range(mix.k):
                    nc.gpsimd.indirect_dma_start(
                        out=back[:, k, t, :], out_offset=None, in_=slots_y[0:mix.tiles * P, :],
                        in_offset=bass.IndirectOffsetOnAxis(ap=hold.slot[:, k, t:t + 1], axis=0)).then_inc(Memory.gathered[t], 16)

        @block.vector
        def _(dve):
            steps = Steps(dve, steps_done)
            for t in range(NT):
                dve.wait_ge(Memory.gathered[t], (Memory.rounds + mix.k) * 16)
                for k in range(mix.k):
                    if k:
                        steps.settle()
                    if mix.name == "f0":
                        steps.step(nc.vector.tensor_tensor(x[:, t, :], x[:, t, :], back[:, k, t, :], ALU.add))
                    else:
                        steps.step(nc.vector.scalar_tensor_tensor(out=x[:, t, :], in0=back[:, k, t, :], scalar=hold.score[:, k, t:t + 1],
                                                                  in1=x[:, t, :], op0=ALU.mult, op1=ALU.add))
            steps.settle()


def mixture_layer(nc, a, x, ident, mix, slots_x, slots_y):
    from contextlib import ExitStack
    with ExitStack() as stack:
        hold = Memory(nc, stack, mix.name)
        hold.slot = hold.sbuf("slot", [P, mix.k, NT], U32)
        hold.score = hold.sbuf("score", [P, mix.k, NT])
        hold.expert = hold.sbuf("expert", [P, mix.tiles], I32)
        hold.w1 = hold.sbuf("w1", [P, E * mix.wide])
        hold.w2 = hold.sbuf("w2", [P, E * mix.h])
        hold.loaded = hold.sem("loaded")
        hold.loads = [(hold.w1[:], a[mix.name + "_w1"]), (hold.w2[:], a[mix.name + "_w2"])]
        if mix.bias:
            hold.b1 = hold.sbuf("b1", [P, E * mix.wide])
            hold.b2 = hold.sbuf("b2", [P, E * D])
            hold.loads += [(hold.b1[:], a[mix.name + "_b1"].to_broadcast([P, E * mix.wide])),
                           (hold.b2[:], a[mix.name + "_b2"].to_broadcast([P, E * D]))]
        mixture_route(nc, a, x, ident, mix, hold, slots_x)
        mixture_experts(nc, a, ident, mix, hold, slots_x, slots_y)
        mixture_gather(nc, x, mix, hold, slots_y)
    Memory.rounds += mix.k



HN = 16
HD = D // HN
SLOT = 32
HG = 4
G = HN // HG
MAX_ROW = 3 * HD
MASKED = -2.0 ** 100


class Heads:
    def __init__(self, name, scale, masked, biased):
        self.name, self.scale, self.masked, self.biased = name, scale, masked, biased


HEADS1 = Heads("h1", HD ** -0.5, True, False)
HEADS2 = Heads("h2", 1.0, False, True)


def heads_layer(nc, a, x, ident, hw):
    from contextlib import ExitStack
    with ExitStack() as stack:
        mem = Memory(nc, stack, hw.name)
        nb = NormBuffers(mem)
        w_qk = mem.sbuf("w_qk", [P, 2, G, P])
        w_v = mem.sbuf("w_v", [P, D])
        w_o = mem.sbuf("w_o", [P, D])
        b_v = mem.sbuf("b_v", [P, D])
        b_o = mem.sbuf("b_o", [P, D])
        b_qk = mem.sbuf("b_qk", [P, 2, G])
        b_low = mem.sbuf("b_low", [P, 2, G])
        low = mem.sbuf("low", [P, 2])
        ctx_t = mem.sbuf("ctx_t", [P, 2, S])
        xn = mem.sbuf("xn", [P, 2, TB, D])
        xn_t = mem.sbuf("xn_t", [P, 2, S])
        high = mem.sbuf("high", [P, 2, 2, S], F32R)
        qk = mem.sbuf("qk", [P, 2, 2, G, S], F32R)
        v = mem.sbuf("v", [P, 2, TB, HN, SLOT])
        neg_max = mem.sbuf("neg_max", [P, TB, G, HG])
        max_high = mem.sbuf("max_high", [P, TB, G, HG], F32R)
        max_rows = mem.sbuf("max_rows", [P, TB, G, HG, SLOT])
        p_t = mem.sbuf("p_t", [P, 8, 2, S])
        o_t = mem.sbuf("o_t", [P, G, S])
        recip = mem.sbuf("recip", [P, TB, HN, 1])
        o_n = mem.sbuf("o_n", [P, TB, D])
        on_t = mem.sbuf("on_t", [P, S])
        if hw.masked:
            mask_in = mem.sbuf("mask_in", [P, 2, TB, S], I32)
            mask = mem.sbuf("mask", [P, 2, TB, S], BF16)
            ident_b = mem.sbuf("ident_b", [P, P], BF16)
        work = [mem.psum(f"work{i}", [P, 512]) for i in range(2)]
        sn_ps = [mem.psum(f"sn_ps{i}", [P, 2, 2, S]) for i in range(2)]
        st_ps = [mem.psum(f"st_ps{i}", [P, 2, S]) for i in range(2)]

        const_in = mem.sem("const_in")
        const_set = mem.sem("const_set")
        ctx_in = [mem.sem(f"ctx_in_{j}") for j in range(2)]
        xt_done = mem.sem("xt_done")
        xt_ready = mem.sem("xt_ready")
        proj_done = mem.sem("proj_done")
        high_ready = mem.sem("high_ready")
        split_ready = mem.sem("split_ready")
        v_done = mem.sem("v_done")
        v_ready = mem.sem("v_ready")
        sn_done = mem.sem("sn_done")
        sn_read = mem.sem("sn_read")
        max_steps = mem.sem("max_steps")
        mt_done = mem.sem("mt_done")
        q_max_ready = mem.sem("q_max_ready")
        st_done = mem.sem("st_done")
        p_ready = mem.sem("p_ready")
        pv_done = mem.sem("pv_done")
        ot_ready = mem.sem("ot_ready")
        on_done = mem.sem("on_done")
        on_ready = mem.sem("on_ready")
        ont_done = mem.sem("ont_done")
        ont_ready = mem.sem("ont_ready")
        out_done = mem.sem("out_done")
        x_ready = mem.sem("x_ready")
        norm_steps = mem.sem("norm_steps")
        out_steps = mem.sem("out_steps")
        block = stack.enter_context(nc.Block())
        consts = [(w_qk, "w_qk"), (w_v, "w_v"), (w_o, "w_o"), (b_v, "b_v"), (b_o, "b_o"), (b_qk, "b_qk"),
                  (b_low, "b_low"), (low, "low")]
        if hw.masked:
            consts.append((mask_in, "mask"))

        def need(engine, sem, value):
            if not isinstance(value, int) or value > 0:
                engine.wait_ge(sem, value)

        def turns(engine, turn):
            turn(0, 0, True, False)
            turn(1, 1, True, True)
            with engine.Fori(1, B // 2) as i:
                for j in range(2):
                    turn(i * 2 + j, j, True, True)
            turn(B, 0, False, True)

        @block.sync
        def _(sync):
            for t, n in consts:
                sync.dma_start(t[:], a[hw.name + "_" + n]).then_inc(const_in, 16)

            def turn(t, j, now, before):
                if now:
                    need(sync, v_done, t - 1)
                    sync.dma_start(ctx_t[:, j, :], a["ctx_t"][:, bass.ds(t, 1), :]).then_inc(ctx_in[j], 16)

            turns(sync, turn)

        @block.gpsimd
        def _(pool):
            norm_power_set(nc, pool, nb)
            with pool.Fori(0, B) as b:
                norm_gpsimd(nc, pool, nb, b)

        @block.tensor
        def _(pe):
            pe.wait_ge(const_in, len(consts) * 16)
            pe.wait_ge(const_set, 4)

            def scores(out, t, j, left, right, tile, g, hh, n):
                rows = slice(hh * SLOT, (hh + 1) * SLOT)
                return nc.tensor.matmul(out, qk[rows, j, left, g, tile * P:(tile + 1) * P], qk[rows, j, right, g, :],
                                        start=n == 0 or not hw.masked, stop=not hw.masked, skip_group_check=hw.masked)

            def turn(t, j, now, before):
                if now:
                    pe.wait_ge(nb.ready, t + 1)
                    need(pe, ont_ready, t - 1)
                    for n in range(TB):
                        last = nc.tensor.transpose(work[0][:, n * P:(n + 1) * P], xn[:, j, n, :], ident[:])
                    last.then_inc(xt_done, 1)
                    pe.wait_ge(xt_ready, t + 1)
                    pe.wait_ge(ctx_in[j], (t // 2 if isinstance(t, int) else (t - j) // 2) * 16 + 16)
                    for n in range(4):
                        if n == 0:
                            need(pe, x_ready, t - 1)
                        if n >= 2:
                            pe.wait_ge(split_ready, t * 4 + n - 1)
                        for g in range(2):
                            last = nc.tensor.matmul(work[(n + 1) % 2][:, g * S:(g + 1) * S],
                                                    w_qk[:, n // 2, n % 2 * 2 + g, :],
                                                    xn_t[:, j, :] if n < 2 else ctx_t[:, j, :], start=True, stop=True)
                        last.then_inc(proj_done, 1)
                    pe.wait_ge(split_ready, t * 4 + 3)
                    for n in range(TB):
                        last = nc.tensor.matmul(work[1][:, n * D:(n + 1) * D], ctx_t[:, j, n * P:(n + 1) * P], w_v[:],
                                                start=True, stop=True)
                    last.then_inc(v_done, 1)
                    pe.wait_ge(split_ready, t * 4 + 4)
                for s in range(8):
                    if now:
                        gp, qt, hp = s // 4, s // 2 % 2, s % 2
                        need(pe, sn_read, t * 8 + s - 1)
                        for n in range(2):
                            for g in range(2):
                                last = scores(sn_ps[s % 2][:, n, g, :], t, j, 0, 1, qt, gp * 2 + g, hp * 2 + n, g)
                            if hw.masked:
                                last = nc.tensor.matmul(sn_ps[s % 2][:, n], ident_b[:],
                                                        mask[:, 0, qt:qt + 1, :].to_broadcast([P, 2, S]),
                                                        start=False, stop=True, skip_group_check=True)
                        last.then_inc(sn_done, 1)
                    if before:
                        if s == 0:
                            pe.wait_ge(q_max_ready, (t - 1) * 2 + 2)
                        for n in range(2):
                            unit = s * 2 + n
                            gp, kt, hh = unit // 8, unit // 4 % 2, unit % 4
                            need(pe, p_ready, (t - 1) * 16 + unit - 1)
                            for g in range(2):
                                last = scores(st_ps[n][:, g, :], t, 1 - j, 1, 0, kt, gp * 2 + g, hh, g)
                            if hw.masked:
                                last = nc.tensor.matmul(st_ps[n][:], ident_b[:], mask[:, 1, kt:kt + 1, :].to_broadcast([P, 2, S]),
                                                        start=False, stop=True, skip_group_check=True)
                            last.then_inc(st_done, 1)
                        if s % 2 == 0 and s:
                            sums(pe, t, j, s // 2 - 1, now)
                if before:
                    sums(pe, t, j, 3, now)
                if now:
                    pe.wait_ge(max_steps, (t + 1) * 4)
                    if not before:
                        pe.wait_ge(v_ready, t + 1)
                    for gp in range(2):
                        if before:
                            pe.wait_ge(ot_ready, (t - 1) * 2 + gp + 1)
                        for g in range(2):
                            for qt in range(TB):
                                last = nc.tensor.transpose(work[gp][:, g * S + qt * P:g * S + (qt + 1) * P],
                                                           max_rows[:, qt, gp * 2 + g].rearrange("p h s -> p (h s)"), ident[:])
                        last.then_inc(mt_done, 1)
                if before:
                    for qt in range(TB):
                        pe.wait_ge(ot_ready, (t - 1) * 2 + 2)
                        if now:
                            pe.wait_ge(q_max_ready, t * 2 + qt + 1)
                        for g in range(G):
                            last = nc.tensor.transpose(work[qt][:, g * P:(g + 1) * P], o_t[:, g, qt * P:(qt + 1) * P], ident[:])
                        last.then_inc(on_done, 1)
                    pe.wait_ge(on_ready, (t - 1) * 2 + 2)
                    for qt in range(TB):
                        last = nc.tensor.transpose(work[0][:, qt * P:(qt + 1) * P], o_n[:, qt, :], ident[:])
                    last.then_inc(ont_done, 1)
                    pe.wait_ge(ont_ready, t)
                    for qt in range(TB):
                        last = nc.tensor.matmul(work[1][:, qt * D:(qt + 1) * D], on_t[:, qt * P:(qt + 1) * P], w_o[:],
                                                start=True, stop=True)
                    last.then_inc(out_done, 1)

            def sums(pe, t, j, u, now):
                gp, kt = u // 2, u % 2
                pe.wait_ge(p_ready, (t - 1) * 16 + u * 4 + 4)
                if u == 0:
                    pe.wait_ge(v_ready, t)
                if u == 2 and now:
                    pe.wait_ge(v_ready, t + 1)
                if u == 2 and not now:
                    pe.wait_ge(x_ready, t - 1)
                for g in range(2):
                    for hh in range(HG):
                        last = nc.tensor.matmul(work[gp][hh * SLOT:(hh + 1) * SLOT, g * S:(g + 1) * S],
                                                v[:, 1 - j, kt, (gp * 2 + g) * HG + hh, :], p_t[:, u % 2 * 4 + hh, g, :],
                                                start=kt == 0 and g == 0, stop=kt == 1, skip_group_check=True)
                last.then_inc(pv_done, 1)

            turns(pe, turn)

        @block.scalar
        def _(act):
            act.wait_ge(const_in, len(consts) * 16)

            def turn(t, j, now, before):
                if now:
                    act.wait_ge(xt_done, t + 1)
                    need(act, proj_done, t * 4 - 6)
                    nc.scalar.activation(xn_t[:, j, :], work[0][:, 0:S], ACT.Copy).then_inc(xt_ready, 1)
                    for n in range(4):
                        act.wait_ge(proj_done, t * 4 + n + 1)
                        need(act, split_ready, t * 4 + n - 1)
                        for g in range(2):
                            last = nc.scalar.activation(
                                high[:, n % 2, g, :], work[(n + 1) % 2][:, g * S:(g + 1) * S], ACT.Identity,
                                bias=b_low[:, n // 2, n % 2 * 2 + g:n % 2 * 2 + g + 1], scale=low[:, n // 2:n // 2 + 1])
                        last.then_inc(high_ready, 1)
                    if not hw.biased:
                        act.wait_ge(v_done, t + 1)
                        need(act, pv_done, (t - 1) * 4)
                        nc.scalar.activation(v[:, j, :, :, 0:HD].rearrange("p t h d -> p (t h) d"),
                                             work[1][:, 0:TB * D].rearrange("p (n d) -> p n d", d=HD),
                                             ACT.Copy).then_inc(v_ready, 1)
                if before:
                    for unit in range(16):
                        act.wait_ge(st_done, (t - 1) * 16 + unit + 1)
                        need(act, pv_done, (t - 1) * 4 + unit // 4 - 1)
                        nc.scalar.activation(p_t[:, unit % 8], st_ps[unit % 2][:], ACT.Exp, scale=hw.scale).then_inc(p_ready, 1)
                        if unit in (11, 15):
                            gp = unit // 8 if unit == 15 else 0
                            act.wait_ge(pv_done, (t - 1) * 4 + gp * 2 + 2)
                            need(act, on_done, (t - 1) * 2)
                            nc.scalar.activation(o_t[:, gp * 2:gp * 2 + 2, :].rearrange("p g s -> p (g s)"), work[gp][:],
                                                 ACT.Copy).then_inc(ot_ready, 1)
                    act.wait_ge(ont_done, t)
                    nc.scalar.activation(on_t[:], work[0][:, 0:S], ACT.Copy).then_inc(ont_ready, 1)

            turns(act, turn)

        @block.vector
        def _(dve):
            nc.vector.memset(v[:], 0.0).then_inc(const_set, 1)
            nc.vector.memset(max_rows[:], 0.0).then_inc(const_set, 1)
            dve.wait_ge(const_set, 2)
            nc.vector.memset(v[:, :, :, :, HD:HD + 1].rearrange("p j t h o -> p (j t h) o"), 1.0).then_inc(const_set, 1)
            dve.wait_ge(const_in, len(consts) * 16)
            if hw.masked:
                for n in range(2):
                    nc.vector.tensor_scalar(out=mask[:, n], in0=mask_in[:, n], scalar1=0.0, scalar2=MASKED,
                                            op0=ALU.is_equal, op1=ALU.mult)
                nc.vector.tensor_copy(ident_b[:], ident[:]).then_inc(const_set, 1)
            else:
                dve.sem_inc(const_set, 1)
            dve.wait_ge(const_set, 4)

            def turn(t, j, now, before):
                if now:
                    steps = Steps(dve, norm_steps, t, NORM_STEPS)
                    need(dve, xt_done, t - 1)
                    norm_vector(nc, dve, steps, nb, x, t, xn[:, j])
                    for n in range(4):
                        dve.wait_ge(high_ready, t * 4 + n + 1)
                        need(dve, st_done, (t - 1) * 16)
                        for g in range(2):
                            at = n % 2 * 2 + g
                            last = nc.vector.scalar_tensor_tensor(
                                out=qk[:, j, n // 2, at, :], in0=work[(n + 1) % 2][:, g * S:(g + 1) * S],
                                scalar=b_qk[:, n // 2, at:at + 1], in1=high[:, n % 2, g, :].bitcast(F32),
                                op0=ALU.add, op1=ALU.subtract)
                        last.then_inc(split_ready, 1)
                    if hw.biased:
                        dve.wait_ge(v_done, t + 1)
                        need(dve, pv_done, (t - 1) * 4)
                        for n in range(TB):
                            last = nc.vector.tensor_tensor(v[:, j, n, :, 0:HD],
                                                           work[1][:, n * D:(n + 1) * D].rearrange("p (h d) -> p h d", d=HD),
                                                           b_v[:].rearrange("p (h d) -> p h d", d=HD), ALU.add)
                        last.then_inc(v_ready, 1)
                    for s in range(8):
                        gp, qt, hp = s // 4, s // 2 % 2, s % 2
                        dve.wait_ge(sn_done, t * 8 + s + 1)
                        if s == 0:
                            need(dve, mt_done, t * 2)
                        nc.vector.tensor_reduce(
                            neg_max[:, qt, gp * 2:gp * 2 + 2, hp * 2:hp * 2 + 2].rearrange("p g h -> p h g"),
                            sn_ps[s % 2][:], AX.X, ALU.max, negate=True).then_inc(sn_read, 1)
                    dve.wait_ge(sn_read, t * 8 + 8)
                    m = Steps(dve, max_steps, t, 4)
                    m.link(nc.vector.tensor_copy(max_high[:], neg_max[:]))
                    for qt in range(TB):
                        m.step(nc.vector.tensor_copy(max_rows[:, qt, :, :, MAX_ROW], max_high[:, qt].bitcast(F32)))
                    nc.vector.tensor_tensor(max_rows[:, 0, :, :, MAX_ROW + 1], neg_max[:, 0], max_high[:, 0].bitcast(F32), ALU.subtract)
                    m.step(nc.vector.tensor_tensor(max_rows[:, 1, :, :, MAX_ROW + 1], neg_max[:, 1], max_high[:, 1].bitcast(F32), ALU.subtract))
                    m.close()
                    for gp in range(2):
                        dve.wait_ge(mt_done, t * 2 + gp + 1)
                        nc.vector.tensor_tensor(
                            qk[:, j, 0, gp * 2:gp * 2 + 2, :], qk[:, j, 0, gp * 2:gp * 2 + 2, :].bitcast(F32),
                            work[gp][:].rearrange("p (g s) -> p g s", g=2), ALU.add).then_inc(q_max_ready, 1)
                if before:
                    out = Steps(dve, out_steps, t - 1, 2 + (1 if hw.biased else 0))
                    for qt in range(TB):
                        dve.wait_ge(on_done, (t - 1) * 2 + qt + 1)
                        sums = work[qt][:].rearrange("p (h s) -> p h s", s=SLOT)
                        out.link(nc.vector.reciprocal(recip[:, qt], sums[:, :, HD:HD + 1]))
                        nc.vector.tensor_tensor(o_n[:, qt, :].rearrange("p (h d) -> p h d", d=HD), sums[:, :, 0:HD],
                                                recip[:, qt].to_broadcast([P, HN, HD]), ALU.mult).then_inc(on_ready, 1)
                    dve.wait_ge(out_done, t)
                    xb = x[:, bass.ds((t - 1) * TB, TB), :]
                    if hw.biased:
                        out.link(nc.vector.tensor_tensor(xb, xb, b_o[:].unsqueeze(1).to_broadcast([P, TB, D]), ALU.add))
                    nc.vector.tensor_tensor(xb, xb, work[1][:, 0:TB * D].rearrange("p (t d) -> p t d", t=TB),
                                            ALU.add).then_inc(x_ready, 1)
                    out.close()

            turns(dve, turn)



PH = 4
PK = 128
HALF = 64
TOP = 8
EX = 16
EXPERT_BLOCKS = EX
MLP_BLOCKS = 4
UP_BLOCKS = EXPERT_BLOCKS + MLP_BLOCKS
DOWN_BLOCKS = UP_BLOCKS + MLP_BLOCKS
PICKS = PH * TOP
Q4 = P // PICKS
BANK_GROUPS = 8
PICK_STEPS = 21


def keyed_layer(nc, a, x, ident):
    from contextlib import ExitStack
    with ExitStack() as stack:
        mem = Memory(nc, stack, "pk")
        nb = NormBuffers(mem)
        w_q = mem.sbuf("w_q", [HALF, 2 * PH, D])
        keys = mem.sbuf("keys", [HALF, 2 * PH, PK])
        folded = mem.sbuf("folded", [P, 2, PH * PK])
        down = mem.sbuf("down", [P, DOWN_BLOCKS, P])
        up = mem.sbuf("up", [P, UP_BLOCKS, D])
        iota = mem.sbuf("iota", [P, PK])
        xn = mem.sbuf("xn", [P, TB, D])
        xn_t = mem.sbuf("xn_t", [P, 2, S])
        sim = mem.sbuf("sim", [P, 2, TB, PH, PK])
        best = mem.sbuf("best", [P, 2, TB * PH, TOP])
        best_at = mem.sbuf("best_at", [P, 2, TB * PH, TOP], U32)
        at = mem.sbuf("at", [P, 2, TB * PH, TOP])
        sums = mem.sbuf("sums", [P, TB * PH, TOP, TOP])
        top = mem.sbuf("top", [P, TB * PH, TOP])
        top_at = mem.sbuf("top_at", [P, TB * PH, TOP], U32)
        rank_at = mem.sbuf("rank_at", [P, 2, TB * PH, TOP], U32)
        rank = mem.sbuf("rank", [P, 2, TB * PH, TOP])
        chosen = mem.sbuf("chosen", [P, 2 * TB * PH, TOP, TOP])
        pick = mem.sbuf("pick", [P, 2, TB * PH, TOP])
        beyond = mem.sbuf("beyond", [P, TB * PH, TOP])
        gap = mem.sbuf("gap", [P, TB * PH, TOP])
        ex = mem.sbuf("ex", [P, TB * PH, TOP])
        total = mem.sbuf("total", [P, TB * PH])
        weight = mem.sbuf("weight", [P, TB * PH, TOP])
        spread = mem.sbuf("spread", [P, TB, EX, PICKS])
        spread_t = mem.sbuf("spread_t", [P, TB, EX, PICKS])
        y_t = mem.sbuf("y_t", [P, TB, PICKS])
        ones_y = mem.sbuf("ones_y", [P, 2, TB, PICKS, PK])
        by_token = mem.sbuf("by_token", [P, 2, TB, PICKS, Q4, EX])
        acts = mem.sbuf("acts", [P, DOWN_BLOCKS, S])
        xt_ps = mem.psum("xt_ps", [P, 512])
        sim_ps = mem.psum("sim_ps", [P, 2, 512])
        d_ps = mem.psum("d_ps", [P, 2, 2, S])
        g_ps = mem.psum("g_ps", [P, 2, BANK_GROUPS, Q4, EX])
        y_ps = mem.psum("y_ps", [P, 512])

        const_in = mem.sem("const_in")
        const_set = mem.sem("const_set")
        fold_done = mem.sem("fold_done")
        fold_ready = mem.sem("fold_ready")
        xt_done = mem.sem("xt_done")
        xt_ready = mem.sem("xt_ready")
        sim_done = mem.sem("sim_done")
        sim_ready = mem.sem("sim_ready")
        gap_ready = mem.sem("gap_ready")
        exp_ready = mem.sem("exp_ready")
        spread_ready = mem.sem("spread_ready")
        by_token_ready = mem.sem("by_token_ready")
        ones_ready = mem.sem("ones_ready")
        d_done = mem.sem("d_done")
        d_ready = mem.sem("d_ready")
        g_done = mem.sem("g_done")
        w_ready = mem.sem("w_ready")
        y_done = mem.sem("y_done")
        x_ready = mem.sem("x_ready")
        norm_steps = mem.sem("norm_steps")
        pick_steps = mem.sem("pick_steps")
        block = stack.enter_context(nc.Block())
        FILLS = DOWN_BLOCKS // 2
        GATE_FILL = EXPERT_BLOCKS // 2
        GF = TB * PICKS // BANK_GROUPS
        CONSTS = 5

        def need(engine, sem, value):
            if not isinstance(value, int) or value > 0:
                engine.wait_ge(sem, value)

        def turns(engine, turn):
            turn(0, 0, True, False)
            turn(1, 1, True, True)
            with engine.Fori(1, B // 2) as i:
                for j in range(2):
                    turn(i * 2 + j, j, True, True)
            turn(B, 0, False, True)

        @block.sync
        def _(sync):
            for t, n in ((w_q, "pk_w_q"), (keys, "pk_keys"), (down, "pk_down"), (up, "pk_up"), (iota, "iota")):
                sync.dma_start(t[:], a[n]).then_inc(const_in, 16)
            sync.wait_ge(const_in, CONSTS * 16)

        @block.gpsimd
        def _(pool):
            norm_power_set(nc, pool, nb)
            with pool.Fori(0, B) as b:
                norm_gpsimd(nc, pool, nb, b)

        @block.tensor
        def _(pe):
            pe.wait_ge(const_in, CONSTS * 16)
            for p in range(2):
                for h in range(PH):
                    last = nc.tensor.matmul(sim_ps[:, p, h * PK:(h + 1) * PK], w_q[:, p * PH + h, :], keys[:, p * PH + h, :],
                                            start=True, stop=True)
            last.then_inc(fold_done, 1)
            pe.wait_ge(fold_ready, 1)
            pe.wait_ge(const_set, 1)

            def turn(t, j, now, before):
                if now:
                    pe.wait_ge(nb.ready, t + 1)
                    need(pe, xt_ready, t)
                    for n in range(TB):
                        last = nc.tensor.transpose(xt_ps[:, n * P:(n + 1) * P], xn[:, n, :], ident[:])
                    last.then_inc(xt_done, 1)
                    pe.wait_ge(xt_ready, t + 1)
                    for n in range(TB):
                        for p in range(2):
                            need(pe, sim_ready, t * 4 + n * 2 + p - 1)
                            nc.tensor.matmul(sim_ps[:, p, :], xn_t[:, j, n * P:(n + 1) * P], folded[:, p, :],
                                             start=True, stop=True).then_inc(sim_done, 1)
                if before:
                    for n in range(FILLS):
                        need(pe, d_ready, (t - 1) * FILLS + n - 1)
                        for c in range(2):
                            last = nc.tensor.matmul(d_ps[:, n % 2, c, :], down[:, n * 2 + c, :], xn_t[:, 1 - j, :],
                                                    start=True, stop=True)
                        last.then_inc(d_done, 1)
                    pe.wait_ge(by_token_ready, t)
                    pe.wait_ge(ones_ready, t)
                    for n in range(TB):
                        for k in range(GF // TB):
                            f = n * (GF // TB) + k
                            need(pe, w_ready, (t - 1) * (GF + 1) + f if f >= 2 else ((t - 1) * (GF + 1) + f - 1))
                            for u in range(BANK_GROUPS):
                                group = k * BANK_GROUPS + u
                                last = nc.tensor.matmul(g_ps[:, f % 2, u], ones_y[:, 1 - j, n, group, :],
                                                        by_token[:, 1 - j, n, group], start=True, stop=True)
                            last.then_inc(g_done, 1)
                    for n in range(TB):
                        pe.wait_ge(w_ready, (t - 1) * (GF + 1) + 1 + (n + 1) * (GF // TB))
                        if n == 0:
                            need(pe, x_ready, t - 1)
                        for c in range(UP_BLOCKS):
                            last = nc.tensor.matmul(y_ps[:, n * D:(n + 1) * D], acts[:, c, n * P:(n + 1) * P], up[:, c, :],
                                                    start=c == 0, stop=c == UP_BLOCKS - 1)
                    last.then_inc(y_done, 1)

            turns(pe, turn)

        @block.scalar
        def _(act):
            act.wait_ge(fold_done, 1)
            nc.scalar.activation(folded[:], sim_ps[:], ACT.Copy).then_inc(fold_ready, 1)

            def turn(t, j, now, before):
                if now:
                    act.wait_ge(xt_done, t + 1)
                    need(act, d_done, (t - 1) * FILLS)
                    nc.scalar.activation(xn_t[:, j, :], xt_ps[:, 0:S], ACT.Copy).then_inc(xt_ready, 1)
                    need(act, gap_ready, t)
                    for n in range(TB):
                        for p in range(2):
                            act.wait_ge(sim_done, t * 4 + n * 2 + p + 1)
                            nc.scalar.activation(sim[:, p, n], sim_ps[:, p, :].rearrange("p (h k) -> p h k", h=PH),
                                                 ACT.Copy).then_inc(sim_ready, 1)
                if before:
                    need(act, y_done, t - 1)
                    for n in range(FILLS):
                        act.wait_ge(d_done, (t - 1) * FILLS + n + 1)
                        nc.scalar.activation(acts[:, n * 2:n * 2 + 2, :], d_ps[:, n % 2],
                                             ACT.Silu if n < UP_BLOCKS // 2 else ACT.Copy).then_inc(d_ready, 1)
                if now:
                    act.wait_ge(gap_ready, t + 1)
                    need(act, spread_ready, t)
                    nc.scalar.activation(ex[:], gap[:], ACT.Exp).then_inc(exp_ready, 1)
                    act.wait_ge(spread_ready, t + 1)
                    need(act, g_done, (t - 1) * GF)
                    for n in range(TB):
                        for q in range(Q4):
                            rows = slice(q * PICKS, (q + 1) * PICKS)
                            last = nc.scalar.activation(by_token[rows, j, n, :, q, :],
                                                        spread_t[rows, n].rearrange("p r g -> p g r"), ACT.Copy)
                    last.then_inc(by_token_ready, 1)

            turns(act, turn)

        @block.vector
        def _(dve):
            nc.vector.memset(by_token[:], 0.0).then_inc(const_set, 1)
            dve.wait_ge(const_in, CONSTS * 16)
            squares = [P, 2 * TB * PH, TOP, TOP]

            def turn(t, j, now, before):
                if now:
                    steps = Steps(dve, norm_steps, t, NORM_STEPS)
                    need(dve, xt_done, t)
                    norm_vector(nc, dve, steps, nb, x, t, xn)
                    s = Steps(dve, pick_steps, t, PICK_STEPS)
                    for n in range(TB):
                        for p in range(2):
                            dve.wait_ge(sim_ready, t * 4 + n * 2 + p + 1)
                            apart(dve)
                            for h in range(PH):
                                last = nc.vector.max(best[:, p, n * PH + h, :], sim[:, p, n, h, :])
                    s.link(last)
                    apart(dve)
                    for p in range(2):
                        for n in range(TB):
                            for h in range(PH):
                                last = nc.vector.max_index(best_at[:, p, n * PH + h, :], best[:, p, n * PH + h, :], sim[:, p, n, h, :])
                    s.step(last)
                    s.link(nc.vector.tensor_tensor(sums[:], best[:, 0].unsqueeze(3).to_broadcast([P, TB * PH, TOP, TOP]),
                                                   best[:, 1].unsqueeze(2).to_broadcast([P, TB * PH, TOP, TOP]), ALU.add))
                    s.step(nc.vector.tensor_copy(at[:], best_at[:]))
                    for h in range(TB * PH):
                        last = nc.vector.max(top[:, h, :], sums[:, h].rearrange("p i j -> p (i j)"))
                    s.link(last)
                    apart(dve)
                    for h in range(TB * PH):
                        last = nc.vector.max_index(top_at[:, h, :], top[:, h, :], sums[:, h].rearrange("p i j -> p (i j)"))
                    s.step(last)
                    nc.vector.tensor_tensor(gap[:], top[:], top[:, :, 0:1].to_broadcast([P, TB * PH, TOP]),
                                            ALU.subtract).then_inc(gap_ready, 1)
                    s.settle()
                    s.step(nc.vector.tensor_scalar(out=rank_at[:, 0], in0=top_at[:], scalar1=3, scalar2=None,
                                                   op0=ALU.logical_shift_right))
                    s.link(nc.vector.tensor_scalar(out=rank_at[:, 1], in0=top_at[:], scalar1=TOP - 1, scalar2=None,
                                                   op0=ALU.bitwise_and))
                    s.link(nc.vector.tensor_copy(rank[:], rank_at[:]))
                    s.link(nc.vector.tensor_tensor(chosen[:], rank[:].rearrange("p a h s -> p (a h) s").unsqueeze(3).to_broadcast(squares),
                                                   iota[:, 0:TOP].unsqueeze(1).unsqueeze(1).to_broadcast(squares), ALU.is_equal))
                    s.link(nc.vector.tensor_tensor(chosen[:], chosen[:],
                                                   at[:].rearrange("p a h s -> p (a h) s").unsqueeze(2).to_broadcast(squares), ALU.mult))
                    s.link(nc.vector.tensor_reduce(pick[:].rearrange("p a h s -> p (a h) s"), chosen[:], AX.X, ALU.add))
                    s.link(nc.vector.tensor_scalar(out=beyond[:], in0=pick[:, 0], scalar1=EX - 0.5, scalar2=PK - 1.0,
                                                   op0=ALU.is_gt, op1=ALU.mult))
                    s.step(nc.vector.tensor_scalar(out=pick[:, 0], in0=pick[:, 0], scalar1=EX - 1.0, scalar2=None, op0=ALU.min))
                    s.link(nc.vector.tensor_tensor(pick[:, 1], pick[:, 1], beyond[:], ALU.max))
                    s.link(nc.vector.transpose(y_t[:].rearrange("p n g -> p (n g)"), pick[:, 1].rearrange("p h s -> p (h s)")))
                    wide = [P, TB * PICKS, PK]
                    need(dve, g_done, (t - 1) * GF)
                    nc.vector.tensor_tensor(ones_y[:, j].rearrange("p n g k -> p (n g) k"),
                                            y_t[:].rearrange("p n g -> p (n g)").unsqueeze(2).to_broadcast(wide),
                                            iota[:].unsqueeze(1).to_broadcast(wide), ALU.is_equal).then_inc(ones_ready, 1)
                    dve.wait_ge(exp_ready, t + 1)
                    s.link(nc.vector.tensor_reduce(total[:], ex[:], AX.X, ALU.add))
                    s.link(nc.vector.reciprocal(total[:], total[:]))
                    s.link(nc.vector.tensor_tensor(weight[:], ex[:], total[:].unsqueeze(2).to_broadcast([P, TB * PH, TOP]), ALU.mult))
                    by_x = [P, TB, EX, PICKS]
                    s.link(nc.vector.tensor_tensor(
                        spread[:], pick[:, 0].rearrange("p (n h) s -> p n (h s)", n=TB).unsqueeze(2).to_broadcast(by_x),
                        iota[:, 0:EX].unsqueeze(1).unsqueeze(3).to_broadcast(by_x), ALU.is_equal))
                    s.link(nc.vector.tensor_tensor(
                        spread[:], spread[:], weight[:].rearrange("p (n h) s -> p n (h s)", n=TB).unsqueeze(2).to_broadcast(by_x),
                        ALU.mult))
                    s.close()
                    need(dve, by_token_ready, t)
                    nc.vector.transpose(spread_t[:].rearrange("p n r g -> p (n r g)"),
                                        spread[:].rearrange("p n r s -> p (n r s)")).then_inc(spread_ready, 1)
                if before:
                    dve.wait_ge(d_ready, t * FILLS)
                    nc.vector.tensor_tensor(acts[:, EXPERT_BLOCKS:UP_BLOCKS, :], acts[:, EXPERT_BLOCKS:UP_BLOCKS, :],
                                            acts[:, UP_BLOCKS:DOWN_BLOCKS, :], ALU.mult).then_inc(w_ready, 1)
                    for n in range(TB):
                        for k in range(GF // TB):
                            f = n * (GF // TB) + k
                            dve.wait_ge(g_done, (t - 1) * GF + f + 1)
                            rows = acts[:, 0:EXPERT_BLOCKS, n * P:(n + 1) * P].rearrange("p r (q g) -> p g q r", q=Q4)[
                                :, k * BANK_GROUPS:(k + 1) * BANK_GROUPS]
                            nc.vector.tensor_tensor(rows, rows, g_ps[:, f % 2], ALU.mult).then_inc(w_ready, 1)
                    dve.wait_ge(y_done, t)
                    xb = x[:, bass.ds((t - 1) * TB, TB), :]
                    nc.vector.tensor_tensor(xb, xb, y_ps[:, 0:TB * D].rearrange("p (t d) -> p t d", t=TB),
                                            ALU.add).then_inc(x_ready, 1)

            turns(dve, turn)





def one_head_layer(nc, a, x, ident):
    from contextlib import ExitStack
    scale = D ** -0.5
    with ExitStack() as stack:
        mem = Memory(nc, stack, "k3")
        nb = NormBuffers(mem)
        w = mem.sbuf("w", [P, 4, D])
        b_qk = mem.sbuf("b_qk", [P, 2])
        b_vo = mem.sbuf("b_vo", [P, 2, D])
        mask_in = mem.sbuf("mask_in", [1, B, S], U8)
        mask = mem.sbuf("mask", [1, B, S], BF16)
        ones = mem.sbuf("ones", [1, P], BF16)
        ctx_t = mem.sbuf("ctx_t", [P, 2, S])
        xn = mem.sbuf("xn", [P, 2, TB, D])
        xn_t = mem.sbuf("xn_t", [P, 2, S])
        q_t = mem.sbuf("q_t", [P, 2, S])
        k_t = mem.sbuf("k_t", [P, 2, S])
        v = mem.sbuf("v", [P, 2, TB, D])
        neg_max = mem.sbuf("neg_max", [P, 2, TB])
        p = mem.sbuf("p", [P, 2, TB, S])
        total = mem.sbuf("total", [P, 2, TB])
        p_t = mem.sbuf("p_t", [P, TB, S])
        o_t = mem.sbuf("o_t", [P, S])
        recip = mem.sbuf("recip", [P, TB])
        xt_ps = mem.psum("xt_ps", [P, 512])
        qk_ps = mem.psum("qk_ps", [P, 2, S])
        v_ps = mem.psum("v_ps", [P, 512])
        s_ps = mem.psum("s_ps", [P, 2, TB, S])
        pt_ps = mem.psum("pt_ps", [P, TB, S])
        o_ps = mem.psum("o_ps", [P, 512])
        out_ps = mem.psum("out_ps", [P, 512])

        const_in = mem.sem("const_in")
        const_set = mem.sem("const_set")
        ctx_in = [mem.sem(f"ctx_in_{j}") for j in range(2)]
        xt_done = mem.sem("xt_done")
        xt_ready = mem.sem("xt_ready")
        qk_done = mem.sem("qk_done")
        qk_ready = mem.sem("qk_ready")
        v_done = mem.sem("v_done")
        v_ready = mem.sem("v_ready")
        s_done = mem.sem("s_done")
        max_ready = mem.sem("max_ready")
        p_ready = mem.sem("p_ready")
        pt_done = mem.sem("pt_done")
        pt_ready = mem.sem("pt_ready")
        o_done = mem.sem("o_done")
        o_ready = mem.sem("o_ready")
        out_done = mem.sem("out_done")
        x_ready = mem.sem("x_ready")
        norm_steps = mem.sem("norm_steps")
        out_steps = mem.sem("out_steps")
        block = stack.enter_context(nc.Block())

        def need(engine, sem, value):
            if not isinstance(value, int) or value > 0:
                engine.wait_ge(sem, value)

        def turns(engine, turn):
            turn(0, 0, True, False)
            turn(1, 1, True, True)
            with engine.Fori(1, B // 2) as i:
                for j in range(2):
                    turn(i * 2 + j, j, True, True)
            turn(B, 0, False, True)

        def half(t, j):
            return t // 2 if isinstance(t, int) else (t - j) // 2

        @block.sync
        def _(sync):
            for t, n in ((w, "k3_w"), (b_qk, "k3_b_qk"), (b_vo, "k3_b_vo"), (mask_in, "k3_mask")):
                sync.dma_start(t[:], a[n]).then_inc(const_in, 16)

            def turn(t, j, now, before):
                if now:
                    need(sync, qk_done, t - 1)
                    sync.dma_start(ctx_t[:, j, :], a["ctx_t"][:, bass.ds(t, 1), :]).then_inc(ctx_in[j], 16)

            turns(sync, turn)

        @block.gpsimd
        def _(pool):
            norm_power_set(nc, pool, nb)
            with pool.Fori(0, B) as b:
                norm_gpsimd(nc, pool, nb, b)

        @block.tensor
        def _(pe):
            pe.wait_ge(const_in, 64)
            pe.wait_ge(const_set, 2)

            def turn(t, j, now, before):
                if now:
                    pe.wait_ge(ctx_in[j], half(t, j) * 16 + 16)
                    need(pe, v_ready, t)
                    for n in range(TB):
                        last = nc.tensor.matmul(v_ps[:, n * D:(n + 1) * D], ctx_t[:, j, n * P:(n + 1) * P], w[:, 2, :],
                                                start=True, stop=True)
                    last.then_inc(v_done, 1)
                    pe.wait_ge(nb.ready, t + 1)
                    need(pe, xt_ready, t)
                    for n in range(TB):
                        last = nc.tensor.transpose(xt_ps[:, n * P:(n + 1) * P], xn[:, j, n, :], ident[:])
                    last.then_inc(xt_done, 1)
                    need(pe, qk_ready, t)
                    nc.tensor.matmul(qk_ps[:, 1, :], w[:, 1, :], ctx_t[:, j, :], start=True, stop=True)
                    pe.wait_ge(xt_ready, t + 1)
                    nc.tensor.matmul(qk_ps[:, 0, :], w[:, 0, :], xn_t[:, j, :], start=True, stop=True).then_inc(qk_done, 1)
                if before:
                    pe.wait_ge(p_ready, t)
                    need(pe, pt_ready, t - 1)
                    for kt in range(TB):
                        for qt in range(TB):
                            last = nc.tensor.transpose(pt_ps[:, kt, qt * P:(qt + 1) * P], p[:, 1 - j, qt, kt * P:(kt + 1) * P],
                                                       ident[:])
                    last.then_inc(pt_done, 1)
                if now:
                    pe.wait_ge(qk_ready, t + 1)
                    need(pe, p_ready, t - 1)
                    for qt in range(TB):
                        nc.tensor.matmul(s_ps[:, j, qt, :], q_t[:, j, qt * P:(qt + 1) * P], k_t[:, j, :],
                                         start=qt == 0, stop=False, skip_group_check=True)
                    nc.tensor.matmul(s_ps[:, j], ones[:], mask[:, bass.ds(t, 1), :].to_broadcast([1, TB, S]),
                                     start=False, stop=True, skip_group_check=True).then_inc(s_done, 1)
                if before:
                    pe.wait_ge(pt_ready, t)
                    pe.wait_ge(v_ready, t)
                    need(pe, o_ready, t - 1)
                    for kt in range(TB):
                        last = nc.tensor.matmul(o_ps[:, 0:S], v[:, 1 - j, kt, :], p_t[:, kt, :], start=kt == 0, stop=kt == 1)
                    last.then_inc(o_done, 1)
                    pe.wait_ge(o_ready, t)
                    need(pe, x_ready, t - 1)
                    for qt in range(TB):
                        last = nc.tensor.matmul(out_ps[:, qt * D:(qt + 1) * D], o_t[:, qt * P:(qt + 1) * P], w[:, 3, :],
                                                start=True, stop=True)
                    last.then_inc(out_done, 1)

            turns(pe, turn)

        @block.scalar
        def _(act):
            def turn(t, j, now, before):
                if now:
                    act.wait_ge(xt_done, t + 1)
                    need(act, qk_done, t - 1)
                    nc.scalar.activation(xn_t[:, j, :], xt_ps[:, 0:S], ACT.Copy).then_inc(xt_ready, 1)
                if before:
                    act.wait_ge(pt_done, t)
                    need(act, o_done, t - 1)
                    nc.scalar.activation(p_t[:], pt_ps[:], ACT.Copy).then_inc(pt_ready, 1)
                    act.wait_ge(o_done, t)
                    need(act, out_done, t - 1)
                    nc.scalar.activation(o_t[:], o_ps[:, 0:S], ACT.Copy).then_inc(o_ready, 1)
                if now:
                    act.wait_ge(max_ready, t + 1)
                    need(act, pt_done, t - 1)
                    need(act, x_ready, t - 1)
                    for qt in range(TB):
                        last = nc.scalar.activation(p[:, j, qt, :], s_ps[:, j, qt, :], ACT.Exp, bias=neg_max[:, j, qt:qt + 1],
                                                    accum_out=total[:, j, qt:qt + 1])
                    last.then_inc(p_ready, 1)

            turns(act, turn)

        @block.vector
        def _(dve):
            nc.vector.memset(ones[:], 1.0).then_inc(const_set, 1)
            dve.wait_ge(const_in, 64)
            nc.vector.tensor_scalar(out=mask[:], in0=mask_in[:], scalar1=0.0, scalar2=MASKED,
                                    op0=ALU.is_equal, op1=ALU.mult).then_inc(const_set, 1)

            def turn(t, j, now, before):
                if now:
                    steps = Steps(dve, norm_steps, t, NORM_STEPS)
                    need(dve, xt_done, t - 1)
                    norm_vector(nc, dve, steps, nb, x, t, xn[:, j])
                    dve.wait_ge(v_done, t + 1)
                    need(dve, o_done, t - 1)
                    nc.vector.tensor_tensor(v[:, j], v_ps[:, 0:TB * D].rearrange("p (t d) -> p t d", t=TB),
                                            b_vo[:, 0:1, :].to_broadcast([P, TB, D]), ALU.add).then_inc(v_ready, 1)
                    dve.wait_ge(qk_done, t + 1)
                    need(dve, s_done, t - 1)
                    nc.vector.tensor_scalar(out=k_t[:, j, :], in0=qk_ps[:, 1, :], scalar1=b_qk[:, 1:2], scalar2=None, op0=ALU.add)
                    nc.vector.tensor_scalar(out=q_t[:, j, :], in0=qk_ps[:, 0, :], scalar1=b_qk[:, 0:1], scalar2=scale,
                                            op0=ALU.add, op1=ALU.mult).then_inc(qk_ready, 1)
                    dve.wait_ge(s_done, t + 1)
                    need(dve, p_ready, t - 1)
                    nc.vector.tensor_reduce(neg_max[:, j, :], s_ps[:, j], AX.X, ALU.max, negate=True).then_inc(max_ready, 1)
                if before:
                    out = Steps(dve, out_steps, t - 1, 3)
                    xb = x[:, bass.ds((t - 1) * TB, TB), :]
                    need(dve, x_ready, t - 1)
                    out.step(nc.vector.tensor_tensor(xb, xb, b_vo[:, 1:2, :].to_broadcast([P, TB, D]), ALU.add))
                    dve.wait_ge(p_ready, t)
                    out.link(nc.vector.reciprocal(recip[:], total[:, 1 - j, :]))
                    dve.wait_ge(out_done, t)
                    out.step(nc.vector.scalar_tensor_tensor(out=x[:, bass.ds((t - 1) * TB, 1), :], in0=out_ps[:, 0:D],
                                                            scalar=recip[:, 0:1], in1=x[:, bass.ds((t - 1) * TB, 1), :],
                                                            op0=ALU.mult, op1=ALU.add))
                    nc.vector.scalar_tensor_tensor(out=x[:, bass.ds((t - 1) * TB + 1, 1), :], in0=out_ps[:, D:2 * D],
                                                   scalar=recip[:, 1:2], in1=x[:, bass.ds((t - 1) * TB + 1, 1), :],
                                                   op0=ALU.mult, op1=ALU.add).then_inc(x_ready, 1)
                    out.close()

            turns(dve, turn)



def build(nc, a, out):
    from contextlib import ExitStack
    with ExitStack() as stack:
        mem = Memory(nc, stack, "all")
        x = mem.sbuf("x", [P, NT, D])
        ident = mem.sbuf("ident", [P, P])
        zeros = mem.sbuf("zeros", [P, D])
        slots_x = nc.dram_tensor("slots_x", (MOST_SLOTS, D), F32, kind="Internal").ap()
        slots_y = nc.dram_tensor("slots_y", (MOST_SLOTS, D), F32, kind="Internal").ap()
        start_in = mem.sem("start_in")
        zeros_set = mem.sem("zeros_set")
        stored = mem.sem("stored")
        Memory.carried = mem.sem("carried")
        Memory.scattered = mem.sem("scattered")
        Memory.gathered = [mem.sem(f"gathered_{t}") for t in range(NT)]
        Memory.rounds = 0
        Memory.used = []
        with nc.Block() as block:
            @block.sync
            def _(sync):
                sync.dma_start(x[:], a["x"]).then_inc(start_in, 16)
                sync.dma_start(ident[:], a["ident"]).then_inc(start_in, 16)
                sync.wait_ge(zeros_set, 1)
                sync.dma_start(slots_x.rearrange("(n p) d -> p n d", p=P),
                               zeros[:].unsqueeze(1).to_broadcast([P, MOST_SLOTS // P, D])).then_inc(start_in, 16)
                sync.wait_ge(start_in, 48)

            @block.vector
            def _(dve):
                nc.vector.memset(zeros[:], 0.0).then_inc(zeros_set, 1)
        with ExitStack() as layer:
            m = Memory(nc, layer, "l0")
            xn_t = m.sbuf("xn_t", [P, B * S])
            cols = (m.sbuf("g_col", [P, TB, BH]), m.sbuf("e_col", [P, TB, BH]), m.sbuf("neg_g_row", [1, BH * S]))
            mlstm_gates(nc, a, x, ident, xn_t, cols)
            mlstm_attention(nc, a, x, xn_t, cols)
        clear_semaphores(nc)
        mixture_layer(nc, a, x, ident, MIX0, slots_x, slots_y)
        clear_semaphores(nc)

        heads_layer(nc, a, x, ident, HEADS1)
        clear_semaphores(nc)

        mixture_layer(nc, a, x, ident, MIX1, slots_x, slots_y)
        clear_semaphores(nc)

        heads_layer(nc, a, x, ident, HEADS2)
        clear_semaphores(nc)

        keyed_layer(nc, a, x, ident)
        clear_semaphores(nc)

        one_head_layer(nc, a, x, ident)
        clear_semaphores(nc)

        mixture_layer(nc, a, x, ident, MIX3, slots_x, slots_y)
        with nc.Block() as block:
            @block.sync
            def _(sync):
                sync.dma_start(out, x[:]).then_inc(stored, 16)
                sync.wait_ge(stored, 16)


def rows_by_tile(m):
    return m.reshape(NT, P, D).transpose(1, 0, 2)


def laid_out(v):
    g = {n: np.asarray(m) for n, m in v.items()}
    z = {}
    z["x"] = rows_by_tile(g["x"])
    z["ctx_n"] = rows_by_tile(g["ctx_1024"])
    z["ctx_t"] = g["ctx_1024"].transpose(2, 0, 1)
    z["ident"] = np.eye(P, dtype=np.float32)
    w = np.zeros((P, 3, 36), np.float32)
    w[:, :, 0:MH] = g["L0_xattn_w_igate"].reshape(MH, 3, D).transpose(2, 1, 0)
    w[:, :, 32:32 + MH] = g["L0_xattn_w_fgate"].reshape(MH, 3, D).transpose(2, 1, 0)
    z["w_gates"] = w
    z["b_gates"] = np.stack([np.repeat(g["L0_xattn_b_igate"], B), np.repeat(g["L0_xattn_b_fgate"], B)], axis=1)
    s = np.arange(S)
    z["causal"] = np.where(np.arange(P)[:, None] <= s[None, :], 0.0, -1e30).astype(np.float32)
    z["ln_scale"] = np.tile(g["L0_xattn_ln_weight"], (P, 1))
    z["before"] = np.triu(np.ones((P, P), np.float32), 1)
    z["iota_e"] = np.tile(np.arange(E, dtype=np.float32), (P, 1))
    z["keep"] = np.tile((np.arange(NT) > 0).astype(np.float32), (P, E, 1))
    z["tile_starts"] = np.tile(np.arange(NT, dtype=np.float32) * P, (P, 1))
    none = np.zeros(E, np.float32)
    for mix, router, biases, w1, w2 in (
            (MIX0, g["L0_ffn_gate_w"].T, (g["L0_ffn_gate_b"], g["L0_ffn_expert_bias"]), g["L0_ffn_w1"], g["L0_ffn_w2"]),
            (MIX1, g["L1_ffn_router_w"], (g["L1_ffn_router_b"], none), g["L1_ffn_w1"], g["L1_ffn_w2"]),
            (MIX3, g["L3_ffn_Wr"], (g["L3_ffn_br"], none), g["L3_ffn_W1"], g["L3_ffn_W2"])):
        n = mix.name
        z[n + "_router"] = router
        z[n + "_router_b"] = np.tile(np.stack(biases), (P, 1, 1))
        z[n + "_iota_s"] = np.tile(np.arange(mix.tiles, dtype=np.float32), (P, 1))
        z[n + "_w1"] = w1.transpose(1, 0, 2).reshape(P, E * mix.wide)
        z[n + "_w2"] = w2.reshape(E, mix.h // P, P, D).transpose(2, 0, 1, 3).reshape(P, E * mix.h)
    z["f0_b1"], z["f0_b2"] = g["L0_ffn_b1"].reshape(1, -1), g["L0_ffn_b2"].reshape(1, -1)
    z["f3_b1"], z["f3_b2"] = g["L3_ffn_b1"].reshape(1, -1), g["L3_ffn_b2"].reshape(1, -1)

    def slots(w):
        heads = w.reshape(-1, G, HG, HD)
        return np.concatenate([heads] * 3 + [np.zeros_like(heads)], axis=3).reshape(-1, G, P)

    z["ctx_t"] = g["ctx_1024"].transpose(2, 0, 1)
    row = np.arange(P) % SLOT
    low = np.stack([(row >= 2 * HD) & (row < 3 * HD), (row >= HD) & (row < 2 * HD)], axis=1).astype(np.float32)
    ones = ((row >= MAX_ROW) & (row < MAX_ROW + 2)).astype(np.float32)
    nil = np.zeros(D, np.float32)
    for n, q, k, v, o, bq, bk, bv, bo in (
            ("h1", *(g["L1_xattn_W_" + c].T for c in "qkvo"), nil, nil, nil, nil),
            ("h2", *(g["L2_xattn_W" + c].T for c in "qkvo"), *(g["L2_xattn_b" + c] for c in "qkvo"))):
        z[n + "_w_qk"] = np.stack([slots(q), slots(k)], axis=1)
        z[n + "_w_v"], z[n + "_w_o"] = v, o
        z[n + "_b_v"], z[n + "_b_o"] = np.tile(bv, (P, 1)), np.tile(bo, (P, 1))
        b = np.stack([slots(bq[None])[0].T, slots(bk[None])[0].T], axis=1)
        z[n + "_b_low"] = np.where(low[:, :, None] > 0, b, 0.0).astype(np.float32)
        b[:, 1] = np.where(ones[:, None] > 0, np.float32(1.0), b[:, 1])
        z[n + "_b_qk"] = b
        z[n + "_low"] = low
    mask = g["mask_1x1xSxS2_ik0"][0, 0]
    z["h1_mask"] = np.stack([mask.reshape(TB, P, S), mask.T.reshape(TB, P, S)]).transpose(2, 0, 1, 3)



    z["iota"] = np.tile(np.arange(PK, dtype=np.float32), (P, 1))
    z["pk_w_q"] = g["L2_ffn_Wq"].reshape(2 * PH, HALF, D).transpose(1, 0, 2)
    z["pk_keys"] = g["L2_ffn_keys"].transpose(3, 2, 0, 1).reshape(HALF, 2 * PH, PK)
    z["pk_down"] = np.concatenate([g["L2_ffn_down_embed"].reshape(EX, PK, D), g["L2_ffn_Wg"].reshape(MLP_BLOCKS, P, D),
                                   g["L2_ffn_Wu"].reshape(MLP_BLOCKS, P, D)]).transpose(2, 0, 1)
    z["pk_up"] = np.concatenate([g["L2_ffn_up_embed"].reshape(EX, PK, D),
                                 g["L2_ffn_Wd"].T.reshape(MLP_BLOCKS, P, D)]).transpose(1, 0, 2)

    z["k3_w"] = np.stack([g["L3_xattn_W" + c] for c in "qkvo"], axis=1)
    z["k3_b_qk"] = np.stack([g["L3_xattn_bq"], g["L3_xattn_bk"]], axis=1)
    z["k3_b_vo"] = np.tile(np.stack([g["L3_xattn_bv"], g["L3_xattn_bo"]]), (P, 1, 1))
    z["k3_mask"] = g["mask_BxS2_bk0"][None]
    return {n: np.ascontiguousarray(m) for n, m in z.items()}


def kernel(**inputs):
    import concourse.bacc as bacc
    from concourse.bass_utils import run_bass_kernel_spmd

    arrays = laid_out(inputs)
    nc = bacc.Bacc("TRN2", target_bir_lowering=False, num_devices=1)
    a = {n: nc.dram_tensor(f"in_{n}", m.shape, mybir.dt.from_np(m.dtype), kind="ExternalInput").ap()
         for n, m in arrays.items()}
    out = nc.dram_tensor("out_x", (P, NT, D), F32, kind="ExternalOutput").ap()
    build(nc, a, out)
    r = run_bass_kernel_spmd(nc, [{f"in_{n}": m for n, m in arrays.items()}], core_ids=[0])
    return r.results[0]["out_x"].transpose(1, 0, 2).reshape(B, S, D)
```

```python
import numpy as np

import concourse.bass as bass
import concourse.mybir as mybir

F32 = mybir.dt.float32
F32R = mybir.dt.float32r
BF16 = mybir.dt.bfloat16
I32 = mybir.dt.int32
U32 = mybir.dt.uint32
U8 = mybir.dt.uint8
ALU = mybir.AluOpType
ACT = mybir.ActivationFunctionType
AX = mybir.AxisListType

P = 128
D = 128
B = 8
S = 256
TB = S // P
NT = B * TB
LN_EPS = 1e-5


class Memory:

    carried = None
    used = []
    zeroed = None
    scattered = None
    gathered = []
    loaded = {}
    rounds = 0

    def __init__(self, nc, stack, prefix):
        self.nc, self.stack, self.prefix = nc, stack, prefix

    def sbuf(self, name, shape, dtype=F32):
        return self.stack.enter_context(self.nc.sbuf_tensor(f"{self.prefix}_{name}", shape, dtype))

    def psum(self, name, shape, dtype=F32):
        return self.stack.enter_context(self.nc.psum_tensor(f"{self.prefix}_{name}", shape, dtype))

    def sem(self, name):
        sem = self.stack.enter_context(self.nc.semaphore(f"{self.prefix}_{name}"))
        Memory.used.append(sem)
        return sem


def apart(engine):
    engine.sem_inc(Memory.carried, 1)


def clear_semaphores(nc):
    with nc.Block() as block:
        @block.gpsimd
        def _(pool):
            for sem in Memory.used:
                pool.sem_clear(sem)
    Memory.used = []


class Steps:

    def __init__(self, engine, sem, turn=0, per_turn=0):
        self.engine, self.sem, self.base, self.n, self.per_turn = engine, sem, turn * per_turn, 0, per_turn

    def step(self, instruction):
        instruction.then_inc(self.sem, 1)
        self.n += 1

    def settle(self):
        self.engine.wait_ge(self.sem, self.base + self.n)

    def link(self, instruction):
        self.step(instruction)
        self.settle()

    def close(self):
        assert not self.per_turn or self.n == self.per_turn, (self.n, self.per_turn)


class NormBuffers:

    def __init__(self, mem):
        self.stats = mem.sbuf("ln_stats", [P, TB, 6])
        self.mean_var = mem.sbuf("ln_mean_var", [P, TB, 2])
        self.var_eps = mem.sbuf("ln_var_eps", [P, TB])
        self.rstd = mem.sbuf("ln_rstd", [P, TB])
        self.power = mem.sbuf("ln_power", [P, TB])
        self.power_set = mem.sem("ln_power_set")
        self.moments_ready = mem.sem("ln_moments_ready")
        self.rstd_ready = mem.sem("ln_rstd_ready")
        self.ready = mem.sem("ln_ready")

NORM_STEPS = 4


def norm_moments(nc, dve, steps, nb, x, b):
    for t in range(TB):
        steps.step(nc.vector.bn_stats(nb.stats[:, t, :], x[:, bass.ds(b * TB + t, 1), :]))
    steps.settle()
    apart(dve)
    steps.step(nc.vector.bn_aggr(nb.mean_var[:, 0, :], nb.stats[:, 0, :]))
    nc.vector.bn_aggr(nb.mean_var[:, 1, :], nb.stats[:, 1, :]).then_inc(nb.moments_ready, 1)


def norm_apply(nc, dve, steps, nb, x, b, out):
    dve.wait_ge(nb.rstd_ready, b * 2 + 2)
    steps.step(nc.vector.tensor_scalar(out=out[:, 0, :], in0=x[:, bass.ds(b * TB, 1), :],
                                       scalar1=nb.mean_var[:, 0, 0:1], scalar2=nb.rstd[:, 0:1],
                                       op0=ALU.subtract, op1=ALU.mult))
    nc.vector.tensor_scalar(out=out[:, 1, :], in0=x[:, bass.ds(b * TB + 1, 1), :],
                            scalar1=nb.mean_var[:, 1, 0:1], scalar2=nb.rstd[:, 1:2],
                            op0=ALU.subtract, op1=ALU.mult).then_inc(nb.ready, 1)
    dve.wait_ge(nb.ready, b + 1)


def norm_vector(nc, dve, steps, nb, x, b, out):
    norm_moments(nc, dve, steps, nb, x, b)
    norm_apply(nc, dve, steps, nb, x, b, out)


def norm_power_set(nc, pool, nb):
    nc.gpsimd.memset(nb.power[:], -0.5).then_inc(nb.power_set, 1)
    pool.wait_ge(nb.power_set, 1)


def norm_gpsimd(nc, pool, nb, b):
    pool.wait_ge(nb.moments_ready, b + 1)
    apart(pool)
    nc.gpsimd.tensor_scalar(out=nb.var_eps[:], in0=nb.mean_var[:, :, 1], scalar1=LN_EPS, scalar2=None,
                            op0=ALU.add).then_inc(nb.rstd_ready, 1)
    pool.wait_ge(nb.rstd_ready, b * 2 + 1)
    nc.gpsimd.tensor_tensor(nb.rstd[:], nb.var_eps[:], nb.power[:], ALU.pow).then_inc(nb.rstd_ready, 1)



MH = 4
MD = D // MH
BH = MH * B
MSCALE = 1.0 / MD ** 0.5


def mlstm_gates(nc, a, x, ident, xn_t, cols, later_loads):
    g_col, e_col, neg_g_row = cols
    from contextlib import ExitStack
    with ExitStack() as stack:
        mem = Memory(nc, stack, "m0")
        nb = NormBuffers(mem)
        xn = mem.sbuf("xn", [P, 2, TB, D])
        ctx_t = mem.sbuf("ctx_t", [P, B, S])
        w_gates = mem.sbuf("w_gates", [P, 3, 36])
        b_gates = mem.sbuf("b_gates", [BH, 2])
        gates = mem.sbuf("gates", [36, B, S])
        i_rows = mem.sbuf("i_rows", [BH, S])
        f_rows = mem.sbuf("f_rows", [BH, S])
        abs_f = mem.sbuf("abs_f", [BH, S])
        exp_f = mem.sbuf("exp_f", [BH, S])
        ln_f = mem.sbuf("ln_f", [BH, S])
        log_f = mem.sbuf("log_f", [BH, S])
        ones = mem.sbuf("ones", [BH, S])
        f_sum = mem.sbuf("f_sum", [BH, S])
        g_rows = mem.sbuf("g_rows", [BH, S])
        g_max = mem.sbuf("g_max", [BH, S])
        neg_g = mem.sbuf("neg_g", [BH, S])
        top = mem.sbuf("top", [BH, S])
        t_ps = mem.psum("t_ps", [P, 2, 512])
        gate_ps = mem.psum("gate_ps", [36, 2, 512])
        col_ps = mem.psum("col_ps", [P, 512])

        const_in = mem.sem("const_in")
        transposed = mem.sem("transposed")
        xn_t_ready = mem.sem("xn_t_ready")
        projected = mem.sem("projected")
        gates_ready = mem.sem("gates_ready")
        rows_in = mem.sem("rows_in")
        steps_done = mem.sem("steps_done")
        row_steps = mem.sem("row_steps")
        abs_ready = mem.sem("abs_ready")
        exp_ready = mem.sem("exp_ready")
        log_ready = mem.sem("log_ready")
        scans_ready = mem.sem("scans_ready")
        cols_ready = mem.sem("cols_ready")
        cols_out = mem.sem("cols_out")
        row_out = mem.sem("row_out")
        block = stack.enter_context(nc.Block())

        @block.sync
        def _(sync):
            sync.dma_start(w_gates[:], a["w_gates"]).then_inc(const_in, 16)
            sync.dma_start(b_gates[:], a["b_gates"]).then_inc(const_in, 16)
            sync.dma_start(ctx_t[:], a["ctx_t"]).then_inc(const_in, 16)
            sync.wait_ge(gates_ready, B + 2)
            for h in range(MH):
                for rows, at in ((f_rows, 32 + h), (i_rows, h)):
                    sync.dma_start(rows[h * B:(h + 1) * B, :], gates[at:at + 1, :, :]).then_inc(rows_in, 16)
            sync.wait_ge(scans_ready, 2)
            sync.dma_start(neg_g_row[0:1, :].rearrange("o (r s) -> o r s", s=S),
                           neg_g[:, :]).then_inc(row_out, 16)
            sync.wait_ge(row_out, 16)

        @block.gpsimd
        def _(pool):
            norm_power_set(nc, pool, nb)
            with pool.Fori(0, B) as b:
                norm_gpsimd(nc, pool, nb, b)

        @block.vector
        def _(dve):
            nc.vector.memset(ones[:], 1.0).then_inc(row_steps, 1)
            with dve.Fori(0, B // 2) as i:
                for j in range(2):
                    b = i * 2 + j
                    steps = Steps(dve, steps_done, b, NORM_STEPS)
                    dve.wait_ge(transposed, b + 1)
                    norm_vector(nc, dve, steps, nb, x, b, xn[:, j])
                    steps.close()
            dve.wait_ge(rows_in, 2 * MH * 16)
            rows = Steps(dve, row_steps)
            rows.n = 1
            rows.link(nc.vector.tensor_scalar(out=f_rows[:], in0=f_rows[:], scalar1=b_gates[:, 1:2],
                                              scalar2=None, op0=ALU.add))
            nc.vector.scalar_tensor_tensor(out=abs_f[:], in0=f_rows[:], scalar=-1.0, in1=f_rows[:],
                                           op0=ALU.mult, op1=ALU.max).then_inc(abs_ready, 1)
            dve.wait_ge(log_ready, 1)
            rows.link(nc.vector.scalar_tensor_tensor(out=log_f[:], in0=f_rows[:], scalar=0.0, in1=ln_f[:],
                                                     op0=ALU.min, op1=ALU.subtract))
            rows.link(nc.vector.tensor_tensor_scan(f_sum[:], ones[:], log_f[:], 0.0, ALU.mult, ALU.add))
            rows.link(nc.vector.scalar_tensor_tensor(out=g_rows[:], in0=i_rows[:], scalar=b_gates[:, 0:1],
                                                     in1=f_sum[:], op0=ALU.add, op1=ALU.subtract))
            rows.link(nc.vector.tensor_tensor_scan(g_max[:], g_rows[:], g_rows[:], -3e38, ALU.max, ALU.max))
            nc.vector.tensor_tensor(top[:], f_sum[:], g_max[:], ALU.add).then_inc(scans_ready, 1)
            nc.vector.tensor_scalar(out=neg_g[:], in0=g_max[:], scalar1=-1.0, scalar2=None,
                                    op0=ALU.mult).then_inc(scans_ready, 1)

        @block.tensor
        def _(pe):
            pe.wait_ge(const_in, 48)
            pe.sem_inc(transposed, 2)
            with pe.Fori(0, B // 2) as i:
                for j in range(2):
                    b = i * 2 + j
                    pe.wait_ge(nb.ready, b + 1)
                    pe.wait_ge(xn_t_ready, b + 1)
                    for t in range(TB):
                        last = nc.tensor.transpose(t_ps[:, j, t * P:(t + 1) * P], xn[:, j, t, :], ident[:])
                    last.then_inc(transposed, 1)
                    pe.wait_ge(gates_ready, b + 1)
                    pe.wait_ge(xn_t_ready, b + 3)
                    nc.tensor.matmul(gate_ps[:, j, 0:S], w_gates[:, 0, :], xn_t[:, bass.ds(b * S, S)],
                                     start=True, stop=False)
                    nc.tensor.matmul(gate_ps[:, j, 0:S], w_gates[:, 1, :], ctx_t[:, bass.ds(b, 1), :],
                                     start=False, stop=False)
                    nc.tensor.matmul(gate_ps[:, j, 0:S], w_gates[:, 2, :], ctx_t[:, bass.ds(b, 1), :],
                                     start=False, stop=True).then_inc(projected, 1)
            pe.wait_ge(scans_ready, 1)
            for n, rows in enumerate((g_rows, top)):
                for t in range(TB):
                    last = nc.tensor.transpose(col_ps[:, (n * TB + t) * BH:(n * TB + t + 1) * BH],
                                               rows[:, t * P:(t + 1) * P], ident[0:BH, 0:BH])
            last.then_inc(cols_ready, 1)

        @block.scalar
        def _(act):
            act.wait_ge(const_in, 48)
            later_loads(act)
            act.sem_inc(xn_t_ready, 2)
            act.sem_inc(gates_ready, 2)
            with act.Fori(0, B // 2) as i:
                for j in range(2):
                    b = i * 2 + j
                    act.wait_ge(transposed, b + 3)
                    nc.scalar.activation(xn_t[:, bass.ds(b * S, S)], t_ps[:, j, 0:S], ACT.Copy).then_inc(xn_t_ready, 1)
                    act.wait_ge(projected, b + 1)
                    nc.scalar.activation(gates[:, bass.ds(b, 1), :], gate_ps[:, j, 0:S], ACT.Copy).then_inc(gates_ready, 1)
            act.wait_ge(abs_ready, 1)
            nc.scalar.activation(exp_f[:], abs_f[:], ACT.Exp, scale=-1.0).then_inc(exp_ready, 1)
            act.wait_ge(exp_ready, 1)
            nc.scalar.activation(ln_f[:], exp_f[:], ACT.Ln, bias=1.0).then_inc(log_ready, 1)
            act.wait_ge(cols_ready, 1)
            nc.scalar.activation(g_col[:].rearrange("p t r -> p (t r)"), col_ps[:, 0:TB * BH],
                                 ACT.Copy).then_inc(cols_out, 1)
            nc.scalar.activation(e_col[:].rearrange("p t r -> p (t r)"), col_ps[:, TB * BH:2 * TB * BH],
                                 ACT.Exp, scale=-1.0).then_inc(cols_out, 1)
            act.wait_ge(cols_out, 2)


def mlstm_attention(nc, a, x, xn_t, cols):
    g_col, e_col, neg_g_row = cols
    W = S + P
    from contextlib import ExitStack
    with ExitStack() as stack:
        mem = Memory(nc, stack, "m1")
        ctx_t = mem.sbuf("ctx_t", [P, 2, S])
        q_t = mem.sbuf("q_t", [P, 2, S])
        v_one = mem.sbuf("v_one", [P, 2, TB, MH, MD + 1])
        causal = mem.sbuf("causal", [P, S])
        ln_scale = mem.sbuf("ln_scale", [P, D])
        ones = mem.sbuf("ones", [1, P])
        g_now = mem.sbuf("g_now", [P, 2, TB, MH])
        e_now = mem.sbuf("e_now", [P, TB, MH])
        d_arg = mem.sbuf("d_arg", [P, 2, MH, W])
        d_exp = mem.sbuf("d_exp", [P, 2, MH, W])
        c = mem.sbuf("c", [P, 2, MH, W])
        den = mem.sbuf("den", [P, TB * MH, 1])
        h = mem.sbuf("h", [P, TB * MH, MD])
        sq = mem.sbuf("sq", [P, TB * MH, MD])
        mean = mem.sbuf("mean", [P, TB * MH])
        var = mem.sbuf("var", [P, TB * MH])
        rstd = mem.sbuf("rstd", [P, TB * MH])
        power = mem.sbuf("power", [P, TB * MH])
        g_ps = mem.psum("g_ps", [P, MH * S])
        s_ps = mem.psum("s_ps", [P, MH, 512])
        o_ps = mem.psum("o_ps", [P, TB * MH, MD + 1])

        const_in = mem.sem("const_in")
        ones_set = mem.sem("ones_set")
        ctx_in = [mem.sem(f"ctx_in_{j}") for j in range(2)]
        q_ready = mem.sem("q_ready")
        g_spread = mem.sem("g_spread")
        g_read = mem.sem("g_read")
        d_ready = mem.sem("d_ready")
        scores_ready = mem.sem("scores_ready")
        c_ready = mem.sem("c_ready")
        out_ready = mem.sem("out_ready")
        out_read = mem.sem("out_read")
        var_ready = mem.sem("var_ready")
        rstd_ready = mem.sem("rstd_ready")
        steps_done = mem.sem("steps_done")
        arg_steps = mem.sem("arg_steps")
        block = stack.enter_context(nc.Block())

        def turns(engine, turn):
            turn(0, 0, True, False)
            turn(1, 1, True, True)
            with engine.Fori(1, B // 2) as i:
                for j in range(2):
                    turn(i * 2 + j, j, True, True)
            turn(B, 0, False, True)

        @block.sync
        def _(sync):
            sync.dma_start(causal[:], a["causal"]).then_inc(const_in, 16)
            sync.dma_start(ln_scale[:], a["ln_scale"]).then_inc(const_in, 16)
            sync.wait_ge(ones_set, 2)
            with sync.Fori(0, B // 2) as i:
                for j in range(2):
                    b = i * 2 + j
                    sync.wait_ge(out_ready, b + 1)
                    sync.dma_start(ctx_t[:, j, :], a["ctx_t"][:, bass.ds(b, 1), :]).then_inc(ctx_in[j], 16)
                    for t in range(TB):
                        sync.dma_start(v_one[:, j, t, :, 0:MD],
                                       a["ctx_n"][:, bass.ds(b * TB + t, 1), :].rearrange("p t (h d) -> p (t h) d", d=MD)).then_inc(ctx_in[j], 16)

        @block.gpsimd
        def _(pool):
            nc.gpsimd.memset(power[:], -0.5).then_inc(rstd_ready, 1)

            def turn(b, j, now, before):
                if now:
                    pool.wait_ge(out_ready, b + 1)
                    apart(pool)
                    nc.gpsimd.tensor_copy(q_t[:, j, :], xn_t[:, bass.ds(b * S, S)]).then_inc(q_ready, 1)
                if before:
                    pool.wait_ge(var_ready, b)
                    pool.wait_ge(rstd_ready, b)
                    nc.gpsimd.tensor_tensor(rstd[:], var[:], power[:], ALU.pow).then_inc(rstd_ready, 1)

            turns(pool, turn)

        @block.vector
        def _(dve):
            nc.vector.memset(v_one[:], 1.0).then_inc(ones_set, 1)
            nc.vector.memset(ones[:], 1.0).then_inc(ones_set, 1)
            dve.wait_ge(const_in, 32)
            nc.vector.tensor_scalar(out=ln_scale[:], in0=ln_scale[:], scalar1=1.0, scalar2=None,
                                    op0=ALU.add).then_inc(ones_set, 1)
            dve.wait_ge(ones_set, 3)
            dve.sem_inc(g_read, 1)
            dve.sem_inc(c_ready, 1)
            dve.sem_inc(out_read, 1)

            def output(b):
                steps = Steps(dve, steps_done, b, 13)
                steps.link(nc.vector.tensor_copy(e_now[:], e_col[:].rearrange("p t (h b) -> p t h b", b=B)[:, :, :, bass.ds(b, 1)]))
                dve.wait_ge(out_ready, b + 3)
                steps.link(nc.vector.scalar_tensor_tensor(
                    out=den[:, :, 0], in0=o_ps[:, :, MD], scalar=-1.0,
                    in1=e_now[:].rearrange("p t h -> p (t h)"), op0=ALU.mult, op1=ALU.max))
                steps.link(nc.vector.tensor_tensor(den[:, :, 0], o_ps[:, :, MD], den[:, :, 0], ALU.max))
                steps.link(nc.vector.tensor_scalar(out=den[:], in0=den[:], scalar1=1e-6, scalar2=None, op0=ALU.add))
                steps.link(nc.vector.reciprocal(den[:], den[:]))
                nc.vector.tensor_tensor(h[:], o_ps[:, :, 0:MD], den[:].to_broadcast([P, TB * MH, MD]),
                                        ALU.mult).then_inc(out_read, 1)
                dve.wait_ge(out_read, b + 2)
                steps.link(nc.vector.tensor_reduce(mean[:], h[:], AX.X, ALU.add))
                steps.link(nc.vector.tensor_scalar(out=mean[:], in0=mean[:], scalar1=1.0 / MD, scalar2=None, op0=ALU.mult))
                steps.link(nc.vector.tensor_tensor(h[:], h[:], mean[:].unsqueeze(2).to_broadcast([P, TB * MH, MD]), ALU.subtract))
                steps.link(nc.vector.tensor_tensor(sq[:], h[:], h[:], ALU.mult))
                steps.link(nc.vector.tensor_reduce(var[:], sq[:], AX.X, ALU.add))
                nc.vector.tensor_scalar(out=var[:], in0=var[:], scalar1=1.0 / MD, scalar2=LN_EPS,
                                        op0=ALU.mult, op1=ALU.add).then_inc(var_ready, 1)
                dve.wait_ge(rstd_ready, b + 2)
                steps.link(nc.vector.tensor_tensor(h[:], h[:], rstd[:].unsqueeze(2).to_broadcast([P, TB * MH, MD]), ALU.mult))
                flat = h[:].rearrange("p (t h) d -> p t (h d)", t=TB)
                steps.link(nc.vector.tensor_tensor(flat, flat, ln_scale[:].unsqueeze(1).to_broadcast([P, TB, D]), ALU.mult))
                steps.link(nc.vector.tensor_tensor(x[:, bass.ds(b * TB, TB), :], x[:, bass.ds(b * TB, TB), :], flat, ALU.add))
                steps.close()

            def turn(b, j, now, before):
                if now:
                    steps = Steps(dve, arg_steps, b, 2 * MH)
                    steps.link(nc.vector.tensor_copy(g_now[:, j], g_col[:].rearrange("p t (h b) -> p t h b", b=B)[:, :, :, bass.ds(b, 1)]))
                    dve.wait_ge(g_spread, b + 1)
                    for n in range(MH):
                        steps.step(nc.vector.scalar_tensor_tensor(
                            out=d_arg[:, j, n, 0:S], in0=g_ps[:, n * S:(n + 1) * S],
                            scalar=g_now[:, j, 0, n:n + 1], in1=causal[:], op0=ALU.add, op1=ALU.min))
                        later = nc.vector.scalar_tensor_tensor(
                            out=d_arg[:, j, n, S:W], in0=g_ps[:, n * S + P:(n + 1) * S],
                            scalar=g_now[:, j, 1, n:n + 1], in1=causal[:, 0:P], op0=ALU.add, op1=ALU.min)
                        if n < MH - 1:
                            steps.step(later)
                    later.then_inc(g_read, 1)
                    steps.close()
                    dve.wait_ge(scores_ready, b + 1)
                    dve.wait_ge(d_ready, b + 1)
                    nc.vector.scalar_tensor_tensor(out=c[:, j], in0=s_ps[:, :, 0:W], scalar=MSCALE, in1=d_exp[:, j],
                                                   op0=ALU.mult, op1=ALU.mult).then_inc(c_ready, 1)
                if before:
                    output(b - 1)

            turns(dve, turn)

        @block.tensor
        def _(pe):
            pe.wait_ge(ones_set, 3)
            pe.sem_inc(out_ready, 2)

            def turn(b, j, now, before):
                if now:
                    pe.wait_ge(g_read, b + 1)
                    for n in range(MH):
                        last = nc.tensor.matmul(g_ps[:, n * S:(n + 1) * S], ones[:],
                                                neg_g_row[0:1, bass.ds(b * S + n * (B * S), S)],
                                                start=True, stop=True)
                    last.then_inc(g_spread, 1)
                    half = b // 2 if isinstance(b, int) else (b - j) // 2
                    pe.wait_ge(ctx_in[j], half * 48 + 48)
                    pe.wait_ge(q_ready, b + 1)
                    pe.wait_ge(c_ready, b + 1)
                    for n in range(MH):
                        rows = slice(n * MD, (n + 1) * MD)
                        nc.tensor.matmul(s_ps[:, n, 0:S], ctx_t[rows, j, 0:P], q_t[rows, j, :], start=True, stop=True)
                        last = nc.tensor.matmul(s_ps[:, n, S:W], ctx_t[rows, j, P:S], q_t[rows, j, P:S],
                                                start=True, stop=True)
                    last.then_inc(scores_ready, 1)
                if before:
                    pe.wait_ge(c_ready, b + 1)
                    pe.wait_ge(out_read, b)
                    for n in range(MH):
                        nc.tensor.matmul(o_ps[:, n, :], c[:, 1 - j, n, 0:P], v_one[:, 1 - j, 0, n, :], start=True, stop=True)
                        nc.tensor.matmul(o_ps[:, MH + n, :], c[:, 1 - j, n, P:S], v_one[:, 1 - j, 0, n, :], start=True, stop=False)
                        last = nc.tensor.matmul(o_ps[:, MH + n, :], c[:, 1 - j, n, S:W], v_one[:, 1 - j, 1, n, :],
                                                start=False, stop=True)
                    last.then_inc(out_ready, 1)

            turns(pe, turn)

        @block.scalar
        def _(act):
            with act.Fori(0, B // 2) as i:
                for j in range(2):
                    b = i * 2 + j
                    act.wait_ge(g_read, b + 2)
                    nc.scalar.activation(d_exp[:, j].rearrange("p h w -> p (h w)"),
                                         d_arg[:, j].rearrange("p h w -> p (h w)"), ACT.Exp).then_inc(d_ready, 1)



E = 8


AHEAD = 4


class Mixture:

    def __init__(self, name, k, h, gated, bias):
        self.name, self.k, self.h, self.gated, self.bias = name, k, h, gated, bias
        self.wide = 2 * h if gated else h
        tiles = k * NT + E - 1
        self.tiles = -(-tiles // AHEAD) * AHEAD
        self.second_bias = name == "f0"
        self.top_probability = name == "f1"


MIX0 = Mixture("f0", 1, 512, False, True)
MIX1 = Mixture("f1", 1, 512, True, False)
MIX3 = Mixture("f3", 2, 256, True, True)
MOST_SLOTS = MIX3.tiles * P


def mixture_route(nc, a, x, ident, mix, hold, slots_x):
    from contextlib import ExitStack
    K = mix.k
    with ExitStack() as stack:
        mem = Memory(nc, stack, mix.name + "r")
        nb = NormBuffers(mem)
        xn = mem.sbuf("xn", [P, NT, D])
        xn_now = mem.sbuf("xn_now", [P, 2, TB, D])
        xn_t = mem.sbuf("xn_t", [P, 2, S])
        router = mem.sbuf("router", [P, E])
        router_b = mem.sbuf("router_b", [P, 2, E])
        before = mem.sbuf("before", [P, P])
        ones = mem.sbuf("ones", [P, P])
        iota_e = mem.sbuf("iota_e", [P, E])
        iota_s = mem.sbuf("iota_s", [P, mix.tiles])
        keep = mem.sbuf("keep", [P, E, NT])
        tile_starts = mem.sbuf("tile_starts", [P, NT])
        logits = mem.sbuf("logits", [P, NT, E])
        top = mem.sbuf("top", [P, NT, E])
        top_at = mem.sbuf("top_at", [P, NT, E], U32)
        at = mem.sbuf("at", [P, K, NT])
        chosen = mem.sbuf("chosen", [P, K, NT, E])
        both = mem.sbuf("both", [P, NT, E])
        count = mem.sbuf("count", [P, E, NT])
        cum = mem.sbuf("cum", [P, E, NT])
        over = mem.sbuf("over", [P, E, NT])
        n_tiles = mem.sbuf("n_tiles", [P, E])
        ends = mem.sbuf("ends", [P, E])
        base = mem.sbuf("base", [P, E])
        offset = mem.sbuf("offset", [P, E, NT])
        place = mem.sbuf("place", [P, NT, E])
        picked = mem.sbuf("picked", [P, K, NT, E])
        slot = mem.sbuf("slot", [P, K, NT])
        past = mem.sbuf("past", [P, mix.tiles, E])
        expert = mem.sbuf("expert", [P, mix.tiles])
        gap = mem.sbuf("gap", [P, NT, E])
        exp_gap = mem.sbuf("exp_gap", [P, NT, E])
        total = mem.sbuf("total", [P, NT])
        t_ps = mem.psum("t_ps", [P, 2, 512])
        l_ps = mem.psum("l_ps", [P, 2, 512])
        c_ps = mem.psum("c_ps", [P, 2, 512])

        const_in = mem.sem("const_in")
        transposed = mem.sem("transposed")
        xn_t_ready = mem.sem("xn_t_ready")
        logits_done = mem.sem("logits_done")
        logits_ready = mem.sem("logits_ready")
        steps_done = mem.sem("steps_done")
        bias_steps = mem.sem("bias_steps")
        route_steps = mem.sem("route_steps")
        both_ready = mem.sem("both_ready")
        counted = mem.sem("counted")
        slots_ready = mem.sem("slots_ready")
        gap_ready = mem.sem("gap_ready")
        exp_ready = mem.sem("exp_ready")
        block = stack.enter_context(nc.Block())

        @block.sync
        def _(sync):
            for t, n in ((router, mix.name + "_router"), (router_b, mix.name + "_router_b"), (before, "before"),
                         (iota_e, "iota_e"), (iota_s, mix.name + "_iota_s"), (keep, "keep"), (tile_starts, "tile_starts")):
                sync.dma_start(t[:], a[n]).then_inc(const_in, 16)

        @block.gpsimd
        def _(pool):
            norm_power_set(nc, pool, nb)
            with pool.Fori(0, B) as b:
                norm_gpsimd(nc, pool, nb, b)
            pool.wait_ge(slots_ready, 1)
            pool.wait_ge(Memory.zeroed, 16)
            for k in range(K):
                for t in range(NT):
                    nc.gpsimd.indirect_dma_start(
                        out=slots_x[:, :], out_offset=bass.IndirectOffsetOnAxis(ap=hold.slot[:, k, t:t + 1], axis=0),
                        in_=xn[:, t, :], in_offset=None).then_inc(Memory.scattered, 16)
            pool.wait_ge(Memory.scattered, (Memory.rounds + K) * NT * 16)

        @block.tensor
        def _(pe):
            pe.wait_ge(const_in, 7 * 16)
            pe.sem_inc(transposed, 2)
            pe.sem_inc(logits_done, 2)

            def turn_x(b, j):
                pe.wait_ge(nb.ready, b + 1)
                pe.wait_ge(xn_t_ready, b + 1)
                for t in range(TB):
                    last = nc.tensor.transpose(t_ps[:, j, t * P:(t + 1) * P], xn_now[:, j, t, :], ident[:])
                last.then_inc(transposed, 1)

            def logits_of(b, j):
                pe.wait_ge(logits_ready, b + 1)
                pe.wait_ge(xn_t_ready, b + 3)
                for t in range(TB):
                    last = nc.tensor.matmul(l_ps[:, j, t * E:(t + 1) * E], xn_t[:, j, t * P:(t + 1) * P], router[:],
                                            start=True, stop=True)
                last.then_inc(logits_done, 1)

            with pe.Fori(0, B // 2) as i:
                for j in range(2):
                    turn_x(i * 2 + j, j)
                    logits_of(i * 2 + j, j)
            pe.wait_ge(both_ready, 1)
            nc.tensor.matmul(c_ps[:, 0, 0:NT * E], before[:], both[:].rearrange("p t e -> p (t e)"), start=True, stop=True)
            nc.tensor.matmul(c_ps[:, 1, 0:NT * E], ones[:], both[:].rearrange("p t e -> p (t e)"),
                             start=True, stop=True).then_inc(counted, 1)

        @block.scalar
        def _(act):
            act.sem_inc(xn_t_ready, 2)
            with act.Fori(0, B // 2) as i:
                for j in range(2):
                    b = i * 2 + j
                    act.wait_ge(transposed, b + 3)
                    act.wait_ge(logits_done, b + 1)
                    nc.scalar.activation(xn_t[:, j, :], t_ps[:, j, 0:S], ACT.Copy).then_inc(xn_t_ready, 1)
            if K == 2 or mix.top_probability:
                act.wait_ge(gap_ready, 1)
                nc.scalar.activation(exp_gap[:], gap[:], ACT.Exp).then_inc(exp_ready, 1)

        @block.vector
        def _(dve):
            nc.vector.memset(ones[:], 1.0).then_inc(route_steps, 1)
            dve.wait_ge(const_in, 7 * 16)
            dve.sem_inc(logits_ready, 2)

            def logits_of(b, j):
                dve.wait_ge(logits_done, b + 3)
                add = nc.vector.tensor_tensor(logits[:, bass.ds(b * TB, TB), :],
                                              l_ps[:, j, 0:TB * E].rearrange("p (t e) -> p t e", e=E),
                                              router_b[:, 0:1, :].to_broadcast([P, TB, E]), ALU.add)
                if mix.second_bias:
                    second = Steps(dve, bias_steps, b, 1)
                    second.link(add)
                    add = nc.vector.tensor_tensor(logits[:, bass.ds(b * TB, TB), :], logits[:, bass.ds(b * TB, TB), :],
                                                  router_b[:, 1:2, :].to_broadcast([P, TB, E]), ALU.add)
                add.then_inc(logits_ready, 1)

            def turn(b, j, before):
                steps = Steps(dve, steps_done, b, NORM_STEPS + 1)
                dve.wait_ge(transposed, b + 1)
                norm_vector(nc, dve, steps, nb, x, b, xn_now[:, j])
                steps.step(nc.vector.tensor_copy(xn[:, bass.ds(b * TB, TB), :], xn_now[:, j]))
                steps.close()
                if before:
                    logits_of(b - 1, 1 - j)

            turn(0, 0, False)
            turn(1, 1, True)
            with dve.Fori(1, B // 2) as i:
                for j in range(2):
                    turn(i * 2 + j, j, True)
            logits_of(B - 1, 1)
            dve.wait_ge(logits_ready, B + 2)
            r = Steps(dve, route_steps)
            r.n = 1
            for t in range(NT):
                r.step(nc.vector.max(top[:, t, :], logits[:, t, :]))
            r.settle()
            for t in range(NT):
                r.step(nc.vector.max_index(top_at[:, t, :], top[:, t, :], logits[:, t, :]))
            r.settle()
            wide = [P, NT, E]
            for k in range(K):
                r.link(nc.vector.tensor_copy(at[:, k, :], top_at[:, :, k]))
                r.link(nc.vector.tensor_tensor(chosen[:, k], iota_e[:].unsqueeze(1).to_broadcast(wide),
                                               at[:, k, :].unsqueeze(2).to_broadcast(wide), ALU.is_equal))
            if K == 2:
                nc.vector.tensor_tensor(both[:], chosen[:, 0], chosen[:, 1], ALU.add).then_inc(both_ready, 1)
            else:
                nc.vector.tensor_copy(both[:], chosen[:, 0]).then_inc(both_ready, 1)
            if mix.top_probability:
                nc.vector.tensor_tensor(gap[:], logits[:], top[:, :, 0:1].to_broadcast(wide),
                                        ALU.subtract).then_inc(gap_ready, 1)
                dve.wait_ge(exp_ready, 1)
                r.link(nc.vector.tensor_reduce(total[:], exp_gap[:], AX.X, ALU.add))
                r.link(nc.vector.reciprocal(hold.score[:, 0, :], total[:]))
            if K == 2:
                nc.vector.tensor_tensor(gap[:], top[:], top[:, :, 0:1].to_broadcast(wide),
                                        ALU.subtract).then_inc(gap_ready, 1)
                dve.wait_ge(exp_ready, 1)
                r.link(nc.vector.tensor_tensor(total[:], exp_gap[:, :, 0], exp_gap[:, :, 1], ALU.add))
                r.link(nc.vector.reciprocal(total[:], total[:]))
                for k in range(K):
                    r.link(nc.vector.tensor_tensor(hold.score[:, k, :], exp_gap[:, :, k], total[:], ALU.mult))
            dve.wait_ge(counted, 1)
            r.link(nc.vector.tensor_copy(count[:], c_ps[:, 1, 0:NT * E].rearrange("p (t e) -> p e t", e=E)))
            r.link(nc.vector.tensor_tensor_scan(cum[:].rearrange("p e t -> p (e t)"), keep[:].rearrange("p e t -> p (e t)"),
                                                count[:].rearrange("p e t -> p (e t)"), 0.0, ALU.mult, ALU.add))
            by_e = [P, E, NT]
            r.link(nc.vector.tensor_tensor(over[:], cum[:, :, NT - 1:NT].to_broadcast(by_e),
                                           tile_starts[:].unsqueeze(1).to_broadcast(by_e), ALU.is_gt))
            r.link(nc.vector.tensor_reduce(n_tiles[:], over[:], AX.X, ALU.add))
            r.link(nc.vector.tensor_tensor_scan(ends[:], ones[:, 0:E], n_tiles[:], 0.0, ALU.mult, ALU.add))
            r.link(nc.vector.tensor_tensor(base[:], ends[:], n_tiles[:], ALU.subtract))
            r.link(nc.vector.tensor_tensor(offset[:], cum[:], count[:], ALU.subtract))
            r.link(nc.vector.scalar_tensor_tensor(out=offset[:], in0=base[:].unsqueeze(2).to_broadcast(by_e), scalar=float(P),
                                                  in1=offset[:], op0=ALU.mult, op1=ALU.add))
            r.link(nc.vector.tensor_tensor(place[:], c_ps[:, 0, 0:NT * E].rearrange("p (t e) -> p t e", e=E),
                                           offset[:].rearrange("p e t -> p t e"), ALU.add))
            for k in range(K):
                r.link(nc.vector.tensor_tensor(picked[:, k], chosen[:, k], place[:], ALU.mult))
                r.link(nc.vector.tensor_reduce(slot[:, k, :], picked[:, k], AX.X, ALU.add))
            nc.vector.tensor_copy(hold.slot[:], slot[:]).then_inc(slots_ready, 1)
            by_s = [P, mix.tiles, E]
            r.link(nc.vector.tensor_tensor(past[:], iota_s[:].unsqueeze(2).to_broadcast(by_s),
                                           ends[:].unsqueeze(1).to_broadcast(by_s), ALU.is_ge))
            r.link(nc.vector.tensor_reduce(expert[:], past[:], AX.X, ALU.add))
            r.link(nc.vector.tensor_scalar(out=hold.expert[:], in0=expert[:], scalar1=float(E - 1), scalar2=None, op0=ALU.min))


def mixture_experts(nc, a, ident, mix, hold, slots_x, slots_y):
    from contextlib import ExitStack
    H, W, NS, HC = mix.h, mix.wide, mix.tiles, mix.h // P
    with ExitStack() as stack:
        mem = Memory(nc, stack, mix.name + "e")
        xs = mem.sbuf("xs", [P, AHEAD, D])
        xs_t = mem.sbuf("xs_t", [P, 2, P])
        wide = mem.sbuf("wide", [P, 2, W])
        gate = mem.sbuf("gate", [P, 2, H])
        hidden = mem.sbuf("hidden", [P, 2, H])
        hidden_t = mem.sbuf("hidden_t", [P, 2, HC, P])
        ys = mem.sbuf("ys", [P, 2, D])
        xt_ps = mem.psum("xt_ps", [P, 512])
        h_ps = mem.psum("h_ps", [P, 2, max(W, 512)])
        ht_ps = mem.psum("ht_ps", [P, 512])
        y_ps = mem.psum("y_ps", [P, 512])

        row_in = [mem.sem(f"row_in_{j}") for j in range(AHEAD)]
        row_out = [mem.sem(f"row_out_{j}") for j in range(2)]
        xt_done = mem.sem("xt_done")
        xt_ready = mem.sem("xt_ready")
        h_done = mem.sem("h_done")
        wide_ready = mem.sem("wide_ready")
        gate_ready = mem.sem("gate_ready")
        hidden_ready = mem.sem("hidden_ready")
        ht_done = mem.sem("ht_done")
        ht_ready = mem.sem("ht_ready")
        y_done = mem.sem("y_done")
        y_ready = mem.sem("y_ready")
        block = stack.enter_context(nc.Block())

        def half(t, j):
            return t // 2 if isinstance(t, int) else (t - j) // 2

        def turns(engine, turn, lag, step=2):
            for t in range(step):
                turn(t, t % step, "ends")
            with engine.Fori(1, NS // step - 1) as i:
                for j in range(step):
                    turn(i * step + j, j, "middle")
            for t in range(NS - step, NS + lag):
                turn(t, t % step, "ends")

        def of(t, lag, where):
            return where == "middle" or 0 <= t - lag < NS

        @block.sync
        def _(sync):
            def load(s, b):
                if not isinstance(s, int) or s >= AHEAD:
                    sync.wait_ge(xt_done, s - AHEAD + 3)
                sync.dma_start(xs[:, b, :], slots_x[bass.ds(s * P, P), :]).then_inc(row_in[b], 16)

            def turn(t, j, where):
                if of(t, 1 - AHEAD, where):
                    load(t + AHEAD - 1, (j + AHEAD - 1) % AHEAD)
                if of(t, 3, where) and (not isinstance(t, int) or t >= 3):
                    s, b = t - 3, (j + 1) % 2
                    sync.wait_ge(y_ready, s + 2)
                    sync.dma_start(slots_y[bass.ds(s * P, P), :], ys[:, b, :]).then_inc(row_out[b], 16)

            for j in range(2):
                sync.sem_inc(row_out[j], 16)
            for s in range(AHEAD - 1):
                load(s, s)
            turns(sync, turn, 3, AHEAD)
            for j in range(2):
                sync.wait_ge(row_out[j], NS // 2 * 16 + 16)

        @block.tensor
        def _(pe):
            pe.wait_ge(hold.loaded, len(hold.loads) * 16)
            pe.sem_inc(xt_done, 2)
            pe.sem_inc(h_done, 2)
            pe.sem_inc(y_done, 2)

            def turn_rows(s, b):
                generation = s // AHEAD if isinstance(s, int) else (s - b) // AHEAD
                pe.wait_ge(row_in[b], generation * 16 + 16)
                pe.wait_ge(xt_ready, s + 1)
                nc.tensor.transpose(xt_ps[:, 0:P], xs[:, b, :], ident[:]).then_inc(xt_done, 1)

            def turn(t, b, where):
                j = b % 2
                if of(t, 0, where):
                    e = pe.value_load(hold.expert[0:1, bass.ds(t, 1)], min_val=0, max_val=E - 1)
                    pe.wait_ge(xt_ready, t + 2)
                    pe.wait_ge(hidden_ready, t + 1)
                    for c in range(0, W, 512):
                        last = nc.tensor.matmul(h_ps[:, j, c:c + 512], xs_t[:, j, :], hold.w1[:, bass.ds(e * W + c, 512)],
                                                start=True, stop=True)
                    last.then_inc(h_done, 1)
                if of(t, -1, where):
                    turn_rows(t + 1, (b + 1) % AHEAD)
                if of(t, 1, where):
                    pe.wait_ge(hidden_ready, t + 2)
                    pe.wait_ge(ht_ready, t)
                    for c in range(HC):
                        last = nc.tensor.transpose(ht_ps[:, c * P:(c + 1) * P], hidden[:, 1 - j, c * P:(c + 1) * P], ident[:])
                    last.then_inc(ht_done, 1)
                if of(t, 2, where):
                    e = pe.value_load(hold.expert[0:1, bass.ds(t - 2, 1)], min_val=0, max_val=E - 1)
                    pe.wait_ge(ht_ready, t)
                    pe.wait_ge(y_ready, t - 1)
                    for c in range(HC):
                        last = nc.tensor.matmul(y_ps[:, 0:D], hidden_t[:, j, c, :], hold.w2[:, bass.ds(e * (HC * D) + c * D, D)],
                                                start=c == 0, stop=c == HC - 1)
                    last.then_inc(y_done, 1)

            turn_rows(0, 0)
            turns(pe, turn, 2, AHEAD)

        @block.scalar
        def _(act):
            act.sem_inc(xt_ready, 1)
            act.sem_inc(ht_ready, 1)

            def keep_turned(s, j):
                act.wait_ge(xt_done, s + 3)
                act.wait_ge(h_done, s + 1)
                nc.scalar.activation(xs_t[:, j, :], xt_ps[:, 0:P], ACT.Copy).then_inc(xt_ready, 1)

            def turn(t, j, where):
                if of(t, -1, where):
                    keep_turned(t + 1, 1 - j)
                if of(t, 1, where):
                    act.wait_ge(ht_done, t)
                    act.wait_ge(y_done, t)
                    nc.scalar.activation(hidden_t[:, 1 - j].rearrange("p c t -> p (c t)"), ht_ps[:, 0:H],
                                         ACT.Copy if mix.gated else ACT.Relu).then_inc(ht_ready, 1)
                if of(t, 0, where) and mix.gated:
                    if mix.bias:
                        act.wait_ge(wide_ready, t + 1)
                    else:
                        act.wait_ge(h_done, t + 3)
                    act.wait_ge(hidden_ready, t + 1)
                    nc.scalar.activation(gate[:, j, :], (wide if mix.bias else h_ps)[:, j, 0:H], ACT.Silu).then_inc(gate_ready, 1)

            keep_turned(0, 0)
            turns(act, turn, 1)

        @block.vector
        def _(dve):
            dve.wait_ge(hold.loaded, len(hold.loads) * 16)
            dve.sem_inc(hidden_ready, 2)
            dve.sem_inc(y_ready, 1)

            def turn(t, j, where):
                if of(t, 0, where):
                    if mix.bias:
                        e = dve.value_load(hold.expert[0:1, bass.ds(t, 1)], min_val=0, max_val=E - 1)
                    dve.wait_ge(h_done, t + 3)
                    if not isinstance(t, int) or t >= 2:
                        dve.wait_ge(ht_done, t - 1)
                    if not mix.gated:
                        nc.vector.tensor_tensor(hidden[:, j, :], h_ps[:, j, 0:W], hold.b1[:, bass.ds(e * W, W)],
                                                ALU.add).then_inc(hidden_ready, 1)
                    elif mix.bias:
                        nc.vector.tensor_tensor(wide[:, j, :], h_ps[:, j, 0:W], hold.b1[:, bass.ds(e * W, W)],
                                                ALU.add).then_inc(wide_ready, 1)
                if of(t, 2, where):
                    if mix.bias:
                        e = dve.value_load(hold.expert[0:1, bass.ds(t - 2, 1)], min_val=0, max_val=E - 1)
                    dve.wait_ge(y_done, t + 1)
                    dve.wait_ge(row_out[j], half(t, j) * 16)
                    if mix.bias:
                        nc.vector.tensor_tensor(ys[:, j, :], y_ps[:, 0:D], hold.b2[:, bass.ds(e * D, D)], ALU.add).then_inc(y_ready, 1)
                    else:
                        nc.vector.tensor_copy(ys[:, j, :], y_ps[:, 0:D]).then_inc(y_ready, 1)
                if of(t, 0, where) and mix.gated:
                    dve.wait_ge(gate_ready, t + 1)
                    nc.vector.tensor_tensor(hidden[:, j, :], gate[:, j, :], (wide if mix.bias else h_ps)[:, j, H:W],
                                            ALU.mult).then_inc(hidden_ready, 1)

            turns(dve, turn, 2)


def mixture_gather(nc, x, mix, hold, slots_y):
    from contextlib import ExitStack
    with ExitStack() as stack:
        mem = Memory(nc, stack, mix.name + "g")
        back = mem.sbuf("back", [P, mix.k, NT, D])
        steps_done = mem.sem("steps_done")
        block = stack.enter_context(nc.Block())

        @block.gpsimd
        def _(pool):
            for t in range(NT):
                for k in range(mix.k):
                    nc.gpsimd.indirect_dma_start(
                        out=back[:, k, t, :], out_offset=None, in_=slots_y[0:mix.tiles * P, :],
                        in_offset=bass.IndirectOffsetOnAxis(ap=hold.slot[:, k, t:t + 1], axis=0)).then_inc(Memory.gathered[t], 16)

        @block.vector
        def _(dve):
            steps = Steps(dve, steps_done)
            for t in range(NT):
                dve.wait_ge(Memory.gathered[t], (Memory.rounds + mix.k) * 16)
                for k in range(mix.k):
                    if k:
                        steps.settle()
                    if mix.name == "f0":
                        steps.step(nc.vector.tensor_tensor(x[:, t, :], x[:, t, :], back[:, k, t, :], ALU.add))
                    else:
                        steps.step(nc.vector.scalar_tensor_tensor(out=x[:, t, :], in0=back[:, k, t, :], scalar=hold.score[:, k, t:t + 1],
                                                                  in1=x[:, t, :], op0=ALU.mult, op1=ALU.add))
            steps.settle()


def mixture_weights(nc, a, mix, stack):
    hold = Memory(nc, stack, mix.name)
    hold.w1 = hold.sbuf("w1", [P, E * mix.wide])
    hold.w2 = hold.sbuf("w2", [P, E * mix.h])
    hold.loaded = Memory.loaded[mix.name]
    hold.loads = [(hold.w1[:], a[mix.name + "_w1"]), (hold.w2[:], a[mix.name + "_w2"])]
    if mix.bias:
        hold.b1 = hold.sbuf("b1", [P, E * mix.wide])
        hold.b2 = hold.sbuf("b2", [P, E * D])
        hold.loads += [(hold.b1[:], a[mix.name + "_b1"].to_broadcast([P, E * mix.wide])),
                       (hold.b2[:], a[mix.name + "_b2"].to_broadcast([P, E * D]))]

    def start(engine):
        for t, n in hold.loads:
            engine.dma_start(t, n).then_inc(hold.loaded, 16)

    hold.start_loads = start
    return hold


def mixture_layer(nc, a, x, ident, mix, hold, slots_x, slots_y):
    from contextlib import ExitStack
    with ExitStack() as stack:
        mem = Memory(nc, stack, mix.name + "h")
        hold.slot = mem.sbuf("slot", [P, mix.k, NT], U32)
        hold.score = mem.sbuf("score", [P, mix.k, NT])
        hold.expert = mem.sbuf("expert", [P, mix.tiles], I32)
        mixture_route(nc, a, x, ident, mix, hold, slots_x)
        mixture_experts(nc, a, ident, mix, hold, slots_x, slots_y)
        mixture_gather(nc, x, mix, hold, slots_y)
    Memory.rounds += mix.k



HN = 16
HD = D // HN
SLOT = 32
HG = 4
G = HN // HG
MAX_ROW = 3 * HD
MASKED = -2.0 ** 100
UNITS = HN
LAG = 4
STEPS = UNITS + LAG
JOBS = {"x": 3, "turn sums": 4, "turn normalised": 6, "project": [6, 10, 12, 14], "output": 8, "values": 16,
        "sums": [9, 13, 17]}


class Heads:
    def __init__(self, name, scale, masked, biased):
        self.name, self.scale, self.masked, self.biased = name, scale, masked, biased


HEADS1 = Heads("h1", HD ** -0.5, True, False)
HEADS2 = Heads("h2", 1.0, False, True)


def heads_layer(nc, a, x, ident, hw, later_loads=None):
    from contextlib import ExitStack
    with ExitStack() as stack:
        mem = Memory(nc, stack, hw.name)
        nb = NormBuffers(mem)
        w_qk = mem.sbuf("w_qk", [P, 2, G, P])
        w_v = mem.sbuf("w_v", [P, D])
        w_o = mem.sbuf("w_o", [P, D])
        b_v = mem.sbuf("b_v", [P, D])
        b_o = mem.sbuf("b_o", [P, D])
        b_qk = mem.sbuf("b_qk", [P, 2, G])
        b_low = mem.sbuf("b_low", [P, 2, G])
        low = mem.sbuf("low", [P, 2])
        ctx_t = mem.sbuf("ctx_t", [P, 2, S])
        xn = mem.sbuf("xn", [P, 2, TB, D])
        xn_t = mem.sbuf("xn_t", [P, 2, S])
        high = mem.sbuf("high", [P, 2, 2, S], F32R)
        qk = mem.sbuf("qk", [P, 2, 2, G, S], F32R)
        q_less = mem.sbuf("q_less", [P, G, S], F32R)
        k_kept = mem.sbuf("k_kept", [P, 2, G, S], F32R)
        v = mem.sbuf("v", [P, 2, TB, HN, SLOT])
        neg_max = mem.sbuf("neg_max", [P, TB, G, HG])
        max_high = mem.sbuf("max_high", [P, TB, G, HG], F32R)
        max_rows = mem.sbuf("max_rows", [P, TB, G, HG, SLOT])
        p_t = mem.sbuf("p_t", [P, 8, 2, S])
        o_t = mem.sbuf("o_t", [P, G, S])
        recip = mem.sbuf("recip", [P, TB, HN, 1])
        o_n = mem.sbuf("o_n", [P, TB, D])
        on_t = mem.sbuf("on_t", [P, S])
        if hw.masked:
            mask_in = mem.sbuf("mask_in", [P, 2, TB, S], I32)
            mask = mem.sbuf("mask", [P, 2, TB, S], BF16)
            ident_b = mem.sbuf("ident_b", [P, P], BF16)
        work = [mem.psum(f"work{i}", [P, 512]) for i in range(2)]
        side = [mem.psum(f"side{i}", [P, 512]) for i in range(2)]
        sn_ps = [mem.psum(f"sn_ps{i}", [P, 2, S]) for i in range(2)]
        st_ps = [mem.psum(f"st_ps{i}", [P, 2, S]) for i in range(2)]

        const_in = mem.sem("const_in")
        const_set = mem.sem("const_set")
        ctx_in = [mem.sem(f"ctx_in_{j}") for j in range(2)]
        xt_done = mem.sem("xt_done")
        xt_ready = mem.sem("xt_ready")
        proj_done = mem.sem("proj_done")
        high_ready = mem.sem("high_ready")
        split_ready = mem.sem("split_ready")
        v_done = mem.sem("v_done")
        v_ready = mem.sem("v_ready")
        sn_done = mem.sem("sn_done")
        sn_read = mem.sem("sn_read")
        max_steps = mem.sem("max_steps")
        mt_done = mem.sem("mt_done")
        q_max_ready = mem.sem("q_max_ready")
        kept_ready = mem.sem("kept_ready")
        st_done = mem.sem("st_done")
        p_ready = mem.sem("p_ready")
        pv_done = mem.sem("pv_done")
        ot_ready = mem.sem("ot_ready")
        on_done = mem.sem("on_done")
        on_ready = mem.sem("on_ready")
        ont_done = mem.sem("ont_done")
        ont_ready = mem.sem("ont_ready")
        out_done = mem.sem("out_done")
        x_ready = mem.sem("x_ready")
        norm_steps = mem.sem("norm_steps")
        out_steps = mem.sem("out_steps")
        block = stack.enter_context(nc.Block())
        consts = [(w_qk, "w_qk"), (w_v, "w_v"), (w_o, "w_o"), (b_v, "b_v"), (b_o, "b_o"), (b_qk, "b_qk"),
                  (b_low, "b_low"), (low, "low")]
        if hw.masked:
            consts.append((mask_in, "mask"))

        def need(engine, sem, value):
            if not isinstance(value, int) or value > 0:
                engine.wait_ge(sem, value)

        def turns(engine, turn):
            def straight(t):
                turn(t, t % 2, t + 1 < B, 0 <= t < B, 1 <= t <= B, t >= 2)

            for t in range(-1, 2):
                straight(t)
            with engine.Fori(1, B // 2 - 1) as i:
                for j in range(2):
                    turn(i * 2 + j, j, True, True, True, True)
            for t in range(B - 2, B + 2):
                straight(t)

        def unit_of(n):
            return n // 8, n // 4 % 2, n % 4

        @block.sync
        def _(sync):
            for t, n in consts:
                sync.dma_start(t[:], a[hw.name + "_" + n]).then_inc(const_in, 16)

            def load(c, j):
                need(sync, v_done, c - 1)
                sync.dma_start(ctx_t[:, j, :], a["ctx_t"][:, bass.ds(c, 1), :]).then_inc(ctx_in[j], 16)

            load(0, 0)
            load(1, 1)
            with sync.Fori(1, B // 2) as i:
                for j in range(2):
                    load(i * 2 + j, j)

        @block.gpsimd
        def _(pool):
            norm_power_set(nc, pool, nb)

            def turn(t, j, ahead, now, before, last):
                if ahead:
                    norm_gpsimd(nc, pool, nb, t + 1)
                if now:
                    pool.wait_ge(split_ready, t * 4 + 4)
                    need(pool, st_done, (t - 1) * UNITS)
                    apart(pool)
                    nc.gpsimd.tensor_copy(k_kept[:, j], qk[:, j, 1]).then_inc(kept_ready, 1)

            turns(pool, turn)

        @block.tensor
        def _(pe):
            pe.wait_ge(const_in, len(consts) * 16)
            pe.wait_ge(const_set, 4)

            def scores(out, left, right, tile, n, side_of_mask):
                gp, _, hh = unit_of(n)
                rows = slice(hh * SLOT, (hh + 1) * SLOT)
                for g in range(2):
                    last = nc.tensor.matmul(out[:, g, :], left[rows, gp * 2 + g, tile * P:(tile + 1) * P],
                                            right[rows, gp * 2 + g, :], start=g == 0 or not hw.masked,
                                            stop=not hw.masked, skip_group_check=hw.masked)
                if hw.masked:
                    last = nc.tensor.matmul(out[:], ident_b[:], mask[:, side_of_mask, tile:tile + 1, :].to_broadcast([P, 2, S]),
                                            start=False, stop=True, skip_group_check=True)
                return last

            def sums(c, j, u):
                gp, kt, _ = unit_of(u * 4)
                pe.wait_ge(p_ready, c * UNITS + u * 4 + 4)
                for g in range(2):
                    for hh in range(HG):
                        last = nc.tensor.matmul(work[gp][hh * SLOT:(hh + 1) * SLOT, g * S:(g + 1) * S],
                                                v[:, j, kt, (gp * 2 + g) * HG + hh, :], p_t[:, u % 2 * 4 + hh, g, :],
                                                start=kt == 0 and g == 0, stop=kt == 1, skip_group_check=True)
                last.then_inc(pv_done, 1)

            def turn(t, j, ahead, now, before, last_):
                def spread_maxima():
                    pe.wait_ge(max_steps, t * 4)
                    pe.wait_ge(v_ready, t)
                    if now:
                        pe.wait_ge(split_ready, t * 4 + 4)
                    else:
                        pe.wait_ge(x_ready, t - 2)
                    for gp in range(2):
                        for g in range(2):
                            for qt in range(TB):
                                last = nc.tensor.transpose(side[gp][:, g * S + qt * P:g * S + (qt + 1) * P],
                                                           max_rows[:, qt, gp * 2 + g].rearrange("p h s -> p (h s)"), ident[:])
                        last.then_inc(mt_done, 1)

                def transpose_x():
                    pe.wait_ge(nb.ready, t + 2)
                    if before:
                        pe.wait_ge(q_max_ready, (t - 1) * 2 + 1)
                    elif now:
                        pe.wait_ge(split_ready, 4)
                    for n in range(TB):
                        last = nc.tensor.transpose(side[0][:, n * P:(n + 1) * P], xn[:, 1 - j, n, :], ident[:])
                    last.then_inc(xt_done, 1)

                def project(n):
                    if n == 0:
                        pe.wait_ge(xt_ready, t + 2)
                        pe.wait_ge(ctx_in[1 - j], ((t + 1) // 2 if isinstance(t, int) else (t - j) // 2 + j) * 16 + 16)
                    if n == 1 and last_:
                        pe.wait_ge(x_ready, t - 1)
                    elif n == 1 and before:
                        pe.wait_ge(q_max_ready, t * 2)
                    if n >= 2:
                        pe.wait_ge(split_ready, (t + 1) * 4 + n - 1)
                    for g in range(2):
                        last = nc.tensor.matmul(side[n % 2][:, g * S:(g + 1) * S], w_qk[:, n // 2, n % 2 * 2 + g, :],
                                                xn_t[:, 1 - j, :] if n < 2 else ctx_t[:, 1 - j, :], start=True, stop=True)
                    last.then_inc(proj_done, 1)

                def values():
                    if ahead:
                        pe.wait_ge(split_ready, (t + 1) * 4 + 3)
                    elif before:
                        pe.wait_ge(q_max_ready, t * 2)
                    for n in range(TB):
                        last = nc.tensor.matmul(side[0][:, n * D:(n + 1) * D], ctx_t[:, j, n * P:(n + 1) * P], w_v[:],
                                                start=True, stop=True)
                    last.then_inc(v_done, 1)

                def turn_sums():
                    pe.wait_ge(ot_ready, (t - 1) * 2)
                    for qt in range(TB):
                        for g in range(G):
                            last = nc.tensor.transpose(work[qt][:, g * P:(g + 1) * P], o_t[:, g, qt * P:(qt + 1) * P], ident[:])
                        last.then_inc(on_done, 1)

                def turn_normalised():
                    pe.wait_ge(on_ready, (t - 1) * 2)
                    if before:
                        pe.wait_ge(q_max_ready, t * 2)
                    else:
                        pe.wait_ge(x_ready, t - 2)
                    for qt in range(TB):
                        last = nc.tensor.transpose(side[1][:, qt * P:(qt + 1) * P], o_n[:, qt, :], ident[:])
                    last.then_inc(ont_done, 1)

                def output():
                    pe.wait_ge(ont_ready, t - 1)
                    for qt in range(TB):
                        last = nc.tensor.matmul(side[1][:, qt * D:(qt + 1) * D], on_t[:, qt * P:(qt + 1) * P], w_o[:],
                                                start=True, stop=True)
                    last.then_inc(out_done, 1)

                for k in range(STEPS):
                    if k == 0 and before:
                        spread_maxima()
                    if k == 1 and last_:
                        sums(t - 2, j, 3)
                    if k == JOBS["x"] and ahead:
                        transpose_x()
                    if k == JOBS["turn sums"] and last_:
                        turn_sums()
                    if k == JOBS["turn normalised"] and last_:
                        turn_normalised()
                    if k in JOBS["project"] and ahead:
                        project(JOBS["project"].index(k))
                    if k == JOBS["output"] and last_:
                        output()
                    if k == JOBS["values"] and now:
                        values()
                    if k in JOBS["sums"] and before:
                        u = JOBS["sums"].index(k)
                        if u == 0:
                            pe.wait_ge(v_ready, t)
                            if last_:
                                pe.wait_ge(on_ready, (t - 1) * 2)
                        sums(t - 1, 1 - j, u)
                    if now and k < UNITS:
                        if k == 0:
                            pe.wait_ge(split_ready, t * 4 + 4)
                        need(pe, sn_read, t * UNITS + k - 1)
                        scores(sn_ps[k % 2], qk[:, j, 0], qk[:, j, 1], unit_of(k)[1], k, 0).then_inc(sn_done, 1)
                    if before and k >= LAG:
                        n = k - LAG
                        if n == 0:
                            pe.wait_ge(q_max_ready, t * 2)
                            pe.wait_ge(kept_ready, t)
                        need(pe, p_ready, (t - 1) * UNITS + n - 1)
                        scores(st_ps[n % 2], k_kept[:, 1 - j], q_less, unit_of(n)[1], n, 1).then_inc(st_done, 1)

            turns(pe, turn)

        @block.scalar
        def _(act):
            act.wait_ge(const_in, len(consts) * 16)
            if later_loads:
                later_loads(act)

            def keep_sums(c, gp):
                act.wait_ge(pv_done, c * 4 + gp * 2 + 2)
                need(act, on_done, c * 2)
                nc.scalar.activation(o_t[:, gp * 2:gp * 2 + 2, :].rearrange("p g s -> p (g s)"), work[gp][:],
                                     ACT.Copy).then_inc(ot_ready, 1)

            def turn(t, j, ahead, now, before, last_):
                def high_parts(n):
                    act.wait_ge(proj_done, (t + 1) * 4 + n + 1)
                    need(act, split_ready, (t + 1) * 4 + n - 1)
                    for g in range(2):
                        last = nc.scalar.activation(
                            high[:, n % 2, g, :], side[n % 2][:, g * S:(g + 1) * S], ACT.Identity,
                            bias=b_low[:, n // 2, n % 2 * 2 + g:n % 2 * 2 + g + 1], scale=low[:, n // 2:n // 2 + 1])
                    last.then_inc(high_ready, 1)

                for k in range(STEPS):
                    if k == 2 and last_:
                        keep_sums(t - 2, 1)
                    if k == JOBS["x"] + 1 and ahead:
                        act.wait_ge(xt_done, t + 2)
                        need(act, proj_done, (t - 1) * 4 + 2)
                        nc.scalar.activation(xn_t[:, 1 - j, :], side[0][:, 0:S], ACT.Copy).then_inc(xt_ready, 1)
                    if k == JOBS["turn normalised"] + 1 and last_:
                        act.wait_ge(ont_done, t - 1)
                        need(act, out_done, t - 2)
                        nc.scalar.activation(on_t[:], side[1][:, 0:S], ACT.Copy).then_inc(ont_ready, 1)
                    if k - 1 in JOBS["project"] and ahead:
                        high_parts(JOBS["project"].index(k - 1))
                    if k == JOBS["sums"][1] + 1 and before:
                        keep_sums(t - 1, 0)
                    if k == JOBS["values"] + 1 and now and not hw.biased:
                        act.wait_ge(v_done, t + 1)
                        need(act, pv_done, (t - 1) * 4)
                        nc.scalar.activation(v[:, j, :, :, 0:HD].rearrange("p t h d -> p (t h) d"),
                                             side[0][:, 0:TB * D].rearrange("p (n d) -> p n d", d=HD),
                                             ACT.Copy).then_inc(v_ready, 1)
                    if before and k >= LAG:
                        n = k - LAG
                        act.wait_ge(st_done, (t - 1) * UNITS + n + 1)
                        need(act, pv_done, (t - 1) * 4 + n // 4 - 1)
                        nc.scalar.activation(p_t[:, n % 8], st_ps[n % 2][:], ACT.Exp, scale=hw.scale).then_inc(p_ready, 1)

            turns(act, turn)

        @block.vector
        def _(dve):
            nc.vector.memset(v[:], 0.0).then_inc(const_set, 1)
            nc.vector.memset(max_rows[:], 0.0).then_inc(const_set, 1)
            dve.wait_ge(const_set, 2)
            nc.vector.memset(v[:, :, :, :, HD:HD + 1].rearrange("p j t h o -> p (j t h) o"), 1.0).then_inc(const_set, 1)
            dve.wait_ge(const_in, len(consts) * 16)
            if hw.masked:
                for n in range(2):
                    nc.vector.tensor_scalar(out=mask[:, n], in0=mask_in[:, n], scalar1=0.0, scalar2=MASKED,
                                            op0=ALU.is_equal, op1=ALU.mult)
                nc.vector.tensor_copy(ident_b[:], ident[:]).then_inc(const_set, 1)
            else:
                dve.sem_inc(const_set, 1)
            dve.wait_ge(const_set, 4)

            def turn(t, j, ahead, now, before, last_):
                def take_maxima():
                    need(dve, st_done, (t - 1) * UNITS)
                    for gp in range(2):
                        dve.wait_ge(mt_done, (t - 1) * 2 + gp + 1)
                        nc.vector.tensor_tensor(
                            q_less[:, gp * 2:gp * 2 + 2, :], qk[:, 1 - j, 0, gp * 2:gp * 2 + 2, :].bitcast(F32),
                            side[gp][:].rearrange("p (g s) -> p g s", g=2), ALU.add).then_inc(q_max_ready, 1)

                def normalise():
                    need(dve, ont_done, t - 2)
                    for qt in range(TB):
                        dve.wait_ge(on_done, (t - 2) * 2 + qt + 1)
                        sums = work[qt][:].rearrange("p (h s) -> p h s", s=SLOT)
                        out.link(nc.vector.reciprocal(recip[:, qt], sums[:, :, HD:HD + 1]))
                        nc.vector.tensor_tensor(o_n[:, qt, :].rearrange("p (h d) -> p h d", d=HD), sums[:, :, 0:HD],
                                                recip[:, qt].to_broadcast([P, HN, HD]), ALU.mult).then_inc(on_ready, 1)

                def split(n):
                    dve.wait_ge(high_ready, (t + 1) * 4 + n + 1)
                    need(dve, sn_done, t * UNITS)
                    need(dve, kept_ready, t)
                    for g in range(2):
                        at = n % 2 * 2 + g
                        last = nc.vector.scalar_tensor_tensor(
                            out=qk[:, 1 - j, n // 2, at, :], in0=side[n % 2][:, g * S:(g + 1) * S],
                            scalar=b_qk[:, n // 2, at:at + 1], in1=high[:, n % 2, g, :].bitcast(F32),
                            op0=ALU.add, op1=ALU.subtract)
                    last.then_inc(split_ready, 1)

                def output():
                    dve.wait_ge(out_done, t - 1)
                    xb = x[:, bass.ds((t - 2) * TB, TB), :]
                    if hw.biased:
                        out.link(nc.vector.tensor_tensor(xb, xb, b_o[:].unsqueeze(1).to_broadcast([P, TB, D]), ALU.add))
                    nc.vector.tensor_tensor(xb, xb, side[1][:, 0:TB * D].rearrange("p (t d) -> p t d", t=TB),
                                            ALU.add).then_inc(x_ready, 1)
                    out.close()

                def maxima_as_rows():
                    dve.wait_ge(sn_read, t * UNITS + UNITS)
                    need(dve, mt_done, t * 2)
                    m = Steps(dve, max_steps, t, 4)
                    m.link(nc.vector.tensor_copy(max_high[:], neg_max[:]))
                    for qt in range(TB):
                        m.step(nc.vector.tensor_copy(max_rows[:, qt, :, :, MAX_ROW], max_high[:, qt].bitcast(F32)))
                    nc.vector.tensor_tensor(max_rows[:, 0, :, :, MAX_ROW + 1], neg_max[:, 0], max_high[:, 0].bitcast(F32), ALU.subtract)
                    m.step(nc.vector.tensor_tensor(max_rows[:, 1, :, :, MAX_ROW + 1], neg_max[:, 1], max_high[:, 1].bitcast(F32), ALU.subtract))
                    m.close()

                out = Steps(dve, out_steps, t - 2, 2 + (1 if hw.biased else 0))
                norm = Steps(dve, norm_steps, t + 1, NORM_STEPS)
                if ahead:
                    norm_moments(nc, dve, norm, nb, x, t + 1)
                if before:
                    take_maxima()
                for k in range(STEPS):
                    if now and k < UNITS:
                        gp, qt, hh = unit_of(k)
                        dve.wait_ge(sn_done, t * UNITS + k + 1)
                        nc.vector.tensor_reduce(neg_max[:, qt, gp * 2:gp * 2 + 2, hh], sn_ps[k % 2][:], AX.X, ALU.max,
                                                negate=True).then_inc(sn_read, 1)
                    if k == 1 and ahead:
                        need(dve, xt_done, t)
                        norm_apply(nc, dve, norm, nb, x, t + 1, xn[:, 1 - j])
                    if k == JOBS["turn sums"] + 1 and last_:
                        normalise()
                    if k - 1 in JOBS["project"] and ahead:
                        split(JOBS["project"].index(k - 1))
                    if k == JOBS["output"] + 1 and last_:
                        output()
                    if k == UNITS - 1 and now:
                        maxima_as_rows()
                    if k == JOBS["values"] + 1 and now and hw.biased:
                        dve.wait_ge(v_done, t + 1)
                        need(dve, pv_done, (t - 1) * 4)
                        for n in range(TB):
                            last = nc.vector.tensor_tensor(v[:, j, n, :, 0:HD],
                                                           side[0][:, n * D:(n + 1) * D].rearrange("p (h d) -> p h d", d=HD),
                                                           b_v[:].rearrange("p (h d) -> p h d", d=HD), ALU.add)
                        last.then_inc(v_ready, 1)

            turns(dve, turn)



PH = 4
PK = 128
HALF = 64
TOP = 8
EX = 16
EXPERT_BLOCKS = EX
MLP_BLOCKS = 4
UP_BLOCKS = EXPERT_BLOCKS + MLP_BLOCKS
DOWN_BLOCKS = UP_BLOCKS + MLP_BLOCKS
PICKS = PH * TOP
Q4 = P // PICKS
BANK_GROUPS = 8
PICK_STEPS = 20


def keyed_layer(nc, a, x, ident):
    from contextlib import ExitStack
    with ExitStack() as stack:
        mem = Memory(nc, stack, "pk")
        nb = NormBuffers(mem)
        w_q = mem.sbuf("w_q", [HALF, 2 * PH, D])
        keys = mem.sbuf("keys", [HALF, 2 * PH, PK])
        folded = mem.sbuf("folded", [P, 2, PH * PK])
        down = mem.sbuf("down", [P, DOWN_BLOCKS, P])
        up = mem.sbuf("up", [P, UP_BLOCKS, D])
        iota = mem.sbuf("iota", [P, PK])
        xn = mem.sbuf("xn", [P, TB, D])
        xn_t = mem.sbuf("xn_t", [P, 2, S])
        sim = mem.sbuf("sim", [P, 2, TB, PH, PK])
        best = mem.sbuf("best", [P, 2, TB * PH, TOP])
        best_at = mem.sbuf("best_at", [P, 2, TB * PH, TOP], U32)
        at = mem.sbuf("at", [P, 2, TB * PH, TOP])
        sums = mem.sbuf("sums", [P, TB * PH, TOP, TOP])
        top = mem.sbuf("top", [P, TB * PH, TOP])
        top_at = mem.sbuf("top_at", [P, TB * PH, TOP], U32)
        rank_at = mem.sbuf("rank_at", [P, 2, TB * PH, TOP], U32)
        rank = mem.sbuf("rank", [P, 2, TB * PH, TOP])
        chosen = mem.sbuf("chosen", [P, 2 * TB * PH, TOP, TOP])
        pick = mem.sbuf("pick", [P, 2, TB * PH, TOP])
        beyond = mem.sbuf("beyond", [P, TB * PH, TOP])
        gap = mem.sbuf("gap", [P, TB * PH, TOP])
        ex = mem.sbuf("ex", [P, TB * PH, TOP])
        total = mem.sbuf("total", [P, TB * PH])
        weight = mem.sbuf("weight", [P, TB * PH, TOP])
        spread = chosen[:].rearrange("p a s i -> p (a s i)").rearrange("p (n r g) -> p n r g", n=TB, r=EX)
        spread_t = mem.sbuf("spread_t", [P, TB, EX, PICKS])
        y_t = mem.sbuf("y_t", [P, TB, PICKS])
        ones_y = mem.sbuf("ones_y", [P, 2, TB, PICKS, PK])
        by_token = mem.sbuf("by_token", [P, 2, TB, PICKS, Q4, EX])
        acts = mem.sbuf("acts", [P, DOWN_BLOCKS, S])
        g = mem.sbuf("g", [P, EXPERT_BLOCKS, S])
        xt_ps = mem.psum("xt_ps", [P, 512])
        sim_ps = mem.psum("sim_ps", [P, 2, 512])
        d_ps = mem.psum("d_ps", [P, 2, 2, S])
        g_ps = mem.psum("g_ps", [P, 2, BANK_GROUPS, Q4, EX])
        y_ps = mem.psum("y_ps", [P, 512])

        const_in = mem.sem("const_in")
        const_set = mem.sem("const_set")
        fold_done = mem.sem("fold_done")
        fold_ready = mem.sem("fold_ready")
        xt_done = mem.sem("xt_done")
        xt_ready = mem.sem("xt_ready")
        sim_done = mem.sem("sim_done")
        sim_ready = mem.sem("sim_ready")
        gap_ready = mem.sem("gap_ready")
        exp_ready = mem.sem("exp_ready")
        spread_ready = mem.sem("spread_ready")
        by_token_ready = mem.sem("by_token_ready")
        y_t_ready = mem.sem("y_t_ready")
        ones_ready = mem.sem("ones_ready")
        ones_1_ready = mem.sem("ones_1_ready")
        d_done = mem.sem("d_done")
        d_ready = mem.sem("d_ready")
        g_done = mem.sem("g_done")
        g_ready = mem.sem("g_ready")
        w_ready = mem.sem("w_ready")
        y_done = mem.sem("y_done")
        x_ready = mem.sem("x_ready")
        norm_steps = mem.sem("norm_steps")
        pick_steps = mem.sem("pick_steps")
        block = stack.enter_context(nc.Block())
        FILLS = DOWN_BLOCKS // 2
        GATE_FILL = EXPERT_BLOCKS // 2
        GF = TB * PICKS // BANK_GROUPS
        CONSTS = 5

        def need(engine, sem, value):
            if not isinstance(value, int) or value > 0:
                engine.wait_ge(sem, value)

        def turns(engine, turn):
            def straight(t):
                turn(t, t % 2, t + 1 < B, 0 <= t < B, 1 <= t <= B, t >= 2)

            for t in range(-1, 2):
                straight(t)
            with engine.Fori(1, B // 2 - 1) as i:
                for j in range(2):
                    turn(i * 2 + j, j, True, True, True, True)
            for t in range(B - 2, B + 2):
                straight(t)

        @block.sync
        def _(sync):
            for t, n in ((w_q, "pk_w_q"), (keys, "pk_keys"), (down, "pk_down"), (up, "pk_up"), (iota, "iota")):
                sync.dma_start(t[:], a[n]).then_inc(const_in, 16)
            sync.wait_ge(const_in, CONSTS * 16)

        @block.gpsimd
        def _(pool):
            norm_power_set(nc, pool, nb)
            pool.wait_ge(const_in, CONSTS * 16)

            def turn(t, j, ahead, now, before, last):
                if ahead:
                    norm_gpsimd(nc, pool, nb, t + 1)
                if now:
                    pool.wait_ge(y_t_ready, t + 1)
                    need(pool, g_done, (t - 1) * GF)
                    apart(pool)
                    for group in range(PICKS):
                        last_one = nc.gpsimd.tensor_scalar(out=ones_y[:, j, 1, group, :], in0=iota[:],
                                                           scalar1=y_t[:, 1, group:group + 1], scalar2=None, op0=ALU.is_equal)
                    last_one.then_inc(ones_1_ready, 1)

            turns(pool, turn)

        @block.tensor
        def _(pe):
            pe.wait_ge(const_in, CONSTS * 16)
            for p in range(2):
                for h in range(PH):
                    last = nc.tensor.matmul(sim_ps[:, p, h * PK:(h + 1) * PK], w_q[:, p * PH + h, :], keys[:, p * PH + h, :],
                                            start=True, stop=True)
            last.then_inc(fold_done, 1)
            pe.wait_ge(fold_ready, 1)
            pe.wait_ge(const_set, 1)

            def turn(t, j, ahead, now, before, last_):
                if last_:
                    pe.wait_ge(w_ready, (t - 1) * 2)
                    need(pe, x_ready, t - 2)
                    for n in range(TB):
                        for c in range(UP_BLOCKS):
                            last = nc.tensor.matmul(y_ps[:, n * D:(n + 1) * D], acts[:, c, n * P:(n + 1) * P], up[:, c, :],
                                                    start=c == 0, stop=c == UP_BLOCKS - 1)
                    last.then_inc(y_done, 1)
                if before:
                    for n in range(FILLS):
                        need(pe, d_ready, (t - 1) * FILLS + n - 1)
                        for c in range(2):
                            last = nc.tensor.matmul(d_ps[:, n % 2, c, :], down[:, n * 2 + c, :], xn_t[:, 1 - j, :],
                                                    start=True, stop=True)
                        last.then_inc(d_done, 1)
                    pe.wait_ge(by_token_ready, t)
                    pe.wait_ge(ones_ready, t)
                    pe.wait_ge(ones_1_ready, t)
                    for f in range(GF):
                        need(pe, g_ready, (t - 1) * GF + f - 1)
                        for u in range(BANK_GROUPS):
                            n, group = f // (GF // TB), f % (GF // TB) * BANK_GROUPS + u
                            last = nc.tensor.matmul(g_ps[:, f % 2, u], ones_y[:, 1 - j, n, group, :],
                                                    by_token[:, 1 - j, n, group], start=True, stop=True)
                        last.then_inc(g_done, 1)
                if ahead:
                    pe.wait_ge(nb.ready, t + 2)
                    need(pe, xt_ready, t + 1)
                    for n in range(TB):
                        last = nc.tensor.transpose(xt_ps[:, n * P:(n + 1) * P], xn[:, n, :], ident[:])
                    last.then_inc(xt_done, 1)
                    pe.wait_ge(xt_ready, t + 2)
                    for n in range(TB):
                        for p in range(2):
                            need(pe, sim_ready, (t + 1) * 4 + n * 2 + p - 1)
                            nc.tensor.matmul(sim_ps[:, p, :], xn_t[:, 1 - j, n * P:(n + 1) * P], folded[:, p, :],
                                             start=True, stop=True).then_inc(sim_done, 1)

            turns(pe, turn)

        @block.scalar
        def _(act):
            act.wait_ge(fold_done, 1)
            nc.scalar.activation(folded[:], sim_ps[:], ACT.Copy).then_inc(fold_ready, 1)

            def turn(t, j, ahead, now, before, last_):
                if before:
                    need(act, y_done, t - 1)
                    for n in range(FILLS):
                        act.wait_ge(d_done, (t - 1) * FILLS + n + 1)
                        nc.scalar.activation(acts[:, n * 2:n * 2 + 2, :], d_ps[:, n % 2],
                                             ACT.Silu if n < UP_BLOCKS // 2 else ACT.Copy).then_inc(d_ready, 1)
                if now:
                    act.wait_ge(gap_ready, t + 1)
                    need(act, spread_ready, t)
                    nc.scalar.activation(ex[:], gap[:], ACT.Exp).then_inc(exp_ready, 1)
                if before:
                    need(act, w_ready, (t - 1) * 2)
                    for f in range(GF):
                        n, k = f // (GF // TB), f % (GF // TB)
                        act.wait_ge(g_done, (t - 1) * GF + f + 1)
                        nc.scalar.activation(
                            g[:, :, n * P:(n + 1) * P].rearrange("p r (q g) -> p g q r", q=Q4)[:, k * BANK_GROUPS:(k + 1) * BANK_GROUPS],
                            g_ps[:, f % 2], ACT.Copy).then_inc(g_ready, 1)
                if ahead:
                    act.wait_ge(xt_done, t + 2)
                    need(act, d_done, t * FILLS)
                    nc.scalar.activation(xn_t[:, 1 - j, :], xt_ps[:, 0:S], ACT.Copy).then_inc(xt_ready, 1)
                    need(act, gap_ready, t + 1)
                    for n in range(TB):
                        for p in range(2):
                            act.wait_ge(sim_done, (t + 1) * 4 + n * 2 + p + 1)
                            nc.scalar.activation(sim[:, p, n], sim_ps[:, p, :].rearrange("p (h k) -> p h k", h=PH),
                                                 ACT.Copy).then_inc(sim_ready, 1)
                if now:
                    act.wait_ge(spread_ready, t + 1)
                    need(act, g_done, (t - 1) * GF)
                    for n in range(TB):
                        for q in range(Q4):
                            rows = slice(q * PICKS, (q + 1) * PICKS)
                            last = nc.scalar.activation(by_token[rows, j, n, :, q, :],
                                                        spread_t[rows, n].rearrange("p r g -> p g r"), ACT.Copy)
                    last.then_inc(by_token_ready, 1)

            turns(act, turn)

        @block.vector
        def _(dve):
            nc.vector.memset(by_token[:], 0.0).then_inc(const_set, 1)
            dve.wait_ge(const_in, CONSTS * 16)
            squares = [P, 2 * TB * PH, TOP, TOP]

            def output(t):
                dve.wait_ge(y_done, t - 1)
                xb = x[:, bass.ds((t - 2) * TB, TB), :]
                nc.vector.tensor_tensor(xb, xb, y_ps[:, 0:TB * D].rearrange("p (t d) -> p t d", t=TB),
                                        ALU.add).then_inc(x_ready, 1)

            def turn(t, j, ahead, now, before, last_):
                if ahead:
                    steps = Steps(dve, norm_steps, t + 1, NORM_STEPS)
                    norm_moments(nc, dve, steps, nb, x, t + 1)
                if now:
                    s = Steps(dve, pick_steps, t, PICK_STEPS)
                    for n in range(TB):
                        for p in range(2):
                            dve.wait_ge(sim_ready, t * 4 + n * 2 + p + 1)
                            apart(dve)
                            for h in range(PH):
                                last = nc.vector.max(best[:, p, n * PH + h, :], sim[:, p, n, h, :])
                    s.link(last)
                    apart(dve)
                    for p in range(2):
                        for n in range(TB):
                            for h in range(PH):
                                last = nc.vector.max_index(best_at[:, p, n * PH + h, :], best[:, p, n * PH + h, :], sim[:, p, n, h, :])
                    s.step(last)
                    s.link(nc.vector.tensor_tensor(sums[:], best[:, 0].unsqueeze(3).to_broadcast([P, TB * PH, TOP, TOP]),
                                                   best[:, 1].unsqueeze(2).to_broadcast([P, TB * PH, TOP, TOP]), ALU.add))
                    s.step(nc.vector.tensor_copy(at[:], best_at[:]))
                    for h in range(TB * PH):
                        last = nc.vector.max(top[:, h, :], sums[:, h].rearrange("p i j -> p (i j)"))
                    s.link(last)
                    apart(dve)
                    for h in range(TB * PH):
                        last = nc.vector.max_index(top_at[:, h, :], top[:, h, :], sums[:, h].rearrange("p i j -> p (i j)"))
                    s.step(last)
                    nc.vector.tensor_tensor(gap[:], top[:], top[:, :, 0:1].to_broadcast([P, TB * PH, TOP]),
                                            ALU.subtract).then_inc(gap_ready, 1)
                    s.settle()
                    if last_:
                        output(t)
                    s.step(nc.vector.tensor_scalar(out=rank_at[:, 0], in0=top_at[:], scalar1=3, scalar2=None,
                                                   op0=ALU.logical_shift_right))
                    s.link(nc.vector.tensor_scalar(out=rank_at[:, 1], in0=top_at[:], scalar1=TOP - 1, scalar2=None,
                                                   op0=ALU.bitwise_and))
                    s.link(nc.vector.tensor_copy(rank[:], rank_at[:]))
                    s.link(nc.vector.tensor_tensor(chosen[:], rank[:].rearrange("p a h s -> p (a h) s").unsqueeze(3).to_broadcast(squares),
                                                   iota[:, 0:TOP].unsqueeze(1).unsqueeze(1).to_broadcast(squares), ALU.is_equal))
                    s.link(nc.vector.tensor_tensor(chosen[:], chosen[:],
                                                   at[:].rearrange("p a h s -> p (a h) s").unsqueeze(2).to_broadcast(squares), ALU.mult))
                    s.link(nc.vector.tensor_reduce(pick[:].rearrange("p a h s -> p (a h) s"), chosen[:], AX.X, ALU.add))
                    s.link(nc.vector.tensor_scalar(out=beyond[:], in0=pick[:, 0], scalar1=EX - 0.5, scalar2=PK - 1.0,
                                                   op0=ALU.is_gt, op1=ALU.mult))
                    s.step(nc.vector.tensor_scalar(out=pick[:, 0], in0=pick[:, 0], scalar1=EX - 1.0, scalar2=None, op0=ALU.min))
                    s.link(nc.vector.tensor_tensor(pick[:, 1], pick[:, 1], beyond[:], ALU.max))
                    need(dve, ones_1_ready, t)
                    nc.vector.transpose(y_t[:].rearrange("p n g -> p (n g)"),
                                        pick[:, 1].rearrange("p h s -> p (h s)")).then_inc(y_t_ready, 1)
                    dve.wait_ge(y_t_ready, t + 1)
                    need(dve, g_done, (t - 1) * GF)
                    wide = [P, PICKS, PK]
                    nc.vector.tensor_tensor(ones_y[:, j, 0], y_t[:, 0].unsqueeze(2).to_broadcast(wide),
                                            iota[:].unsqueeze(1).to_broadcast(wide), ALU.is_equal).then_inc(ones_ready, 1)
                    dve.wait_ge(exp_ready, t + 1)
                    s.link(nc.vector.tensor_reduce(total[:], ex[:], AX.X, ALU.add))
                    s.link(nc.vector.reciprocal(total[:], total[:]))
                    s.link(nc.vector.tensor_tensor(weight[:], ex[:], total[:].unsqueeze(2).to_broadcast([P, TB * PH, TOP]), ALU.mult))
                    by_x = [P, TB, EX, PICKS]
                    s.link(nc.vector.tensor_tensor(
                        spread, pick[:, 0].rearrange("p (n h) s -> p n (h s)", n=TB).unsqueeze(2).to_broadcast(by_x),
                        iota[:, 0:EX].unsqueeze(1).unsqueeze(3).to_broadcast(by_x), ALU.is_equal))
                    s.link(nc.vector.tensor_tensor(
                        spread, spread, weight[:].rearrange("p (n h) s -> p n (h s)", n=TB).unsqueeze(2).to_broadcast(by_x),
                        ALU.mult))
                    s.close()
                    need(dve, by_token_ready, t)
                    nc.vector.transpose(spread_t[:].rearrange("p n r g -> p (n r g)"),
                                        spread.rearrange("p n r s -> p (n r s)")).then_inc(spread_ready, 1)
                elif last_:
                    output(t)
                if ahead:
                    need(dve, xt_done, t + 1)
                    norm_apply(nc, dve, steps, nb, x, t + 1, xn)
                if before:
                    dve.wait_ge(d_ready, t * FILLS)
                    nc.vector.tensor_tensor(acts[:, EXPERT_BLOCKS:UP_BLOCKS, :], acts[:, EXPERT_BLOCKS:UP_BLOCKS, :],
                                            acts[:, UP_BLOCKS:DOWN_BLOCKS, :], ALU.mult).then_inc(w_ready, 1)
                    dve.wait_ge(g_ready, t * GF)
                    nc.vector.tensor_tensor(acts[:, 0:EXPERT_BLOCKS, :], acts[:, 0:EXPERT_BLOCKS, :], g[:],
                                            ALU.mult).then_inc(w_ready, 1)

            turns(dve, turn)





def one_head_layer(nc, a, x, ident, later_loads):
    from contextlib import ExitStack
    scale = D ** -0.5
    with ExitStack() as stack:
        mem = Memory(nc, stack, "k3")
        nb = NormBuffers(mem)
        w = mem.sbuf("w", [P, 4, D])
        b_qk = mem.sbuf("b_qk", [P, 2])
        b_vo = mem.sbuf("b_vo", [P, 2, D])
        mask_in = mem.sbuf("mask_in", [1, B, S], U8)
        mask = mem.sbuf("mask", [1, B, S], BF16)
        ones = mem.sbuf("ones", [1, P], BF16)
        ctx_t = mem.sbuf("ctx_t", [P, 2, S])
        xn = mem.sbuf("xn", [P, 2, TB, D])
        xn_t = mem.sbuf("xn_t", [P, 2, S])
        q_t = mem.sbuf("q_t", [P, 2, S])
        k_t = mem.sbuf("k_t", [P, 2, S])
        v = mem.sbuf("v", [P, 2, TB, D])
        neg_max = mem.sbuf("neg_max", [P, 2, TB])
        p = mem.sbuf("p", [P, 2, TB, S])
        total = mem.sbuf("total", [P, 2, TB])
        p_t = mem.sbuf("p_t", [P, TB, S])
        o_t = mem.sbuf("o_t", [P, S])
        recip = mem.sbuf("recip", [P, TB])
        xt_ps = mem.psum("xt_ps", [P, 512])
        qk_ps = mem.psum("qk_ps", [P, 2, S])
        v_ps = mem.psum("v_ps", [P, 512])
        s_ps = mem.psum("s_ps", [P, 2, TB, S])
        pt_ps = mem.psum("pt_ps", [P, TB, S])
        o_ps = mem.psum("o_ps", [P, 512])
        out_ps = mem.psum("out_ps", [P, 512])

        const_in = mem.sem("const_in")
        const_set = mem.sem("const_set")
        ctx_in = [mem.sem(f"ctx_in_{j}") for j in range(2)]
        xt_done = mem.sem("xt_done")
        xt_ready = mem.sem("xt_ready")
        qk_done = mem.sem("qk_done")
        qk_ready = mem.sem("qk_ready")
        v_done = mem.sem("v_done")
        v_ready = mem.sem("v_ready")
        s_done = mem.sem("s_done")
        max_ready = mem.sem("max_ready")
        p_ready = mem.sem("p_ready")
        pt_done = mem.sem("pt_done")
        pt_ready = mem.sem("pt_ready")
        o_done = mem.sem("o_done")
        o_ready = mem.sem("o_ready")
        out_done = mem.sem("out_done")
        x_ready = mem.sem("x_ready")
        norm_steps = mem.sem("norm_steps")
        out_steps = mem.sem("out_steps")
        block = stack.enter_context(nc.Block())

        def need(engine, sem, value):
            if not isinstance(value, int) or value > 0:
                engine.wait_ge(sem, value)

        def turns(engine, turn):
            turn(0, 0, True, False)
            turn(1, 1, True, True)
            with engine.Fori(1, B // 2) as i:
                for j in range(2):
                    turn(i * 2 + j, j, True, True)
            turn(B, 0, False, True)

        def half(t, j):
            return t // 2 if isinstance(t, int) else (t - j) // 2

        @block.sync
        def _(sync):
            for t, n in ((w, "k3_w"), (b_qk, "k3_b_qk"), (b_vo, "k3_b_vo"), (mask_in, "k3_mask")):
                sync.dma_start(t[:], a[n]).then_inc(const_in, 16)

            def turn(t, j, now, before):
                if now:
                    need(sync, qk_done, t - 1)
                    sync.dma_start(ctx_t[:, j, :], a["ctx_t"][:, bass.ds(t, 1), :]).then_inc(ctx_in[j], 16)

            turns(sync, turn)

        @block.gpsimd
        def _(pool):
            norm_power_set(nc, pool, nb)
            with pool.Fori(0, B) as b:
                norm_gpsimd(nc, pool, nb, b)

        @block.tensor
        def _(pe):
            pe.wait_ge(const_in, 64)
            pe.wait_ge(const_set, 2)

            def turn(t, j, now, before):
                if now:
                    pe.wait_ge(ctx_in[j], half(t, j) * 16 + 16)
                    need(pe, v_ready, t)
                    for n in range(TB):
                        last = nc.tensor.matmul(v_ps[:, n * D:(n + 1) * D], ctx_t[:, j, n * P:(n + 1) * P], w[:, 2, :],
                                                start=True, stop=True)
                    last.then_inc(v_done, 1)
                    pe.wait_ge(nb.ready, t + 1)
                    need(pe, xt_ready, t)
                    for n in range(TB):
                        last = nc.tensor.transpose(xt_ps[:, n * P:(n + 1) * P], xn[:, j, n, :], ident[:])
                    last.then_inc(xt_done, 1)
                    need(pe, qk_ready, t)
                    nc.tensor.matmul(qk_ps[:, 1, :], w[:, 1, :], ctx_t[:, j, :], start=True, stop=True)
                    pe.wait_ge(xt_ready, t + 1)
                    nc.tensor.matmul(qk_ps[:, 0, :], w[:, 0, :], xn_t[:, j, :], start=True, stop=True).then_inc(qk_done, 1)
                if before:
                    pe.wait_ge(p_ready, t)
                    need(pe, pt_ready, t - 1)
                    for kt in range(TB):
                        for qt in range(TB):
                            last = nc.tensor.transpose(pt_ps[:, kt, qt * P:(qt + 1) * P], p[:, 1 - j, qt, kt * P:(kt + 1) * P],
                                                       ident[:])
                    last.then_inc(pt_done, 1)
                if now:
                    pe.wait_ge(qk_ready, t + 1)
                    need(pe, p_ready, t - 1)
                    for qt in range(TB):
                        nc.tensor.matmul(s_ps[:, j, qt, :], q_t[:, j, qt * P:(qt + 1) * P], k_t[:, j, :],
                                         start=qt == 0, stop=False, skip_group_check=True)
                    nc.tensor.matmul(s_ps[:, j], ones[:], mask[:, bass.ds(t, 1), :].to_broadcast([1, TB, S]),
                                     start=False, stop=True, skip_group_check=True).then_inc(s_done, 1)
                if before:
                    pe.wait_ge(pt_ready, t)
                    pe.wait_ge(v_ready, t)
                    need(pe, o_ready, t - 1)
                    for kt in range(TB):
                        last = nc.tensor.matmul(o_ps[:, 0:S], v[:, 1 - j, kt, :], p_t[:, kt, :], start=kt == 0, stop=kt == 1)
                    last.then_inc(o_done, 1)
                    pe.wait_ge(o_ready, t)
                    need(pe, x_ready, t - 1)
                    for qt in range(TB):
                        last = nc.tensor.matmul(out_ps[:, qt * D:(qt + 1) * D], o_t[:, qt * P:(qt + 1) * P], w[:, 3, :],
                                                start=True, stop=True)
                    last.then_inc(out_done, 1)

            turns(pe, turn)

        @block.scalar
        def _(act):
            act.wait_ge(const_in, 64)
            later_loads(act)

            def turn(t, j, now, before):
                if now:
                    act.wait_ge(xt_done, t + 1)
                    need(act, qk_done, t - 1)
                    nc.scalar.activation(xn_t[:, j, :], xt_ps[:, 0:S], ACT.Copy).then_inc(xt_ready, 1)
                if before:
                    act.wait_ge(pt_done, t)
                    need(act, o_done, t - 1)
                    nc.scalar.activation(p_t[:], pt_ps[:], ACT.Copy).then_inc(pt_ready, 1)
                    act.wait_ge(o_done, t)
                    need(act, out_done, t - 1)
                    nc.scalar.activation(o_t[:], o_ps[:, 0:S], ACT.Copy).then_inc(o_ready, 1)
                if now:
                    act.wait_ge(max_ready, t + 1)
                    need(act, pt_done, t - 1)
                    need(act, x_ready, t - 1)
                    for qt in range(TB):
                        last = nc.scalar.activation(p[:, j, qt, :], s_ps[:, j, qt, :], ACT.Exp, bias=neg_max[:, j, qt:qt + 1],
                                                    accum_out=total[:, j, qt:qt + 1])
                    last.then_inc(p_ready, 1)

            turns(act, turn)

        @block.vector
        def _(dve):
            nc.vector.memset(ones[:], 1.0).then_inc(const_set, 1)
            dve.wait_ge(const_in, 64)
            nc.vector.tensor_scalar(out=mask[:], in0=mask_in[:], scalar1=0.0, scalar2=MASKED,
                                    op0=ALU.is_equal, op1=ALU.mult).then_inc(const_set, 1)

            def turn(t, j, now, before):
                if now:
                    steps = Steps(dve, norm_steps, t, NORM_STEPS)
                    need(dve, xt_done, t - 1)
                    norm_vector(nc, dve, steps, nb, x, t, xn[:, j])
                    dve.wait_ge(v_done, t + 1)
                    need(dve, o_done, t - 1)
                    nc.vector.tensor_tensor(v[:, j], v_ps[:, 0:TB * D].rearrange("p (t d) -> p t d", t=TB),
                                            b_vo[:, 0:1, :].to_broadcast([P, TB, D]), ALU.add).then_inc(v_ready, 1)
                    dve.wait_ge(qk_done, t + 1)
                    need(dve, s_done, t - 1)
                    nc.vector.tensor_scalar(out=k_t[:, j, :], in0=qk_ps[:, 1, :], scalar1=b_qk[:, 1:2], scalar2=None, op0=ALU.add)
                    nc.vector.tensor_scalar(out=q_t[:, j, :], in0=qk_ps[:, 0, :], scalar1=b_qk[:, 0:1], scalar2=scale,
                                            op0=ALU.add, op1=ALU.mult).then_inc(qk_ready, 1)
                    dve.wait_ge(s_done, t + 1)
                    need(dve, p_ready, t - 1)
                    nc.vector.tensor_reduce(neg_max[:, j, :], s_ps[:, j], AX.X, ALU.max, negate=True).then_inc(max_ready, 1)
                if before:
                    out = Steps(dve, out_steps, t - 1, 3)
                    xb = x[:, bass.ds((t - 1) * TB, TB), :]
                    need(dve, x_ready, t - 1)
                    out.step(nc.vector.tensor_tensor(xb, xb, b_vo[:, 1:2, :].to_broadcast([P, TB, D]), ALU.add))
                    dve.wait_ge(p_ready, t)
                    out.link(nc.vector.reciprocal(recip[:], total[:, 1 - j, :]))
                    dve.wait_ge(out_done, t)
                    out.step(nc.vector.scalar_tensor_tensor(out=x[:, bass.ds((t - 1) * TB, 1), :], in0=out_ps[:, 0:D],
                                                            scalar=recip[:, 0:1], in1=x[:, bass.ds((t - 1) * TB, 1), :],
                                                            op0=ALU.mult, op1=ALU.add))
                    nc.vector.scalar_tensor_tensor(out=x[:, bass.ds((t - 1) * TB + 1, 1), :], in0=out_ps[:, D:2 * D],
                                                   scalar=recip[:, 1:2], in1=x[:, bass.ds((t - 1) * TB + 1, 1), :],
                                                   op0=ALU.mult, op1=ALU.add).then_inc(x_ready, 1)
                    out.close()

            turns(dve, turn)



def build(nc, a, out):
    from contextlib import ExitStack
    with ExitStack() as stack:
        mem = Memory(nc, stack, "all")
        x = mem.sbuf("x", [P, NT, D])
        ident = mem.sbuf("ident", [P, P])
        zeros = mem.sbuf("zeros", [P, D])
        slots_x = nc.dram_tensor("slots_x", (MOST_SLOTS, D), F32, kind="Internal").ap()
        slots_y = nc.dram_tensor("slots_y", (MOST_SLOTS, D), F32, kind="Internal").ap()
        start_in = mem.sem("start_in")
        zeros_set = mem.sem("zeros_set")
        stored = mem.sem("stored")
        Memory.carried = mem.sem("carried")
        Memory.zeroed = mem.sem("zeroed")
        Memory.scattered = mem.sem("scattered")
        Memory.gathered = [mem.sem(f"gathered_{t}") for t in range(NT)]
        Memory.loaded = {mix.name: mem.sem(f"loaded_{mix.name}") for mix in (MIX0, MIX1, MIX3)}
        Memory.rounds = 0
        Memory.used = []
        with nc.Block() as block:
            @block.sync
            def _(sync):
                sync.dma_start(x[:], a["x"]).then_inc(start_in, 16)
                sync.dma_start(ident[:], a["ident"]).then_inc(start_in, 16)
                sync.wait_ge(zeros_set, 1)
                sync.dma_start(slots_x.rearrange("(n p) d -> p n d", p=P),
                               zeros[:].unsqueeze(1).to_broadcast([P, MOST_SLOTS // P, D])).then_inc(Memory.zeroed, 16)
                sync.wait_ge(start_in, 32)

            @block.vector
            def _(dve):
                nc.vector.memset(zeros[:], 0.0).then_inc(zeros_set, 1)
        with ExitStack() as layer:
            weights = mixture_weights(nc, a, MIX0, layer)
            with ExitStack() as inner:
                m = Memory(nc, inner, "l0")
                xn_t = m.sbuf("xn_t", [P, B * S])
                cols = (m.sbuf("g_col", [P, TB, BH]), m.sbuf("e_col", [P, TB, BH]), m.sbuf("neg_g_row", [1, BH * S]))
                mlstm_gates(nc, a, x, ident, xn_t, cols, weights.start_loads)
                mlstm_attention(nc, a, x, xn_t, cols)
            clear_semaphores(nc)
            mixture_layer(nc, a, x, ident, MIX0, weights, slots_x, slots_y)
        clear_semaphores(nc)

        with ExitStack() as layer:
            weights = mixture_weights(nc, a, MIX1, layer)
            heads_layer(nc, a, x, ident, HEADS1, weights.start_loads)
            clear_semaphores(nc)

            mixture_layer(nc, a, x, ident, MIX1, weights, slots_x, slots_y)
        clear_semaphores(nc)

        heads_layer(nc, a, x, ident, HEADS2)
        clear_semaphores(nc)

        keyed_layer(nc, a, x, ident)
        clear_semaphores(nc)

        with ExitStack() as layer:
            weights = mixture_weights(nc, a, MIX3, layer)
            one_head_layer(nc, a, x, ident, weights.start_loads)
            clear_semaphores(nc)

            mixture_layer(nc, a, x, ident, MIX3, weights, slots_x, slots_y)
        with nc.Block() as block:
            @block.sync
            def _(sync):
                sync.dma_start(out, x[:]).then_inc(stored, 16)
                sync.wait_ge(stored, 16)


def rows_by_tile(m):
    return m.reshape(NT, P, D).transpose(1, 0, 2)


def laid_out(v):
    g = {n: np.asarray(m) for n, m in v.items()}
    z = {}
    z["x"] = rows_by_tile(g["x"])
    z["ctx_n"] = rows_by_tile(g["ctx_1024"])
    z["ctx_t"] = g["ctx_1024"].transpose(2, 0, 1)
    z["ident"] = np.eye(P, dtype=np.float32)
    w = np.zeros((P, 3, 36), np.float32)
    w[:, :, 0:MH] = g["L0_xattn_w_igate"].reshape(MH, 3, D).transpose(2, 1, 0)
    w[:, :, 32:32 + MH] = g["L0_xattn_w_fgate"].reshape(MH, 3, D).transpose(2, 1, 0)
    z["w_gates"] = w
    z["b_gates"] = np.stack([np.repeat(g["L0_xattn_b_igate"], B), np.repeat(g["L0_xattn_b_fgate"], B)], axis=1)
    s = np.arange(S)
    z["causal"] = np.where(np.arange(P)[:, None] <= s[None, :], 0.0, -1e30).astype(np.float32)
    z["ln_scale"] = np.tile(g["L0_xattn_ln_weight"], (P, 1))
    z["before"] = np.triu(np.ones((P, P), np.float32), 1)
    z["iota_e"] = np.tile(np.arange(E, dtype=np.float32), (P, 1))
    z["keep"] = np.tile((np.arange(NT) > 0).astype(np.float32), (P, E, 1))
    z["tile_starts"] = np.tile(np.arange(NT, dtype=np.float32) * P, (P, 1))
    none = np.zeros(E, np.float32)
    for mix, router, biases, w1, w2 in (
            (MIX0, g["L0_ffn_gate_w"].T, (g["L0_ffn_gate_b"], g["L0_ffn_expert_bias"]), g["L0_ffn_w1"], g["L0_ffn_w2"]),
            (MIX1, g["L1_ffn_router_w"], (g["L1_ffn_router_b"], none), g["L1_ffn_w1"], g["L1_ffn_w2"]),
            (MIX3, g["L3_ffn_Wr"], (g["L3_ffn_br"], none), g["L3_ffn_W1"], g["L3_ffn_W2"])):
        n = mix.name
        z[n + "_router"] = router
        z[n + "_router_b"] = np.tile(np.stack(biases), (P, 1, 1))
        z[n + "_iota_s"] = np.tile(np.arange(mix.tiles, dtype=np.float32), (P, 1))
        z[n + "_w1"] = w1.transpose(1, 0, 2).reshape(P, E * mix.wide)
        z[n + "_w2"] = w2.reshape(E, mix.h // P, P, D).transpose(2, 0, 1, 3).reshape(P, E * mix.h)
    z["f0_b1"], z["f0_b2"] = g["L0_ffn_b1"].reshape(1, -1), g["L0_ffn_b2"].reshape(1, -1)
    z["f3_b1"], z["f3_b2"] = g["L3_ffn_b1"].reshape(1, -1), g["L3_ffn_b2"].reshape(1, -1)

    def slots(w):
        heads = w.reshape(-1, G, HG, HD)
        return np.concatenate([heads] * 3 + [np.zeros_like(heads)], axis=3).reshape(-1, G, P)

    z["ctx_t"] = g["ctx_1024"].transpose(2, 0, 1)
    row = np.arange(P) % SLOT
    low = np.stack([(row >= 2 * HD) & (row < 3 * HD), (row >= HD) & (row < 2 * HD)], axis=1).astype(np.float32)
    ones = ((row >= MAX_ROW) & (row < MAX_ROW + 2)).astype(np.float32)
    nil = np.zeros(D, np.float32)
    for n, q, k, v, o, bq, bk, bv, bo in (
            ("h1", *(g["L1_xattn_W_" + c].T for c in "qkvo"), nil, nil, nil, nil),
            ("h2", *(g["L2_xattn_W" + c].T for c in "qkvo"), *(g["L2_xattn_b" + c] for c in "qkvo"))):
        z[n + "_w_qk"] = np.stack([slots(q), slots(k)], axis=1)
        z[n + "_w_v"], z[n + "_w_o"] = v, o
        z[n + "_b_v"], z[n + "_b_o"] = np.tile(bv, (P, 1)), np.tile(bo, (P, 1))
        b = np.stack([slots(bq[None])[0].T, slots(bk[None])[0].T], axis=1)
        z[n + "_b_low"] = np.where(low[:, :, None] > 0, b, 0.0).astype(np.float32)
        b[:, 1] = np.where(ones[:, None] > 0, np.float32(1.0), b[:, 1])
        z[n + "_b_qk"] = b
        z[n + "_low"] = low
    mask = g["mask_1x1xSxS2_ik0"][0, 0]
    z["h1_mask"] = np.stack([mask.reshape(TB, P, S), mask.T.reshape(TB, P, S)]).transpose(2, 0, 1, 3)



    z["iota"] = np.tile(np.arange(PK, dtype=np.float32), (P, 1))
    z["pk_w_q"] = g["L2_ffn_Wq"].reshape(2 * PH, HALF, D).transpose(1, 0, 2)
    z["pk_keys"] = g["L2_ffn_keys"].transpose(3, 2, 0, 1).reshape(HALF, 2 * PH, PK)
    z["pk_down"] = np.concatenate([g["L2_ffn_down_embed"].reshape(EX, PK, D), g["L2_ffn_Wg"].reshape(MLP_BLOCKS, P, D),
                                   g["L2_ffn_Wu"].reshape(MLP_BLOCKS, P, D)]).transpose(2, 0, 1)
    z["pk_up"] = np.concatenate([g["L2_ffn_up_embed"].reshape(EX, PK, D),
                                 g["L2_ffn_Wd"].T.reshape(MLP_BLOCKS, P, D)]).transpose(1, 0, 2)

    z["k3_w"] = np.stack([g["L3_xattn_W" + c] for c in "qkvo"], axis=1)
    z["k3_b_qk"] = np.stack([g["L3_xattn_bq"], g["L3_xattn_bk"]], axis=1)
    z["k3_b_vo"] = np.tile(np.stack([g["L3_xattn_bv"], g["L3_xattn_bo"]]), (P, 1, 1))
    z["k3_mask"] = g["mask_BxS2_bk0"][None]
    return {n: np.ascontiguousarray(m) for n, m in z.items()}


def kernel(**inputs):
    import concourse.bacc as bacc
    from concourse.bass_utils import run_bass_kernel_spmd

    arrays = laid_out(inputs)
    nc = bacc.Bacc("TRN2", target_bir_lowering=False, num_devices=1)
    a = {n: nc.dram_tensor(f"in_{n}", m.shape, mybir.dt.from_np(m.dtype), kind="ExternalInput").ap()
         for n, m in arrays.items()}
    out = nc.dram_tensor("out_x", (P, NT, D), F32, kind="ExternalOutput").ap()
    build(nc, a, out)
    r = run_bass_kernel_spmd(nc, [{f"in_{n}": m for n, m in arrays.items()}], core_ids=[0])
    return r.results[0]["out_x"].transpose(1, 0, 2).reshape(B, S, D)
```

```python
import numpy as np

import concourse.bass as bass
import concourse.mybir as mybir

F32 = mybir.dt.float32
F32R = mybir.dt.float32r
BF16 = mybir.dt.bfloat16
I32 = mybir.dt.int32
U32 = mybir.dt.uint32
U8 = mybir.dt.uint8
ALU = mybir.AluOpType
ACT = mybir.ActivationFunctionType
AX = mybir.AxisListType

P = 128
D = 128
B = 8
S = 256
TB = S // P
NT = B * TB
LN_EPS = 1e-5


class Memory:

    carried = None
    used = []
    zeroed = None
    scattered = None
    gathered = []
    loaded = {}
    rounds = 0

    def __init__(self, nc, stack, prefix):
        self.nc, self.stack, self.prefix = nc, stack, prefix

    def sbuf(self, name, shape, dtype=F32):
        return self.stack.enter_context(self.nc.sbuf_tensor(f"{self.prefix}_{name}", shape, dtype))

    def psum(self, name, shape, dtype=F32):
        return self.stack.enter_context(self.nc.psum_tensor(f"{self.prefix}_{name}", shape, dtype))

    def sem(self, name):
        sem = self.stack.enter_context(self.nc.semaphore(f"{self.prefix}_{name}"))
        Memory.used.append(sem)
        return sem


def apart(engine):
    engine.sem_inc(Memory.carried, 1)


def clear_semaphores(nc):
    with nc.Block() as block:
        @block.gpsimd
        def _(pool):
            for sem in Memory.used:
                pool.sem_clear(sem)
    Memory.used = []


class Steps:

    def __init__(self, engine, sem, turn=0, per_turn=0):
        self.engine, self.sem, self.base, self.n, self.per_turn = engine, sem, turn * per_turn, 0, per_turn

    def step(self, instruction):
        instruction.then_inc(self.sem, 1)
        self.n += 1

    def settle(self):
        self.engine.wait_ge(self.sem, self.base + self.n)

    def link(self, instruction):
        self.step(instruction)
        self.settle()

    def close(self):
        assert not self.per_turn or self.n == self.per_turn, (self.n, self.per_turn)


class NormBuffers:

    def __init__(self, mem):
        self.stats = mem.sbuf("ln_stats", [P, TB, 6])
        self.mean_var = mem.sbuf("ln_mean_var", [P, TB, 2])
        self.var_eps = mem.sbuf("ln_var_eps", [P, TB])
        self.rstd = mem.sbuf("ln_rstd", [P, TB])
        self.power = mem.sbuf("ln_power", [P, TB])
        self.power_set = mem.sem("ln_power_set")
        self.moments_ready = mem.sem("ln_moments_ready")
        self.rstd_ready = mem.sem("ln_rstd_ready")
        self.ready = mem.sem("ln_ready")

NORM_STEPS = 4


def norm_moments(nc, dve, steps, nb, x, b):
    for t in range(TB):
        steps.step(nc.vector.bn_stats(nb.stats[:, t, :], x[:, bass.ds(b * TB + t, 1), :]))
    steps.settle()
    apart(dve)
    steps.step(nc.vector.bn_aggr(nb.mean_var[:, 0, :], nb.stats[:, 0, :]))
    nc.vector.bn_aggr(nb.mean_var[:, 1, :], nb.stats[:, 1, :]).then_inc(nb.moments_ready, 1)


def norm_apply(nc, dve, steps, nb, x, b, out):
    dve.wait_ge(nb.rstd_ready, b * 2 + 2)
    steps.step(nc.vector.tensor_scalar(out=out[:, 0, :], in0=x[:, bass.ds(b * TB, 1), :],
                                       scalar1=nb.mean_var[:, 0, 0:1], scalar2=nb.rstd[:, 0:1],
                                       op0=ALU.subtract, op1=ALU.mult))
    nc.vector.tensor_scalar(out=out[:, 1, :], in0=x[:, bass.ds(b * TB + 1, 1), :],
                            scalar1=nb.mean_var[:, 1, 0:1], scalar2=nb.rstd[:, 1:2],
                            op0=ALU.subtract, op1=ALU.mult).then_inc(nb.ready, 1)
    dve.wait_ge(nb.ready, b + 1)


def norm_vector(nc, dve, steps, nb, x, b, out):
    norm_moments(nc, dve, steps, nb, x, b)
    norm_apply(nc, dve, steps, nb, x, b, out)


def norm_power_set(nc, pool, nb):
    nc.gpsimd.memset(nb.power[:], -0.5).then_inc(nb.power_set, 1)
    pool.wait_ge(nb.power_set, 1)


def norm_gpsimd(nc, pool, nb, b):
    pool.wait_ge(nb.moments_ready, b + 1)
    apart(pool)
    nc.gpsimd.tensor_scalar(out=nb.var_eps[:], in0=nb.mean_var[:, :, 1], scalar1=LN_EPS, scalar2=None,
                            op0=ALU.add).then_inc(nb.rstd_ready, 1)
    pool.wait_ge(nb.rstd_ready, b * 2 + 1)
    nc.gpsimd.tensor_tensor(nb.rstd[:], nb.var_eps[:], nb.power[:], ALU.pow).then_inc(nb.rstd_ready, 1)



MH = 4
MD = D // MH
BH = MH * B
MSCALE = 1.0 / MD ** 0.5


def mlstm_gates(nc, a, x, ident, xn_t, cols, later_loads):
    g_col, e_col, neg_g_row = cols
    from contextlib import ExitStack
    with ExitStack() as stack:
        mem = Memory(nc, stack, "m0")
        nb = NormBuffers(mem)
        xn = mem.sbuf("xn", [P, 2, TB, D])
        ctx_t = mem.sbuf("ctx_t", [P, B, S])
        w_gates = mem.sbuf("w_gates", [P, 3, 36])
        b_gates = mem.sbuf("b_gates", [BH, 2])
        gates = mem.sbuf("gates", [36, B, S])
        i_rows = mem.sbuf("i_rows", [BH, S])
        f_rows = mem.sbuf("f_rows", [BH, S])
        abs_f = mem.sbuf("abs_f", [BH, S])
        exp_f = mem.sbuf("exp_f", [BH, S])
        ln_f = mem.sbuf("ln_f", [BH, S])
        log_f = mem.sbuf("log_f", [BH, S])
        ones = mem.sbuf("ones", [BH, S])
        f_sum = mem.sbuf("f_sum", [BH, S])
        g_rows = mem.sbuf("g_rows", [BH, S])
        g_max = mem.sbuf("g_max", [BH, S])
        neg_g = mem.sbuf("neg_g", [BH, S])
        neg_g_parts = mem.sbuf("neg_g_parts", [BH, 3, S], BF16)
        top = mem.sbuf("top", [BH, S])
        t_ps = mem.psum("t_ps", [P, 2, 512])
        gate_ps = mem.psum("gate_ps", [36, 2, 512])
        col_ps = mem.psum("col_ps", [P, 512])

        const_in = mem.sem("const_in")
        transposed = mem.sem("transposed")
        xn_t_ready = mem.sem("xn_t_ready")
        projected = mem.sem("projected")
        gates_ready = mem.sem("gates_ready")
        rows_in = mem.sem("rows_in")
        steps_done = mem.sem("steps_done")
        row_steps = mem.sem("row_steps")
        abs_ready = mem.sem("abs_ready")
        exp_ready = mem.sem("exp_ready")
        log_ready = mem.sem("log_ready")
        scans_ready = mem.sem("scans_ready")
        cols_ready = mem.sem("cols_ready")
        cols_out = mem.sem("cols_out")
        row_out = mem.sem("row_out")
        block = stack.enter_context(nc.Block())

        @block.sync
        def _(sync):
            sync.dma_start(w_gates[:], a["w_gates"]).then_inc(const_in, 16)
            sync.dma_start(b_gates[:], a["b_gates"]).then_inc(const_in, 16)
            sync.dma_start(ctx_t[:], a["ctx_t"]).then_inc(const_in, 16)
            sync.wait_ge(gates_ready, B + 2)
            for h in range(MH):
                for rows, at in ((f_rows, 32 + h), (i_rows, h)):
                    sync.dma_start(rows[h * B:(h + 1) * B, :], gates[at:at + 1, :, :]).then_inc(rows_in, 16)
            sync.wait_ge(scans_ready, 2)
            for n in range(3):
                sync.dma_start(neg_g_row[n:n + 1, :].rearrange("o (r s) -> o r s", s=S),
                               neg_g_parts[:, n, :]).then_inc(row_out, 16)
            sync.wait_ge(row_out, 48)

        @block.gpsimd
        def _(pool):
            norm_power_set(nc, pool, nb)
            with pool.Fori(0, B) as b:
                norm_gpsimd(nc, pool, nb, b)

        @block.vector
        def _(dve):
            nc.vector.memset(ones[:], 1.0).then_inc(row_steps, 1)
            with dve.Fori(0, B // 2) as i:
                for j in range(2):
                    b = i * 2 + j
                    steps = Steps(dve, steps_done, b, NORM_STEPS)
                    dve.wait_ge(transposed, b + 1)
                    norm_vector(nc, dve, steps, nb, x, b, xn[:, j])
                    steps.close()
            dve.wait_ge(rows_in, 2 * MH * 16)
            rows = Steps(dve, row_steps)
            rows.n = 1
            rows.link(nc.vector.tensor_scalar(out=f_rows[:], in0=f_rows[:], scalar1=b_gates[:, 1:2],
                                              scalar2=None, op0=ALU.add))
            nc.vector.scalar_tensor_tensor(out=abs_f[:], in0=f_rows[:], scalar=-1.0, in1=f_rows[:],
                                           op0=ALU.mult, op1=ALU.max).then_inc(abs_ready, 1)
            dve.wait_ge(log_ready, 1)
            rows.link(nc.vector.scalar_tensor_tensor(out=log_f[:], in0=f_rows[:], scalar=0.0, in1=ln_f[:],
                                                     op0=ALU.min, op1=ALU.subtract))
            rows.link(nc.vector.tensor_tensor_scan(f_sum[:], ones[:], log_f[:], 0.0, ALU.mult, ALU.add))
            rows.link(nc.vector.scalar_tensor_tensor(out=g_rows[:], in0=i_rows[:], scalar=b_gates[:, 0:1],
                                                     in1=f_sum[:], op0=ALU.add, op1=ALU.subtract))
            rows.link(nc.vector.tensor_tensor_scan(g_max[:], g_rows[:], g_rows[:], -3e38, ALU.max, ALU.max))
            nc.vector.tensor_tensor(top[:], f_sum[:], g_max[:], ALU.add).then_inc(scans_ready, 1)
            rows.link(nc.vector.tensor_scalar(out=neg_g[:], in0=g_max[:], scalar1=-1.0, scalar2=None, op0=ALU.mult))
            for n in range(3):
                part = nc.vector.tensor_copy(neg_g_parts[:, n, :], neg_g[:])
                if n < 2:
                    rows.link(part)
                    rows.link(nc.vector.tensor_tensor(neg_g[:], neg_g[:], neg_g_parts[:, n, :], ALU.subtract))
            part.then_inc(scans_ready, 1)

        @block.tensor
        def _(pe):
            pe.wait_ge(const_in, 48)
            pe.sem_inc(transposed, 2)

            def turn_x(b, j):
                pe.wait_ge(nb.ready, b + 1)
                pe.wait_ge(xn_t_ready, b + 1)
                for t in range(TB):
                    last = nc.tensor.transpose(t_ps[:, j, t * P:(t + 1) * P], xn[:, j, t, :], ident[:])
                last.then_inc(transposed, 1)

            def gates_of(b, j):
                pe.wait_ge(gates_ready, b + 1)
                pe.wait_ge(xn_t_ready, b + 3)
                nc.tensor.matmul(gate_ps[:, j, 0:S], w_gates[:, 0, :], xn_t[:, bass.ds(b * S, S)],
                                 start=True, stop=False)
                nc.tensor.matmul(gate_ps[:, j, 0:S], w_gates[:, 1, :], ctx_t[:, bass.ds(b, 1), :],
                                 start=False, stop=False)
                nc.tensor.matmul(gate_ps[:, j, 0:S], w_gates[:, 2, :], ctx_t[:, bass.ds(b, 1), :],
                                 start=False, stop=True).then_inc(projected, 1)

            turn_x(0, 0)
            with pe.Fori(0, B // 2 - 1) as i:
                for j in range(2):
                    turn_x(i * 2 + j + 1, 1 - j)
                    gates_of(i * 2 + j, j)
            turn_x(B - 1, 1)
            gates_of(B - 2, 0)
            gates_of(B - 1, 1)
            pe.wait_ge(scans_ready, 1)
            for n, rows in enumerate((g_rows, top)):
                for t in range(TB):
                    last = nc.tensor.transpose(col_ps[:, (n * TB + t) * BH:(n * TB + t + 1) * BH],
                                               rows[:, t * P:(t + 1) * P], ident[0:BH, 0:BH])
            last.then_inc(cols_ready, 1)

        @block.scalar
        def _(act):
            act.wait_ge(const_in, 48)
            later_loads(act)
            act.sem_inc(xn_t_ready, 2)
            act.sem_inc(gates_ready, 2)

            def keep_turned(b, j):
                act.wait_ge(transposed, b + 3)
                nc.scalar.activation(xn_t[:, bass.ds(b * S, S)], t_ps[:, j, 0:S], ACT.Copy).then_inc(xn_t_ready, 1)

            def keep_gates(b, j):
                act.wait_ge(projected, b + 1)
                nc.scalar.activation(gates[:, bass.ds(b, 1), :], gate_ps[:, j, 0:S], ACT.Copy).then_inc(gates_ready, 1)

            keep_turned(0, 0)
            with act.Fori(0, B // 2 - 1) as i:
                for j in range(2):
                    keep_turned(i * 2 + j + 1, 1 - j)
                    keep_gates(i * 2 + j, j)
            keep_turned(B - 1, 1)
            keep_gates(B - 2, 0)
            keep_gates(B - 1, 1)
            act.wait_ge(abs_ready, 1)
            nc.scalar.activation(exp_f[:], abs_f[:], ACT.Exp, scale=-1.0).then_inc(exp_ready, 1)
            act.wait_ge(exp_ready, 1)
            nc.scalar.activation(ln_f[:], exp_f[:], ACT.Ln, bias=1.0).then_inc(log_ready, 1)
            act.wait_ge(cols_ready, 1)
            nc.scalar.activation(g_col[:].rearrange("p t r -> p (t r)"), col_ps[:, 0:TB * BH],
                                 ACT.Copy).then_inc(cols_out, 1)
            nc.scalar.activation(e_col[:].rearrange("p t r -> p (t r)"), col_ps[:, TB * BH:2 * TB * BH],
                                 ACT.Exp, scale=-1.0).then_inc(cols_out, 1)
            act.wait_ge(cols_out, 2)


def mlstm_attention(nc, a, x, xn_t, cols):
    g_col, e_col, neg_g_row = cols
    W = S + P
    from contextlib import ExitStack
    with ExitStack() as stack:
        mem = Memory(nc, stack, "m1")
        ctx_t = mem.sbuf("ctx_t", [P, 2, S])
        q_t = mem.sbuf("q_t", [P, 2, S])
        v_one = mem.sbuf("v_one", [P, 2, TB, MH, MD + 1])
        causal = mem.sbuf("causal", [P, S])
        ln_scale = mem.sbuf("ln_scale", [P, D])
        ones = mem.sbuf("ones", [3, P], BF16)
        g_now = mem.sbuf("g_now", [P, 2, TB, MH])
        e_now = mem.sbuf("e_now", [P, TB, MH])
        d_arg = mem.sbuf("d_arg", [P, 2, MH, W])
        d_exp = mem.sbuf("d_exp", [P, 2, MH, W])
        c = mem.sbuf("c", [P, 2, MH, W])
        den = mem.sbuf("den", [P, TB * MH, 1])
        h = mem.sbuf("h", [P, TB * MH, MD])
        sq = mem.sbuf("sq", [P, TB * MH, MD])
        mean = mem.sbuf("mean", [P, TB * MH])
        var = mem.sbuf("var", [P, TB * MH])
        rstd = mem.sbuf("rstd", [P, TB * MH])
        power = mem.sbuf("power", [P, TB * MH])
        g_ps = mem.psum("g_ps", [P, MH * S])
        s_ps = mem.psum("s_ps", [P, MH, 512])
        o_ps = mem.psum("o_ps", [P, TB * MH, MD + 1])

        const_in = mem.sem("const_in")
        ones_set = mem.sem("ones_set")
        ctx_in = [mem.sem(f"ctx_in_{j}") for j in range(2)]
        v_in = [mem.sem(f"v_in_{j}") for j in range(2)]
        q_ready = mem.sem("q_ready")
        g_spread = mem.sem("g_spread")
        g_read = mem.sem("g_read")
        d_ready = mem.sem("d_ready")
        scores_ready = mem.sem("scores_ready")
        c_ready = mem.sem("c_ready")
        out_ready = mem.sem("out_ready")
        out_read = mem.sem("out_read")
        var_ready = mem.sem("var_ready")
        rstd_ready = mem.sem("rstd_ready")
        steps_done = mem.sem("steps_done")
        arg_steps = mem.sem("arg_steps")
        block = stack.enter_context(nc.Block())

        def turns(engine, turn):
            turn(0, 0, True, False, True)
            turn(1, 1, True, True, True)
            with engine.Fori(1, B // 2 - 1) as i:
                for j in range(2):
                    turn(i * 2 + j, j, True, True, True)
            turn(B - 2, 0, True, True, True)
            turn(B - 1, 1, True, True, False)
            turn(B, 0, False, True, False)

        @block.sync
        def _(sync):
            sync.dma_start(causal[:], a["causal"]).then_inc(const_in, 16)
            sync.dma_start(ln_scale[:], a["ln_scale"]).then_inc(const_in, 16)
            sync.wait_ge(ones_set, 2)

            def load(b, j):
                if not isinstance(b, int) or b >= 2:
                    sync.wait_ge(scores_ready, b - 1)
                sync.dma_start(ctx_t[:, j, :], a["ctx_t"][:, bass.ds(b, 1), :]).then_inc(ctx_in[j], 16)
                sync.wait_ge(out_ready, b + 1)
                for t in range(TB):
                    sync.dma_start(v_one[:, j, t, :, 0:MD],
                                   a["ctx_n"][:, bass.ds(b * TB + t, 1), :].rearrange("p t (h d) -> p (t h) d", d=MD)).then_inc(v_in[j], 16)

            load(0, 0)
            load(1, 1)
            with sync.Fori(1, B // 2) as i:
                for j in range(2):
                    load(i * 2 + j, j)

        @block.gpsimd
        def _(pool):
            nc.gpsimd.memset(power[:], -0.5).then_inc(rstd_ready, 1)

            def queries(b, j):
                if not isinstance(b, int) or b >= 2:
                    pool.wait_ge(scores_ready, b - 1)
                    apart(pool)
                nc.gpsimd.tensor_copy(q_t[:, j, :], xn_t[:, bass.ds(b * S, S)]).then_inc(q_ready, 1)

            def turn(b, j, now, before, ahead):
                if ahead:
                    queries(b + 1, 1 - j)
                if before:
                    pool.wait_ge(var_ready, b)
                    pool.wait_ge(rstd_ready, b)
                    nc.gpsimd.tensor_tensor(rstd[:], var[:], power[:], ALU.pow).then_inc(rstd_ready, 1)

            queries(0, 0)
            turns(pool, turn)

        @block.vector
        def _(dve):
            nc.vector.memset(v_one[:], 1.0).then_inc(ones_set, 1)
            nc.vector.memset(ones[:], 1.0).then_inc(ones_set, 1)
            dve.wait_ge(const_in, 32)
            nc.vector.tensor_scalar(out=ln_scale[:], in0=ln_scale[:], scalar1=1.0, scalar2=None,
                                    op0=ALU.add).then_inc(ones_set, 1)
            dve.wait_ge(ones_set, 3)
            dve.sem_inc(g_read, 1)
            dve.sem_inc(c_ready, 1)
            dve.sem_inc(out_read, 1)

            def arguments(b, j):
                steps = Steps(dve, arg_steps, b, 2 * MH)
                steps.link(nc.vector.tensor_copy(g_now[:, j], g_col[:].rearrange("p t (h b) -> p t h b", b=B)[:, :, :, bass.ds(b, 1)]))
                dve.wait_ge(g_spread, b + 1)
                for n in range(MH):
                    steps.step(nc.vector.scalar_tensor_tensor(
                        out=d_arg[:, j, n, 0:S], in0=g_ps[:, n * S:(n + 1) * S],
                        scalar=g_now[:, j, 0, n:n + 1], in1=causal[:], op0=ALU.add, op1=ALU.min))
                    later = nc.vector.scalar_tensor_tensor(
                        out=d_arg[:, j, n, S:W], in0=g_ps[:, n * S + P:(n + 1) * S],
                        scalar=g_now[:, j, 1, n:n + 1], in1=causal[:, 0:P], op0=ALU.add, op1=ALU.min)
                    if n < MH - 1:
                        steps.step(later)
                later.then_inc(g_read, 1)
                steps.close()

            def output(b, meanwhile):
                steps = Steps(dve, steps_done, b, 13)
                steps.link(nc.vector.tensor_copy(e_now[:], e_col[:].rearrange("p t (h b) -> p t h b", b=B)[:, :, :, bass.ds(b, 1)]))
                dve.wait_ge(out_ready, b + 3)
                steps.link(nc.vector.scalar_tensor_tensor(
                    out=den[:, :, 0], in0=o_ps[:, :, MD], scalar=-1.0,
                    in1=e_now[:].rearrange("p t h -> p (t h)"), op0=ALU.mult, op1=ALU.max))
                steps.link(nc.vector.tensor_tensor(den[:, :, 0], o_ps[:, :, MD], den[:, :, 0], ALU.max))
                steps.link(nc.vector.tensor_scalar(out=den[:], in0=den[:], scalar1=1e-6, scalar2=None, op0=ALU.add))
                steps.link(nc.vector.reciprocal(den[:], den[:]))
                nc.vector.tensor_tensor(h[:], o_ps[:, :, 0:MD], den[:].to_broadcast([P, TB * MH, MD]),
                                        ALU.mult).then_inc(out_read, 1)
                dve.wait_ge(out_read, b + 2)
                steps.link(nc.vector.tensor_reduce(mean[:], h[:], AX.X, ALU.add))
                steps.link(nc.vector.tensor_scalar(out=mean[:], in0=mean[:], scalar1=1.0 / MD, scalar2=None, op0=ALU.mult))
                steps.link(nc.vector.tensor_tensor(h[:], h[:], mean[:].unsqueeze(2).to_broadcast([P, TB * MH, MD]), ALU.subtract))
                steps.link(nc.vector.tensor_tensor(sq[:], h[:], h[:], ALU.mult))
                steps.link(nc.vector.tensor_reduce(var[:], sq[:], AX.X, ALU.add))
                nc.vector.tensor_scalar(out=var[:], in0=var[:], scalar1=1.0 / MD, scalar2=LN_EPS,
                                        op0=ALU.mult, op1=ALU.add).then_inc(var_ready, 1)
                meanwhile()
                dve.wait_ge(rstd_ready, b + 2)
                steps.link(nc.vector.tensor_tensor(h[:], h[:], rstd[:].unsqueeze(2).to_broadcast([P, TB * MH, MD]), ALU.mult))
                flat = h[:].rearrange("p (t h) d -> p t (h d)", t=TB)
                steps.link(nc.vector.tensor_tensor(flat, flat, ln_scale[:].unsqueeze(1).to_broadcast([P, TB, D]), ALU.mult))
                steps.link(nc.vector.tensor_tensor(x[:, bass.ds(b * TB, TB), :], x[:, bass.ds(b * TB, TB), :], flat, ALU.add))
                steps.close()

            def turn(b, j, now, before, ahead):
                if now and not before:
                    arguments(b, j)
                if now:
                    dve.wait_ge(scores_ready, b + 1)
                    dve.wait_ge(d_ready, b + 1)
                    nc.vector.scalar_tensor_tensor(out=c[:, j], in0=s_ps[:, :, 0:W], scalar=MSCALE, in1=d_exp[:, j],
                                                   op0=ALU.mult, op1=ALU.mult).then_inc(c_ready, 1)
                if now and not before:
                    arguments(b + 1, 1 - j)
                if before:
                    output(b - 1, lambda: arguments(b + 1, 1 - j) if ahead else None)

            turns(dve, turn)

        @block.tensor
        def _(pe):
            pe.wait_ge(ones_set, 3)
            pe.sem_inc(out_ready, 2)

            def spread(b):
                pe.wait_ge(g_read, b + 1)
                for n in range(MH):
                    last = nc.tensor.matmul(g_ps[:, n * S:(n + 1) * S], ones[:],
                                            neg_g_row[0:3, bass.ds(b * S + n * (B * S), S)],
                                            start=True, stop=True)
                last.then_inc(g_spread, 1)

            def turn(b, j, now, before, ahead):
                if now:
                    half = b // 2 if isinstance(b, int) else (b - j) // 2
                    pe.wait_ge(ctx_in[j], half * 16 + 16)
                    pe.wait_ge(q_ready, b + 1)
                    pe.wait_ge(c_ready, b + 1)
                    for n in range(MH):
                        rows = slice(n * MD, (n + 1) * MD)
                        nc.tensor.matmul(s_ps[:, n, 0:S], ctx_t[rows, j, 0:P], q_t[rows, j, :], start=True, stop=True)
                        last = nc.tensor.matmul(s_ps[:, n, S:W], ctx_t[rows, j, P:S], q_t[rows, j, P:S],
                                                start=True, stop=True)
                    last.then_inc(scores_ready, 1)
                if ahead:
                    spread(b + 1)
                if before:
                    half = b // 2 if isinstance(b, int) else (b - j) // 2
                    pe.wait_ge(v_in[1 - j], (half + j) * 32)
                    pe.wait_ge(c_ready, b + 1)
                    pe.wait_ge(out_read, b)
                    for n in range(MH):
                        nc.tensor.matmul(o_ps[:, n, :], c[:, 1 - j, n, 0:P], v_one[:, 1 - j, 0, n, :], start=True, stop=True)
                        nc.tensor.matmul(o_ps[:, MH + n, :], c[:, 1 - j, n, P:S], v_one[:, 1 - j, 0, n, :], start=True, stop=False)
                        last = nc.tensor.matmul(o_ps[:, MH + n, :], c[:, 1 - j, n, S:W], v_one[:, 1 - j, 1, n, :],
                                                start=False, stop=True)
                    last.then_inc(out_ready, 1)

            spread(0)
            turns(pe, turn)

        @block.scalar
        def _(act):
            with act.Fori(0, B // 2) as i:
                for j in range(2):
                    b = i * 2 + j
                    act.wait_ge(g_read, b + 2)
                    nc.scalar.activation(d_exp[:, j].rearrange("p h w -> p (h w)"),
                                         d_arg[:, j].rearrange("p h w -> p (h w)"), ACT.Exp).then_inc(d_ready, 1)



E = 8


AHEAD = 4


class Mixture:

    def __init__(self, name, k, h, gated, bias):
        self.name, self.k, self.h, self.gated, self.bias = name, k, h, gated, bias
        self.wide = 2 * h if gated else h
        tiles = k * NT + E - 1
        self.tiles = -(-tiles // AHEAD) * AHEAD
        self.second_bias = name == "f0"
        self.top_probability = name == "f1"


MIX0 = Mixture("f0", 1, 512, False, True)
MIX1 = Mixture("f1", 1, 512, True, False)
MIX3 = Mixture("f3", 2, 256, True, True)
MOST_SLOTS = MIX3.tiles * P


def mixture_route(nc, a, x, ident, mix, hold, slots_x):
    from contextlib import ExitStack
    K = mix.k
    with ExitStack() as stack:
        mem = Memory(nc, stack, mix.name + "r")
        stats = mem.sbuf("ln_stats", [P, NT, 6])
        mean_var = mem.sbuf("ln_mean_var", [P, NT, 2])
        var_eps = mem.sbuf("ln_var_eps", [P, NT])
        rstd = mem.sbuf("ln_rstd", [P, NT])
        power = mem.sbuf("ln_power", [P, NT])
        xn = mem.sbuf("xn", [P, NT, D])
        xn_now = mem.sbuf("xn_now", [P, 2, TB, D])
        xn_t = mem.sbuf("xn_t", [P, 2, S])
        router = mem.sbuf("router", [P, E])
        router_b = mem.sbuf("router_b", [P, 2, E])
        before = mem.sbuf("before", [P, P])
        ones = mem.sbuf("ones", [P, P])
        iota_e = mem.sbuf("iota_e", [P, E])
        iota_s = mem.sbuf("iota_s", [P, mix.tiles])
        keep = mem.sbuf("keep", [P, E, NT])
        tile_starts = mem.sbuf("tile_starts", [P, NT])
        logits = mem.sbuf("logits", [P, NT, E])
        top = mem.sbuf("top", [P, NT, E])
        top_at = mem.sbuf("top_at", [P, NT, E], U32)
        at = mem.sbuf("at", [P, K, NT])
        chosen = mem.sbuf("chosen", [P, K, NT, E])
        both = mem.sbuf("both", [P, NT, E])
        count = mem.sbuf("count", [P, E, NT])
        cum = mem.sbuf("cum", [P, E, NT])
        over = mem.sbuf("over", [P, E, NT])
        n_tiles = mem.sbuf("n_tiles", [P, E])
        ends = mem.sbuf("ends", [P, E])
        base = mem.sbuf("base", [P, E])
        offset = mem.sbuf("offset", [P, E, NT])
        place = mem.sbuf("place", [P, NT, E])
        picked = mem.sbuf("picked", [P, K, NT, E])
        slot = mem.sbuf("slot", [P, K, NT])
        past = mem.sbuf("past", [P, mix.tiles, E])
        expert = mem.sbuf("expert", [P, mix.tiles])
        gap = mem.sbuf("gap", [P, NT, E])
        exp_gap = mem.sbuf("exp_gap", [P, NT, E])
        total = mem.sbuf("total", [P, NT])
        t_ps = mem.psum("t_ps", [P, 2, 512])
        l_ps = mem.psum("l_ps", [P, 2, 512])
        c_ps = mem.psum("c_ps", [P, 2, 512])

        const_in = mem.sem("const_in")
        moments_ready = mem.sem("moments_ready")
        rstd_ready = mem.sem("rstd_ready")
        norm_ready = mem.sem("norm_ready")
        xn_ready = mem.sem("xn_ready")
        transposed = mem.sem("transposed")
        xn_t_ready = mem.sem("xn_t_ready")
        logits_done = mem.sem("logits_done")
        logits_ready = mem.sem("logits_ready")
        steps_done = mem.sem("steps_done")
        bias_steps = mem.sem("bias_steps")
        norm_steps = mem.sem("norm_steps")
        route_steps = mem.sem("route_steps")
        both_ready = mem.sem("both_ready")
        counted = mem.sem("counted")
        slots_ready = mem.sem("slots_ready")
        gap_ready = mem.sem("gap_ready")
        exp_ready = mem.sem("exp_ready")
        block = stack.enter_context(nc.Block())

        @block.sync
        def _(sync):
            for t, n in ((router, mix.name + "_router"), (router_b, mix.name + "_router_b"), (before, "before"),
                         (iota_e, "iota_e"), (iota_s, mix.name + "_iota_s"), (keep, "keep"), (tile_starts, "tile_starts")):
                sync.dma_start(t[:], a[n]).then_inc(const_in, 16)

        @block.gpsimd
        def _(pool):
            nc.gpsimd.memset(power[:], -0.5).then_inc(rstd_ready, 1)
            pool.wait_ge(moments_ready, NT)
            nc.gpsimd.tensor_scalar(out=var_eps[:], in0=mean_var[:, :, 1], scalar1=LN_EPS, scalar2=None,
                                    op0=ALU.add).then_inc(rstd_ready, 1)
            pool.wait_ge(rstd_ready, 2)
            nc.gpsimd.tensor_tensor(rstd[:], var_eps[:], power[:], ALU.pow).then_inc(rstd_ready, 1)
            pool.wait_ge(slots_ready, 1)
            pool.wait_ge(xn_ready, B + 2)
            pool.wait_ge(Memory.zeroed, 16)
            for k in range(K):
                for t in range(NT):
                    nc.gpsimd.indirect_dma_start(
                        out=slots_x[:, :], out_offset=bass.IndirectOffsetOnAxis(ap=hold.slot[:, k, t:t + 1], axis=0),
                        in_=xn[:, t, :], in_offset=None).then_inc(Memory.scattered, 16)
            pool.wait_ge(Memory.scattered, (Memory.rounds + K) * NT * 16)

        @block.tensor
        def _(pe):
            pe.wait_ge(const_in, 7 * 16)
            pe.sem_inc(transposed, 2)
            pe.sem_inc(logits_done, 2)

            def turn_x(b, j):
                pe.wait_ge(norm_ready, b + 1)
                pe.wait_ge(xn_t_ready, b + 1)
                for t in range(TB):
                    last = nc.tensor.transpose(t_ps[:, j, t * P:(t + 1) * P], xn_now[:, j, t, :], ident[:])
                last.then_inc(transposed, 1)

            def logits_of(b, j):
                pe.wait_ge(logits_ready, b + 1)
                pe.wait_ge(xn_t_ready, b + 3)
                for t in range(TB):
                    last = nc.tensor.matmul(l_ps[:, j, t * E:(t + 1) * E], xn_t[:, j, t * P:(t + 1) * P], router[:],
                                            start=True, stop=True)
                last.then_inc(logits_done, 1)

            with pe.Fori(0, B // 2) as i:
                for j in range(2):
                    turn_x(i * 2 + j, j)
                    logits_of(i * 2 + j, j)
            pe.wait_ge(both_ready, 1)
            nc.tensor.matmul(c_ps[:, 0, 0:NT * E], before[:], both[:].rearrange("p t e -> p (t e)"), start=True, stop=True)
            nc.tensor.matmul(c_ps[:, 1, 0:NT * E], ones[:], both[:].rearrange("p t e -> p (t e)"),
                             start=True, stop=True).then_inc(counted, 1)

        @block.scalar
        def _(act):
            act.sem_inc(xn_t_ready, 2)
            act.sem_inc(xn_ready, 2)
            with act.Fori(0, B // 2) as i:
                for j in range(2):
                    b = i * 2 + j
                    act.wait_ge(norm_ready, b + 1)
                    nc.scalar.activation(xn[:, bass.ds(b * TB, TB), :], xn_now[:, j], ACT.Copy).then_inc(xn_ready, 1)
                    act.wait_ge(transposed, b + 3)
                    act.wait_ge(logits_done, b + 1)
                    nc.scalar.activation(xn_t[:, j, :], t_ps[:, j, 0:S], ACT.Copy).then_inc(xn_t_ready, 1)
            if K == 2 or mix.top_probability:
                act.wait_ge(gap_ready, 1)
                nc.scalar.activation(exp_gap[:], gap[:], ACT.Exp).then_inc(exp_ready, 1)

        @block.vector
        def _(dve):
            nc.vector.memset(ones[:], 1.0).then_inc(route_steps, 1)
            dve.sem_inc(logits_ready, 2)

            def logits_of(b, j):
                dve.wait_ge(logits_done, b + 3)
                add = nc.vector.tensor_tensor(logits[:, bass.ds(b * TB, TB), :],
                                              l_ps[:, j, 0:TB * E].rearrange("p (t e) -> p t e", e=E),
                                              router_b[:, 0:1, :].to_broadcast([P, TB, E]), ALU.add)
                if mix.second_bias:
                    second = Steps(dve, bias_steps, b, 1)
                    second.link(add)
                    add = nc.vector.tensor_tensor(logits[:, bass.ds(b * TB, TB), :], logits[:, bass.ds(b * TB, TB), :],
                                                  router_b[:, 1:2, :].to_broadcast([P, TB, E]), ALU.add)
                add.then_inc(logits_ready, 1)

            for t in range(NT):
                nc.vector.bn_stats(stats[:, t, :], x[:, t, :]).then_inc(steps_done, 1)
            dve.wait_ge(steps_done, NT)
            for t in range(NT):
                nc.vector.bn_aggr(mean_var[:, t, :], stats[:, t, :]).then_inc(moments_ready, 1)
            dve.wait_ge(moments_ready, NT)
            dve.wait_ge(const_in, 7 * 16)
            dve.wait_ge(rstd_ready, 3)

            def turn(b, j, before):
                dve.wait_ge(transposed, b + 1)
                dve.wait_ge(xn_ready, b + 1)
                norm = Steps(dve, norm_steps, b, 1)
                norm.link(nc.vector.tensor_tensor(xn_now[:, j], x[:, bass.ds(b * TB, TB), :],
                                                  mean_var[:, bass.ds(b * TB, TB), 0:1].to_broadcast([P, TB, D]), ALU.subtract))
                nc.vector.tensor_tensor(xn_now[:, j], xn_now[:, j],
                                        rstd[:, bass.ds(b * TB, TB)].unsqueeze(2).to_broadcast([P, TB, D]),
                                        ALU.mult).then_inc(norm_ready, 1)
                if before:
                    logits_of(b - 1, 1 - j)

            turn(0, 0, False)
            turn(1, 1, True)
            with dve.Fori(1, B // 2) as i:
                for j in range(2):
                    turn(i * 2 + j, j, True)
            logits_of(B - 1, 1)
            dve.wait_ge(logits_ready, B + 2)
            r = Steps(dve, route_steps)
            r.n = 1
            for t in range(NT):
                r.step(nc.vector.max(top[:, t, :], logits[:, t, :]))
            r.settle()
            for t in range(NT):
                r.step(nc.vector.max_index(top_at[:, t, :], top[:, t, :], logits[:, t, :]))
            r.settle()
            wide = [P, NT, E]
            for k in range(K):
                r.link(nc.vector.tensor_copy(at[:, k, :], top_at[:, :, k]))
                r.link(nc.vector.tensor_tensor(chosen[:, k], iota_e[:].unsqueeze(1).to_broadcast(wide),
                                               at[:, k, :].unsqueeze(2).to_broadcast(wide), ALU.is_equal))
            if K == 2:
                nc.vector.tensor_tensor(both[:], chosen[:, 0], chosen[:, 1], ALU.add).then_inc(both_ready, 1)
            else:
                nc.vector.tensor_copy(both[:], chosen[:, 0]).then_inc(both_ready, 1)
            if mix.top_probability:
                nc.vector.tensor_tensor(gap[:], logits[:], top[:, :, 0:1].to_broadcast(wide),
                                        ALU.subtract).then_inc(gap_ready, 1)
                dve.wait_ge(exp_ready, 1)
                r.link(nc.vector.tensor_reduce(total[:], exp_gap[:], AX.X, ALU.add))
                r.link(nc.vector.reciprocal(hold.score[:, 0, :], total[:]))
            if K == 2:
                nc.vector.tensor_tensor(gap[:], top[:], top[:, :, 0:1].to_broadcast(wide),
                                        ALU.subtract).then_inc(gap_ready, 1)
                dve.wait_ge(exp_ready, 1)
                r.link(nc.vector.tensor_tensor(total[:], exp_gap[:, :, 0], exp_gap[:, :, 1], ALU.add))
                r.link(nc.vector.reciprocal(total[:], total[:]))
                for k in range(K):
                    r.link(nc.vector.tensor_tensor(hold.score[:, k, :], exp_gap[:, :, k], total[:], ALU.mult))
            dve.wait_ge(counted, 1)
            r.link(nc.vector.tensor_copy(count[:], c_ps[:, 1, 0:NT * E].rearrange("p (t e) -> p e t", e=E)))
            r.link(nc.vector.tensor_tensor_scan(cum[:].rearrange("p e t -> p (e t)"), keep[:].rearrange("p e t -> p (e t)"),
                                                count[:].rearrange("p e t -> p (e t)"), 0.0, ALU.mult, ALU.add))
            by_e = [P, E, NT]
            r.link(nc.vector.tensor_tensor(over[:], cum[:, :, NT - 1:NT].to_broadcast(by_e),
                                           tile_starts[:].unsqueeze(1).to_broadcast(by_e), ALU.is_gt))
            r.link(nc.vector.tensor_reduce(n_tiles[:], over[:], AX.X, ALU.add))
            r.link(nc.vector.tensor_tensor_scan(ends[:], ones[:, 0:E], n_tiles[:], 0.0, ALU.mult, ALU.add))
            r.link(nc.vector.tensor_tensor(base[:], ends[:], n_tiles[:], ALU.subtract))
            r.link(nc.vector.tensor_tensor(offset[:], cum[:], count[:], ALU.subtract))
            r.link(nc.vector.scalar_tensor_tensor(out=offset[:], in0=base[:].unsqueeze(2).to_broadcast(by_e), scalar=float(P),
                                                  in1=offset[:], op0=ALU.mult, op1=ALU.add))
            r.link(nc.vector.tensor_tensor(place[:], c_ps[:, 0, 0:NT * E].rearrange("p (t e) -> p t e", e=E),
                                           offset[:].rearrange("p e t -> p t e"), ALU.add))
            for k in range(K):
                r.link(nc.vector.tensor_tensor(picked[:, k], chosen[:, k], place[:], ALU.mult))
                r.link(nc.vector.tensor_reduce(slot[:, k, :], picked[:, k], AX.X, ALU.add))
            nc.vector.tensor_copy(hold.slot, slot[:]).then_inc(slots_ready, 1)
            by_s = [P, mix.tiles, E]
            r.link(nc.vector.tensor_tensor(past[:], iota_s[:].unsqueeze(2).to_broadcast(by_s),
                                           ends[:].unsqueeze(1).to_broadcast(by_s), ALU.is_ge))
            r.link(nc.vector.tensor_reduce(expert[:], past[:], AX.X, ALU.add))
            r.link(nc.vector.tensor_scalar(out=hold.expert[:], in0=expert[:], scalar1=float(E - 1), scalar2=None, op0=ALU.min))


def mixture_experts(nc, a, ident, mix, hold, slots_x, slots_y):
    from contextlib import ExitStack
    H, W, NS, HC = mix.h, mix.wide, mix.tiles, mix.h // P
    with ExitStack() as stack:
        mem = Memory(nc, stack, mix.name + "e")
        xs = mem.sbuf("xs", [P, AHEAD, D])
        xs_t = mem.sbuf("xs_t", [P, 2, P])
        wide = mem.sbuf("wide", [P, 2, W])
        gate = mem.sbuf("gate", [P, 2, H])
        hidden = mem.sbuf("hidden", [P, 2, H])
        hidden_t = mem.sbuf("hidden_t", [P, 2, HC, P])
        ys = mem.sbuf("ys", [P, 2, D])
        xt_ps = mem.psum("xt_ps", [P, 512])
        h_ps = mem.psum("h_ps", [P, 2, max(W, 512)])
        ht_ps = mem.psum("ht_ps", [P, 512])
        y_ps = mem.psum("y_ps", [P, 512])

        row_in = [mem.sem(f"row_in_{j}") for j in range(AHEAD)]
        row_out = [mem.sem(f"row_out_{j}") for j in range(2)]
        xt_done = mem.sem("xt_done")
        xt_ready = mem.sem("xt_ready")
        h_done = mem.sem("h_done")
        wide_ready = mem.sem("wide_ready")
        gate_ready = mem.sem("gate_ready")
        hidden_ready = mem.sem("hidden_ready")
        ht_done = mem.sem("ht_done")
        ht_ready = mem.sem("ht_ready")
        y_done = mem.sem("y_done")
        y_ready = mem.sem("y_ready")
        block = stack.enter_context(nc.Block())

        def half(t, j):
            return t // 2 if isinstance(t, int) else (t - j) // 2

        def turns(engine, turn, lag, step=2):
            for t in range(step):
                turn(t, t % step, "ends")
            with engine.Fori(1, NS // step - 1) as i:
                for j in range(step):
                    turn(i * step + j, j, "middle")
            for t in range(NS - step, NS + lag):
                turn(t, t % step, "ends")

        def of(t, lag, where):
            return where == "middle" or 0 <= t - lag < NS

        @block.sync
        def _(sync):
            def load(s, b):
                if not isinstance(s, int) or s >= AHEAD:
                    sync.wait_ge(xt_done, s - AHEAD + 3)
                sync.dma_start(xs[:, b, :], slots_x[bass.ds(s * P, P), :]).then_inc(row_in[b], 16)

            def turn(t, j, where):
                if of(t, 1 - AHEAD, where):
                    load(t + AHEAD - 1, (j + AHEAD - 1) % AHEAD)
                if of(t, 4, where):
                    s, b = t - 4, j % 2
                    sync.wait_ge(y_ready, s + 2)
                    sync.dma_start(slots_y[bass.ds(s * P, P), :], ys[:, b, :]).then_inc(row_out[b], 16)

            for j in range(2):
                sync.sem_inc(row_out[j], 16 + j * 16)
            for s in range(AHEAD - 1):
                load(s, s)
            turns(sync, turn, 4, AHEAD)
            for j in range(2):
                sync.wait_ge(row_out[j], NS // 2 * 16 + 16 + j * 16)

        @block.tensor
        def _(pe):
            pe.wait_ge(hold.loaded, len(hold.loads) * 16)
            pe.sem_inc(xt_done, 2)
            pe.sem_inc(h_done, 2)
            pe.sem_inc(y_done, 2)

            def turn_rows(s, b):
                generation = s // AHEAD if isinstance(s, int) else (s - b) // AHEAD
                pe.wait_ge(row_in[b], generation * 16 + 16)
                pe.wait_ge(xt_ready, s + 1)
                nc.tensor.transpose(xt_ps[:, 0:P], xs[:, b, :], ident[:]).then_inc(xt_done, 1)

            def turn(t, b, where):
                j = b % 2
                if of(t, 0, where):
                    e = pe.value_load(hold.expert[0:1, bass.ds(t, 1)], min_val=0, max_val=E - 1)
                    pe.wait_ge(xt_ready, t + 2)
                    pe.wait_ge(hidden_ready, t + 1)
                    for c in range(0, W, 512):
                        last = nc.tensor.matmul(h_ps[:, j, c:c + 512], xs_t[:, j, :], hold.w1[:, bass.ds(e * W + c, 512)],
                                                start=True, stop=True)
                    last.then_inc(h_done, 1)
                if of(t, -1, where):
                    turn_rows(t + 1, (b + 1) % AHEAD)
                if of(t, 2, where):
                    pe.wait_ge(hidden_ready, t + 1)
                    pe.wait_ge(ht_ready, t - 1)
                    for c in range(HC):
                        last = nc.tensor.transpose(ht_ps[:, c * P:(c + 1) * P], hidden[:, j, c * P:(c + 1) * P], ident[:])
                    last.then_inc(ht_done, 1)
                if of(t, 3, where):
                    e = pe.value_load(hold.expert[0:1, bass.ds(t - 3, 1)], min_val=0, max_val=E - 1)
                    pe.wait_ge(ht_ready, t - 1)
                    pe.wait_ge(y_ready, t - 2)
                    for c in range(HC):
                        last = nc.tensor.matmul(y_ps[:, 0:D], hidden_t[:, 1 - j, c, :], hold.w2[:, bass.ds(e * (HC * D) + c * D, D)],
                                                start=c == 0, stop=c == HC - 1)
                    last.then_inc(y_done, 1)

            turn_rows(0, 0)
            turns(pe, turn, 3, AHEAD)

        @block.scalar
        def _(act):
            act.sem_inc(xt_ready, 1)
            act.sem_inc(ht_ready, 1)

            def keep_turned(s, j):
                act.wait_ge(xt_done, s + 3)
                act.wait_ge(h_done, s + 1)
                nc.scalar.activation(xs_t[:, j, :], xt_ps[:, 0:P], ACT.Copy).then_inc(xt_ready, 1)

            def turn(t, j, where):
                if of(t, -1, where):
                    keep_turned(t + 1, 1 - j)
                if of(t, 2, where):
                    act.wait_ge(ht_done, t - 1)
                    act.wait_ge(y_done, t - 1)
                    nc.scalar.activation(hidden_t[:, j].rearrange("p c t -> p (c t)"), ht_ps[:, 0:H],
                                         ACT.Copy if mix.gated else ACT.Relu).then_inc(ht_ready, 1)
                if of(t, 0, where) and mix.gated:
                    if mix.bias:
                        act.wait_ge(wide_ready, t + 1)
                    else:
                        act.wait_ge(h_done, t + 3)
                    act.wait_ge(hidden_ready, t + 1)
                    nc.scalar.activation(gate[:, j, :], (wide if mix.bias else h_ps)[:, j, 0:H], ACT.Silu).then_inc(gate_ready, 1)

            keep_turned(0, 0)
            turns(act, turn, 2)

        @block.vector
        def _(dve):
            dve.wait_ge(hold.loaded, len(hold.loads) * 16)
            dve.sem_inc(hidden_ready, 2)
            dve.sem_inc(y_ready, 1)

            def hidden_free(t):
                if not isinstance(t, int) or t >= 2:
                    dve.wait_ge(ht_done, t - 1)

            def turn(t, b, where):
                j = b % 2
                if of(t, 0, where):
                    if mix.bias:
                        e = dve.value_load(hold.expert[0:1, bass.ds(t, 1)], min_val=0, max_val=E - 1)
                    dve.wait_ge(h_done, t + 3)
                    if not mix.gated:
                        hidden_free(t)
                        nc.vector.tensor_tensor(hidden[:, j, :], h_ps[:, j, 0:W], hold.b1[:, bass.ds(e * W, W)],
                                                ALU.add).then_inc(hidden_ready, 1)
                    elif mix.bias:
                        nc.vector.tensor_tensor(wide[:, j, :], h_ps[:, j, 0:W], hold.b1[:, bass.ds(e * W, W)],
                                                ALU.add).then_inc(wide_ready, 1)
                if of(t, 3, where):
                    if mix.bias:
                        e = dve.value_load(hold.expert[0:1, bass.ds(t - 3, 1)], min_val=0, max_val=E - 1)
                    dve.wait_ge(y_done, t)
                    dve.wait_ge(row_out[1 - j], half(t, j) * 16)
                    if mix.bias:
                        nc.vector.tensor_tensor(ys[:, 1 - j, :], y_ps[:, 0:D], hold.b2[:, bass.ds(e * D, D)], ALU.add).then_inc(y_ready, 1)
                    else:
                        nc.vector.tensor_copy(ys[:, 1 - j, :], y_ps[:, 0:D]).then_inc(y_ready, 1)
                if of(t, 0, where) and mix.gated:
                    dve.wait_ge(gate_ready, t + 1)
                    hidden_free(t)
                    nc.vector.tensor_tensor(hidden[:, j, :], gate[:, j, :], (wide if mix.bias else h_ps)[:, j, H:W],
                                            ALU.mult).then_inc(hidden_ready, 1)

            turns(dve, turn, 3, AHEAD)


class Arriving:

    def __init__(self, nc, mem, mix, hold, slots_y):
        self.nc, self.mix, self.hold, self.slots_y, self.rounds = nc, mix, hold, slots_y, Memory.rounds
        self.back = mem.sbuf("back", [P, mix.k, NT, D])
        self.arrived = mem.sem("arrived")
        self.steps = mem.sem("arriving_steps")
        Memory.rounds += mix.k

    def gather(self, b):
        for t in range(b * TB, (b + 1) * TB):
            for k in range(self.mix.k):
                self.nc.gpsimd.indirect_dma_start(
                    out=self.back[:, k, t, :], out_offset=None, in_=self.slots_y[0:self.mix.tiles * P, :],
                    in_offset=bass.IndirectOffsetOnAxis(ap=self.hold.slot[:, k, t:t + 1], axis=0)
                ).then_inc(Memory.gathered[t], 16)

    def arrive(self, pool, b):
        if b == 0:
            self.gather(0)
            self.gather(1)
        if b + 2 < B:
            self.gather(b + 2)
        for t in range(b * TB, (b + 1) * TB):
            pool.wait_ge(Memory.gathered[t], (self.rounds + self.mix.k) * 16)
        pool.sem_inc(self.arrived, 1)

    def add(self, dve, x, b):
        dve.wait_ge(self.arrived, b + 1)
        adds = Steps(dve, self.steps, b, self.mix.k * (1 if self.mix.name == "f0" else 2))
        xb = x[:, bass.ds(b * TB, TB), :]
        for k in range(self.mix.k):
            rows = self.back[:, k, bass.ds(b * TB, TB), :]
            if self.mix.name != "f0":
                score = self.hold.score[:, k, bass.ds(b * TB, TB)].unsqueeze(2).to_broadcast([P, TB, D])
                adds.link(self.nc.vector.tensor_tensor(rows, rows, score, ALU.mult))
            adds.link(self.nc.vector.tensor_tensor(xb, xb, rows, ALU.add))
        adds.close()
        apart(dve)


def mixture_output(nc, x, out, arriving, stored):
    with nc.Block() as block:
        @block.gpsimd
        def _(pool):
            for b in range(B):
                arriving.arrive(pool, b)

        @block.vector
        def _(dve):
            for b in range(B):
                arriving.add(dve, x, b)

        @block.sync
        def _(sync):
            for b in range(B):
                sync.wait_ge(arriving.steps, (b + 1) * arriving.mix.k * 2)
                sync.dma_start(out[:, b * TB:(b + 1) * TB, :], x[:, b * TB:(b + 1) * TB, :]).then_inc(stored, 16)
            sync.wait_ge(stored, B * 16)


def mixture_weights(nc, a, mix, stack, slot, score):
    hold = Memory(nc, stack, mix.name)
    hold.slot = slot[:, 0:mix.k, :]
    hold.score = score[:, 0:mix.k, :]
    hold.w1 = hold.sbuf("w1", [P, E * mix.wide])
    hold.w2 = hold.sbuf("w2", [P, E * mix.h])
    hold.loaded = Memory.loaded[mix.name]
    hold.loads = [(hold.w1[:], a[mix.name + "_w1"]), (hold.w2[:], a[mix.name + "_w2"])]
    if mix.bias:
        hold.b1 = hold.sbuf("b1", [P, E * mix.wide])
        hold.b2 = hold.sbuf("b2", [P, E * D])
        hold.loads += [(hold.b1[:], a[mix.name + "_b1"].to_broadcast([P, E * mix.wide])),
                       (hold.b2[:], a[mix.name + "_b2"].to_broadcast([P, E * D]))]

    def start(engine):
        for t, n in hold.loads:
            engine.dma_start(t, n).then_inc(hold.loaded, 16)

    hold.start_loads = start
    return hold


def mixture_layer(nc, a, x, ident, mix, hold, slots_x, slots_y):
    from contextlib import ExitStack
    with ExitStack() as stack:
        mem = Memory(nc, stack, mix.name + "h")
        hold.expert = mem.sbuf("expert", [P, mix.tiles], I32)
        mixture_route(nc, a, x, ident, mix, hold, slots_x)
        mixture_experts(nc, a, ident, mix, hold, slots_x, slots_y)



HN = 16
HD = D // HN
SLOT = 32
HG = 4
G = HN // HG
MAX_ROW = 3 * HD
MASKED = -2.0 ** 100
UNITS = HN
LAG = 4
STEPS = UNITS + LAG


class Heads:
    def __init__(self, name, scale, masked, biased, jobs):
        self.name, self.scale, self.masked, self.biased, self.jobs = name, scale, masked, biased, jobs


HEADS1 = Heads("h1", HD ** -0.5, True, False, {
    "x": 4, "turn sums": 3, "turn normalised": 6, "project": [8, 12, 13, 16], "output": 8, "values": 17, "sums": [10, 14, 19]})
HEADS2 = Heads("h2", 1.0, False, True, {
    "x": 4, "turn sums": 3, "turn normalised": 6, "project": [7, 12, 14, 16], "output": 8, "values": 18, "sums": [10, 16, 17]})


def heads_layer(nc, a, x, ident, hw, mix, hold, slots_y, later_loads=None):
    from contextlib import ExitStack
    jobs = hw.jobs
    with ExitStack() as stack:
        mem = Memory(nc, stack, hw.name)
        nb = NormBuffers(mem)
        arriving = Arriving(nc, mem, mix, hold, slots_y)
        w_qk = mem.sbuf("w_qk", [P, 2, G, P])
        w_v = mem.sbuf("w_v", [P, D])
        w_o = mem.sbuf("w_o", [P, D])
        b_v = mem.sbuf("b_v", [P, D])
        b_o = mem.sbuf("b_o", [P, D])
        b_qk = mem.sbuf("b_qk", [P, 2, G])
        b_low = mem.sbuf("b_low", [P, 2, G])
        low = mem.sbuf("low", [P, 2])
        ctx_t = mem.sbuf("ctx_t", [P, 2, S])
        xn = mem.sbuf("xn", [P, 2, TB, D])
        xn_t = mem.sbuf("xn_t", [P, 2, S])
        high = mem.sbuf("high", [P, 2, 2, S], F32R)
        qk = mem.sbuf("qk", [P, 2, 2, G, S], F32R)
        q_less = mem.sbuf("q_less", [P, G, S], F32R)
        k_kept = mem.sbuf("k_kept", [P, 2, G, S], F32R)
        v = mem.sbuf("v", [P, 2, TB, HN, SLOT])
        neg_max = mem.sbuf("neg_max", [P, TB, G, HG])
        max_high = mem.sbuf("max_high", [P, TB, G, HG], F32R)
        max_rows = mem.sbuf("max_rows", [P, TB, G, HG, SLOT])
        p_t = mem.sbuf("p_t", [P, 8, 2, S])
        o_t = mem.sbuf("o_t", [P, G, S])
        recip = mem.sbuf("recip", [P, TB, HN, 1])
        o_n = mem.sbuf("o_n", [P, TB, D])
        on_t = mem.sbuf("on_t", [P, S])
        if hw.masked:
            mask_in = mem.sbuf("mask_in", [P, 2, TB, S], I32)
            mask = mem.sbuf("mask", [P, 2, TB, S], BF16)
            ident_b = mem.sbuf("ident_b", [P, P], BF16)
        work = [mem.psum(f"work{i}", [P, 512]) for i in range(2)]
        side = [mem.psum(f"side{i}", [P, 512]) for i in range(2)]
        sn_ps = [mem.psum(f"sn_ps{i}", [P, 2, S]) for i in range(2)]
        st_ps = [mem.psum(f"st_ps{i}", [P, 2, S]) for i in range(2)]

        const_in = mem.sem("const_in")
        const_set = mem.sem("const_set")
        ctx_in = [mem.sem(f"ctx_in_{j}") for j in range(2)]
        xt_done = mem.sem("xt_done")
        xt_ready = mem.sem("xt_ready")
        proj_done = mem.sem("proj_done")
        high_ready = mem.sem("high_ready")
        split_ready = mem.sem("split_ready")
        v_done = mem.sem("v_done")
        v_ready = mem.sem("v_ready")
        sn_done = mem.sem("sn_done")
        sn_read = mem.sem("sn_read")
        max_steps = mem.sem("max_steps")
        mt_done = mem.sem("mt_done")
        q_max_ready = mem.sem("q_max_ready")
        kept_ready = mem.sem("kept_ready")
        st_done = mem.sem("st_done")
        p_ready = mem.sem("p_ready")
        pv_done = mem.sem("pv_done")
        ot_ready = mem.sem("ot_ready")
        on_done = mem.sem("on_done")
        on_ready = mem.sem("on_ready")
        ont_done = mem.sem("ont_done")
        ont_ready = mem.sem("ont_ready")
        out_done = mem.sem("out_done")
        x_ready = mem.sem("x_ready")
        norm_steps = mem.sem("norm_steps")
        out_steps = mem.sem("out_steps")
        block = stack.enter_context(nc.Block())
        consts = [(w_qk, "w_qk"), (w_v, "w_v"), (w_o, "w_o"), (b_v, "b_v"), (b_o, "b_o"), (b_qk, "b_qk"),
                  (b_low, "b_low"), (low, "low")]
        if hw.masked:
            consts.append((mask_in, "mask"))

        def need(engine, sem, value):
            if not isinstance(value, int) or value > 0:
                engine.wait_ge(sem, value)

        def turns(engine, turn):
            def straight(t):
                turn(t, t % 2, t + 1 < B, 0 <= t < B, 1 <= t <= B, t >= 2)

            for t in range(-1, 2):
                straight(t)
            with engine.Fori(1, B // 2 - 1) as i:
                for j in range(2):
                    turn(i * 2 + j, j, True, True, True, True)
            for t in range(B - 2, B + 2):
                straight(t)

        def unit_of(n):
            return n // 8, n // 4 % 2, n % 4

        @block.sync
        def _(sync):
            for t, n in consts:
                sync.dma_start(t[:], a[hw.name + "_" + n]).then_inc(const_in, 16)

            def load(c, j):
                need(sync, v_done, c - 1)
                sync.dma_start(ctx_t[:, j, :], a["ctx_t"][:, bass.ds(c, 1), :]).then_inc(ctx_in[j], 16)

            load(0, 0)
            load(1, 1)
            with sync.Fori(1, B // 2) as i:
                for j in range(2):
                    load(i * 2 + j, j)

        @block.gpsimd
        def _(pool):
            norm_power_set(nc, pool, nb)

            def turn(t, j, ahead, now):
                if ahead:
                    arriving.arrive(pool, t + 1)
                    norm_gpsimd(nc, pool, nb, t + 1)
                if now:
                    pool.wait_ge(split_ready, t * 4 + 4)
                    need(pool, st_done, (t - 1) * UNITS)
                    apart(pool)
                    nc.gpsimd.tensor_copy(k_kept[:, j], qk[:, j, 1]).then_inc(kept_ready, 1)

            for t in range(-1, B):
                turn(t, t % 2, t + 1 < B, t >= 0)

        @block.tensor
        def _(pe):

            def scores(out, left, right, tile, n, side_of_mask):
                gp, _, hh = unit_of(n)
                rows = slice(hh * SLOT, (hh + 1) * SLOT)
                for g in range(2):
                    last = nc.tensor.matmul(out[:, g, :], left[rows, gp * 2 + g, tile * P:(tile + 1) * P],
                                            right[rows, gp * 2 + g, :], start=g == 0 or not hw.masked,
                                            stop=not hw.masked, skip_group_check=hw.masked)
                if hw.masked:
                    last = nc.tensor.matmul(out[:], ident_b[:], mask[:, side_of_mask, tile:tile + 1, :].to_broadcast([P, 2, S]),
                                            start=False, stop=True, skip_group_check=True)
                return last

            def sums(c, j, u):
                gp, kt, _ = unit_of(u * 4)
                pe.wait_ge(p_ready, c * UNITS + u * 4 + 4)
                for g in range(2):
                    for hh in range(HG):
                        last = nc.tensor.matmul(work[gp][hh * SLOT:(hh + 1) * SLOT, g * S:(g + 1) * S],
                                                v[:, j, kt, (gp * 2 + g) * HG + hh, :], p_t[:, u % 2 * 4 + hh, g, :],
                                                start=kt == 0 and g == 0, stop=kt == 1, skip_group_check=True)
                last.then_inc(pv_done, 1)

            def turn(t, j, ahead, now, before, last_):
                def spread_maxima():
                    pe.wait_ge(max_steps, t * 4)
                    pe.wait_ge(v_ready, t)
                    if now:
                        pe.wait_ge(split_ready, t * 4 + 4)
                    else:
                        pe.wait_ge(x_ready, t - 2)
                    for gp in range(2):
                        for g in range(2):
                            for qt in range(TB):
                                last = nc.tensor.transpose(side[gp][:, g * S + qt * P:g * S + (qt + 1) * P],
                                                           max_rows[:, qt, gp * 2 + g].rearrange("p h s -> p (h s)"), ident[:])
                        last.then_inc(mt_done, 1)

                def transpose_x():
                    pe.wait_ge(nb.ready, t + 2)
                    if before:
                        pe.wait_ge(q_max_ready, (t - 1) * 2 + 1)
                    elif now:
                        pe.wait_ge(split_ready, 4)
                    for n in range(TB):
                        last = nc.tensor.transpose(side[0][:, n * P:(n + 1) * P], xn[:, 1 - j, n, :], ident[:])
                    last.then_inc(xt_done, 1)

                def project(n):
                    if n == 0:
                        if isinstance(t, int) and t < 0:
                            pe.wait_ge(const_in, len(consts) * 16)
                            pe.wait_ge(const_set, 4)
                        pe.wait_ge(xt_ready, t + 2)
                        pe.wait_ge(ctx_in[1 - j], ((t + 1) // 2 if isinstance(t, int) else (t - j) // 2 + j) * 16 + 16)
                    if n == 1 and last_:
                        pe.wait_ge(x_ready, t - 1)
                    elif n == 1 and before:
                        pe.wait_ge(q_max_ready, t * 2)
                    if n >= 2:
                        pe.wait_ge(split_ready, (t + 1) * 4 + n - 1)
                    for g in range(2):
                        last = nc.tensor.matmul(side[n % 2][:, g * S:(g + 1) * S], w_qk[:, n // 2, n % 2 * 2 + g, :],
                                                xn_t[:, 1 - j, :] if n < 2 else ctx_t[:, 1 - j, :], start=True, stop=True)
                    last.then_inc(proj_done, 1)

                def values():
                    if ahead:
                        pe.wait_ge(split_ready, (t + 1) * 4 + 3)
                    elif before:
                        pe.wait_ge(q_max_ready, t * 2)
                    for n in range(TB):
                        last = nc.tensor.matmul(side[0][:, n * D:(n + 1) * D], ctx_t[:, j, n * P:(n + 1) * P], w_v[:],
                                                start=True, stop=True)
                    last.then_inc(v_done, 1)

                def turn_sums():
                    pe.wait_ge(ot_ready, (t - 1) * 2)
                    for qt in range(TB):
                        for g in range(G):
                            last = nc.tensor.transpose(work[qt][:, g * P:(g + 1) * P], o_t[:, g, qt * P:(qt + 1) * P], ident[:])
                        last.then_inc(on_done, 1)

                def turn_normalised():
                    pe.wait_ge(on_ready, (t - 1) * 2)
                    if before:
                        pe.wait_ge(q_max_ready, t * 2)
                    else:
                        pe.wait_ge(x_ready, t - 2)
                    for qt in range(TB):
                        last = nc.tensor.transpose(side[1][:, qt * P:(qt + 1) * P], o_n[:, qt, :], ident[:])
                    last.then_inc(ont_done, 1)

                def output():
                    pe.wait_ge(ont_ready, t - 1)
                    for qt in range(TB):
                        last = nc.tensor.matmul(side[1][:, qt * D:(qt + 1) * D], on_t[:, qt * P:(qt + 1) * P], w_o[:],
                                                start=True, stop=True)
                    last.then_inc(out_done, 1)

                for k in range(STEPS):
                    if k == 0 and before:
                        spread_maxima()
                    if k == 1 and last_:
                        sums(t - 2, j, 3)
                    if k == jobs["x"] and ahead:
                        transpose_x()
                    if k == jobs["turn sums"] and last_:
                        turn_sums()
                    if k == jobs["turn normalised"] and last_:
                        turn_normalised()
                    if k in jobs["project"] and ahead:
                        project(jobs["project"].index(k))
                    if k == jobs["output"] and last_:
                        output()
                    if k == jobs["values"] and now:
                        values()
                    if k in jobs["sums"] and before:
                        u = jobs["sums"].index(k)
                        if u == 0:
                            pe.wait_ge(v_ready, t)
                            if last_:
                                pe.wait_ge(on_ready, (t - 1) * 2)
                        sums(t - 1, 1 - j, u)
                    if now and k < UNITS:
                        if k == 0:
                            pe.wait_ge(split_ready, t * 4 + 4)
                        need(pe, sn_read, t * UNITS + k - 1)
                        scores(sn_ps[k % 2], qk[:, j, 0], qk[:, j, 1], unit_of(k)[1], k, 0).then_inc(sn_done, 1)
                    if before and k >= LAG:
                        n = k - LAG
                        if n == 0:
                            pe.wait_ge(q_max_ready, t * 2)
                            pe.wait_ge(kept_ready, t)
                        need(pe, p_ready, (t - 1) * UNITS + n - 1)
                        scores(st_ps[n % 2], k_kept[:, 1 - j], q_less, unit_of(n)[1], n, 1).then_inc(st_done, 1)

            turns(pe, turn)

        @block.scalar
        def _(act):
            act.wait_ge(const_in, len(consts) * 16)
            if later_loads:
                later_loads(act)

            def keep_sums(c, gp):
                act.wait_ge(pv_done, c * 4 + gp * 2 + 2)
                need(act, on_done, c * 2)
                nc.scalar.activation(o_t[:, gp * 2:gp * 2 + 2, :].rearrange("p g s -> p (g s)"), work[gp][:],
                                     ACT.Copy).then_inc(ot_ready, 1)

            def turn(t, j, ahead, now, before, last_):
                def high_parts(n):
                    act.wait_ge(proj_done, (t + 1) * 4 + n + 1)
                    need(act, split_ready, (t + 1) * 4 + n - 1)
                    for g in range(2):
                        last = nc.scalar.activation(
                            high[:, n % 2, g, :], side[n % 2][:, g * S:(g + 1) * S], ACT.Identity,
                            bias=b_low[:, n // 2, n % 2 * 2 + g:n % 2 * 2 + g + 1], scale=low[:, n // 2:n // 2 + 1])
                    last.then_inc(high_ready, 1)

                for k in range(STEPS):
                    if k == 2 and last_:
                        keep_sums(t - 2, 1)
                    if k == jobs["x"] + 1 and ahead:
                        act.wait_ge(xt_done, t + 2)
                        need(act, proj_done, (t - 1) * 4 + 2)
                        nc.scalar.activation(xn_t[:, 1 - j, :], side[0][:, 0:S], ACT.Copy).then_inc(xt_ready, 1)
                    if k == jobs["turn normalised"] + 1 and last_:
                        act.wait_ge(ont_done, t - 1)
                        need(act, out_done, t - 2)
                        nc.scalar.activation(on_t[:], side[1][:, 0:S], ACT.Copy).then_inc(ont_ready, 1)
                    if k - 1 in jobs["project"] and ahead:
                        high_parts(jobs["project"].index(k - 1))
                    if k == jobs["sums"][1] + 1 and before:
                        keep_sums(t - 1, 0)
                    if k == jobs["values"] + 1 and now and not hw.biased:
                        act.wait_ge(v_done, t + 1)
                        need(act, pv_done, (t - 1) * 4)
                        nc.scalar.activation(v[:, j, :, :, 0:HD].rearrange("p t h d -> p (t h) d"),
                                             side[0][:, 0:TB * D].rearrange("p (n d) -> p n d", d=HD),
                                             ACT.Copy).then_inc(v_ready, 1)
                    if before and k >= LAG:
                        n = k - LAG
                        act.wait_ge(st_done, (t - 1) * UNITS + n + 1)
                        need(act, pv_done, (t - 1) * 4 + n // 4 - 1)
                        nc.scalar.activation(p_t[:, n % 8], st_ps[n % 2][:], ACT.Exp, scale=hw.scale).then_inc(p_ready, 1)

            turns(act, turn)

        @block.vector
        def _(dve):
            def constants():
                nc.vector.memset(v[:], 0.0).then_inc(const_set, 1)
                nc.vector.memset(max_rows[:], 0.0).then_inc(const_set, 1)
                dve.wait_ge(const_set, 2)
                nc.vector.memset(v[:, :, :, :, HD:HD + 1].rearrange("p j t h o -> p (j t h) o"), 1.0).then_inc(const_set, 1)
                dve.wait_ge(const_in, len(consts) * 16)
                if hw.masked:
                    for n in range(2):
                        nc.vector.tensor_scalar(out=mask[:, n], in0=mask_in[:, n], scalar1=0.0, scalar2=MASKED,
                                                op0=ALU.is_equal, op1=ALU.mult)
                    nc.vector.tensor_copy(ident_b[:], ident[:]).then_inc(const_set, 1)
                else:
                    dve.sem_inc(const_set, 1)
                dve.wait_ge(const_set, 4)

            def turn(t, j, ahead, now, before, last_):
                def take_maxima():
                    need(dve, st_done, (t - 1) * UNITS)
                    for gp in range(2):
                        dve.wait_ge(mt_done, (t - 1) * 2 + gp + 1)
                        nc.vector.tensor_tensor(
                            q_less[:, gp * 2:gp * 2 + 2, :], qk[:, 1 - j, 0, gp * 2:gp * 2 + 2, :].bitcast(F32),
                            side[gp][:].rearrange("p (g s) -> p g s", g=2), ALU.add).then_inc(q_max_ready, 1)

                def normalise():
                    need(dve, ont_done, t - 2)
                    for qt in range(TB):
                        dve.wait_ge(on_done, (t - 2) * 2 + qt + 1)
                        sums = work[qt][:].rearrange("p (h s) -> p h s", s=SLOT)
                        out.link(nc.vector.reciprocal(recip[:, qt], sums[:, :, HD:HD + 1]))
                        nc.vector.tensor_tensor(o_n[:, qt, :].rearrange("p (h d) -> p h d", d=HD), sums[:, :, 0:HD],
                                                recip[:, qt].to_broadcast([P, HN, HD]), ALU.mult).then_inc(on_ready, 1)

                def split(n):
                    dve.wait_ge(high_ready, (t + 1) * 4 + n + 1)
                    need(dve, sn_done, t * UNITS)
                    need(dve, kept_ready, t)
                    for g in range(2):
                        at = n % 2 * 2 + g
                        last = nc.vector.scalar_tensor_tensor(
                            out=qk[:, 1 - j, n // 2, at, :], in0=side[n % 2][:, g * S:(g + 1) * S],
                            scalar=b_qk[:, n // 2, at:at + 1], in1=high[:, n % 2, g, :].bitcast(F32),
                            op0=ALU.add, op1=ALU.subtract)
                    last.then_inc(split_ready, 1)

                def output():
                    dve.wait_ge(out_done, t - 1)
                    xb = x[:, bass.ds((t - 2) * TB, TB), :]
                    if hw.biased:
                        out.link(nc.vector.tensor_tensor(xb, xb, b_o[:].unsqueeze(1).to_broadcast([P, TB, D]), ALU.add))
                    nc.vector.tensor_tensor(xb, xb, side[1][:, 0:TB * D].rearrange("p (t d) -> p t d", t=TB),
                                            ALU.add).then_inc(x_ready, 1)
                    out.close()

                def maxima_as_rows():
                    dve.wait_ge(sn_read, t * UNITS + UNITS)
                    need(dve, mt_done, t * 2)
                    m = Steps(dve, max_steps, t, 4)
                    m.link(nc.vector.tensor_copy(max_high[:], neg_max[:]))
                    for qt in range(TB):
                        m.step(nc.vector.tensor_copy(max_rows[:, qt, :, :, MAX_ROW], max_high[:, qt].bitcast(F32)))
                    nc.vector.tensor_tensor(max_rows[:, 0, :, :, MAX_ROW + 1], neg_max[:, 0], max_high[:, 0].bitcast(F32), ALU.subtract)
                    m.step(nc.vector.tensor_tensor(max_rows[:, 1, :, :, MAX_ROW + 1], neg_max[:, 1], max_high[:, 1].bitcast(F32), ALU.subtract))
                    m.close()

                out = Steps(dve, out_steps, t - 2, 2 + (1 if hw.biased else 0))
                norm = Steps(dve, norm_steps, t + 1, NORM_STEPS)
                if ahead:
                    arriving.add(dve, x, t + 1)
                    norm_moments(nc, dve, norm, nb, x, t + 1)
                if isinstance(t, int) and t < 0:
                    constants()
                if before:
                    take_maxima()
                for k in range(STEPS):
                    if now and k < UNITS:
                        gp, qt, hh = unit_of(k)
                        dve.wait_ge(sn_done, t * UNITS + k + 1)
                        nc.vector.tensor_reduce(neg_max[:, qt, gp * 2:gp * 2 + 2, hh], sn_ps[k % 2][:], AX.X, ALU.max,
                                                negate=True).then_inc(sn_read, 1)
                    if k == 1 and ahead:
                        need(dve, xt_done, t)
                        norm_apply(nc, dve, norm, nb, x, t + 1, xn[:, 1 - j])
                    if k == jobs["turn sums"] + 1 and last_:
                        normalise()
                    if k - 1 in jobs["project"] and ahead:
                        split(jobs["project"].index(k - 1))
                    if k == jobs["output"] + 1 and last_:
                        output()
                    if k == UNITS - 1 and now:
                        maxima_as_rows()
                    if k == jobs["values"] + 1 and now and hw.biased:
                        dve.wait_ge(v_done, t + 1)
                        need(dve, pv_done, (t - 1) * 4)
                        for n in range(TB):
                            last = nc.vector.tensor_tensor(v[:, j, n, :, 0:HD],
                                                           side[0][:, n * D:(n + 1) * D].rearrange("p (h d) -> p h d", d=HD),
                                                           b_v[:].rearrange("p (h d) -> p h d", d=HD), ALU.add)
                        last.then_inc(v_ready, 1)

            turns(dve, turn)



PH = 4
PK = 128
HALF = 64
TOP = 8
EX = 16
EXPERT_BLOCKS = EX
MLP_BLOCKS = 4
UP_BLOCKS = EXPERT_BLOCKS + MLP_BLOCKS
DOWN_BLOCKS = UP_BLOCKS + MLP_BLOCKS
PICKS = PH * TOP
Q4 = P // PICKS
BANK_GROUPS = 8
PICK_STEPS = 20


def keyed_layer(nc, a, x, ident):
    from contextlib import ExitStack
    with ExitStack() as stack:
        mem = Memory(nc, stack, "pk")
        nb = NormBuffers(mem)
        w_q = mem.sbuf("w_q", [HALF, 2 * PH, D])
        keys = mem.sbuf("keys", [HALF, 2 * PH, PK])
        folded = mem.sbuf("folded", [P, 2, PH * PK])
        down = mem.sbuf("down", [P, DOWN_BLOCKS, P])
        up = mem.sbuf("up", [P, UP_BLOCKS, D])
        iota = mem.sbuf("iota", [P, PK])
        xn = mem.sbuf("xn", [P, TB, D])
        xn_t = mem.sbuf("xn_t", [P, 2, S])
        sim = mem.sbuf("sim", [P, 2, TB, PH, PK])
        best = mem.sbuf("best", [P, 2, TB * PH, TOP])
        best_at = mem.sbuf("best_at", [P, 2, TB * PH, TOP], U32)
        at = mem.sbuf("at", [P, 2, TB * PH, TOP])
        sums = mem.sbuf("sums", [P, TB * PH, TOP, TOP])
        top = mem.sbuf("top", [P, TB * PH, TOP])
        top_at = mem.sbuf("top_at", [P, TB * PH, TOP], U32)
        rank_at = mem.sbuf("rank_at", [P, 2, TB * PH, TOP], U32)
        rank = mem.sbuf("rank", [P, 2, TB * PH, TOP])
        chosen = mem.sbuf("chosen", [P, 2 * TB * PH, TOP, TOP])
        pick = mem.sbuf("pick", [P, 2, TB * PH, TOP])
        beyond = mem.sbuf("beyond", [P, TB * PH, TOP])
        gap = mem.sbuf("gap", [P, TB * PH, TOP])
        ex = mem.sbuf("ex", [P, TB * PH, TOP])
        total = mem.sbuf("total", [P, TB * PH])
        weight = mem.sbuf("weight", [P, TB * PH, TOP])
        spread = chosen[:].rearrange("p a s i -> p (a s i)").rearrange("p (n r g) -> p n r g", n=TB, r=EX)
        spread_t = mem.sbuf("spread_t", [P, TB, EX, PICKS])
        y_t = mem.sbuf("y_t", [P, TB, PICKS])
        ones_y = mem.sbuf("ones_y", [P, 2, TB, PICKS, PK])
        by_token = mem.sbuf("by_token", [P, 2, TB, PICKS, Q4, EX])
        acts = mem.sbuf("acts", [P, DOWN_BLOCKS, S])
        g = mem.sbuf("g", [P, EXPERT_BLOCKS, S])
        xt_ps = mem.psum("xt_ps", [P, 512])
        sim_ps = mem.psum("sim_ps", [P, 2, 512])
        d_ps = mem.psum("d_ps", [P, 2, 2, S])
        g_ps = mem.psum("g_ps", [P, 2, BANK_GROUPS, Q4, EX])
        y_ps = mem.psum("y_ps", [P, 512])

        first_in = mem.sem("first_in")
        const_in = mem.sem("const_in")
        const_set = mem.sem("const_set")
        fold_done = mem.sem("fold_done")
        fold_ready = mem.sem("fold_ready")
        xt_done = mem.sem("xt_done")
        xt_ready = mem.sem("xt_ready")
        sim_done = mem.sem("sim_done")
        sim_ready = mem.sem("sim_ready")
        gap_ready = mem.sem("gap_ready")
        exp_ready = mem.sem("exp_ready")
        spread_ready = mem.sem("spread_ready")
        by_token_ready = mem.sem("by_token_ready")
        y_t_ready = mem.sem("y_t_ready")
        ones_ready = mem.sem("ones_ready")
        ones_1_ready = mem.sem("ones_1_ready")
        d_done = mem.sem("d_done")
        d_ready = mem.sem("d_ready")
        g_done = mem.sem("g_done")
        g_ready = mem.sem("g_ready")
        w_ready = mem.sem("w_ready")
        y_done = mem.sem("y_done")
        x_ready = mem.sem("x_ready")
        norm_steps = mem.sem("norm_steps")
        pick_steps = mem.sem("pick_steps")
        block = stack.enter_context(nc.Block())
        FILLS = DOWN_BLOCKS // 2
        GATE_FILL = EXPERT_BLOCKS // 2
        GF = TB * PICKS // BANK_GROUPS

        def need(engine, sem, value):
            if not isinstance(value, int) or value > 0:
                engine.wait_ge(sem, value)

        def turns(engine, turn):
            def straight(t):
                turn(t, t % 2, t + 1 < B, 0 <= t < B, 1 <= t <= B, t >= 2)

            for t in range(-1, 2):
                straight(t)
            with engine.Fori(1, B // 2 - 1) as i:
                for j in range(2):
                    turn(i * 2 + j, j, True, True, True, True)
            for t in range(B - 2, B + 2):
                straight(t)

        @block.sync
        def _(sync):
            for t, n in ((w_q, "pk_w_q"), (keys, "pk_keys"), (iota, "iota")):
                sync.dma_start(t[:], a[n]).then_inc(first_in, 16)
            for t, n in ((down, "pk_down"), (up, "pk_up")):
                sync.dma_start(t[:], a[n]).then_inc(const_in, 16)

        @block.gpsimd
        def _(pool):
            norm_power_set(nc, pool, nb)
            pool.wait_ge(first_in, 48)

            def turn(t, j, ahead, now, before, last):
                if ahead:
                    norm_gpsimd(nc, pool, nb, t + 1)
                if isinstance(t, int) and t < 0:
                    nc.gpsimd.memset(by_token[:], 0.0).then_inc(const_set, 1)
                if now:
                    pool.wait_ge(y_t_ready, t + 1)
                    need(pool, g_done, (t - 1) * GF)
                    apart(pool)
                    for group in range(PICKS):
                        last_one = nc.gpsimd.tensor_scalar(out=ones_y[:, j, 1, group, :], in0=iota[:],
                                                           scalar1=y_t[:, 1, group:group + 1], scalar2=None, op0=ALU.is_equal)
                    last_one.then_inc(ones_1_ready, 1)

            turns(pool, turn)

        @block.tensor
        def _(pe):
            pe.wait_ge(first_in, 48)
            for p in range(2):
                for h in range(PH):
                    last = nc.tensor.matmul(sim_ps[:, p, h * PK:(h + 1) * PK], w_q[:, p * PH + h, :], keys[:, p * PH + h, :],
                                            start=True, stop=True)
            last.then_inc(fold_done, 1)
            pe.wait_ge(fold_ready, 1)
            def turn(t, j, ahead, now, before, last_):
                if last_:
                    pe.wait_ge(w_ready, (t - 1) * 2)
                    need(pe, x_ready, t - 2)
                    for n in range(TB):
                        for c in range(UP_BLOCKS):
                            last = nc.tensor.matmul(y_ps[:, n * D:(n + 1) * D], acts[:, c, n * P:(n + 1) * P], up[:, c, :],
                                                    start=c == 0, stop=c == UP_BLOCKS - 1)
                    last.then_inc(y_done, 1)
                if isinstance(t, int) and t == 1:
                    pe.wait_ge(const_in, 32)
                if before:
                    for n in range(FILLS):
                        need(pe, d_ready, (t - 1) * FILLS + n - 1)
                        for c in range(2):
                            last = nc.tensor.matmul(d_ps[:, n % 2, c, :], down[:, n * 2 + c, :], xn_t[:, 1 - j, :],
                                                    start=True, stop=True)
                        last.then_inc(d_done, 1)
                    pe.wait_ge(by_token_ready, t)
                    pe.wait_ge(ones_ready, t)
                    pe.wait_ge(ones_1_ready, t)
                    for f in range(GF):
                        need(pe, g_ready, (t - 1) * GF + f - 1)
                        for u in range(BANK_GROUPS):
                            n, group = f // (GF // TB), f % (GF // TB) * BANK_GROUPS + u
                            last = nc.tensor.matmul(g_ps[:, f % 2, u], ones_y[:, 1 - j, n, group, :],
                                                    by_token[:, 1 - j, n, group], start=True, stop=True)
                        last.then_inc(g_done, 1)
                if ahead:
                    pe.wait_ge(nb.ready, t + 2)
                    need(pe, xt_ready, t + 1)
                    for n in range(TB):
                        last = nc.tensor.transpose(xt_ps[:, n * P:(n + 1) * P], xn[:, n, :], ident[:])
                    last.then_inc(xt_done, 1)
                    pe.wait_ge(xt_ready, t + 2)
                    for n in range(TB):
                        for p in range(2):
                            need(pe, sim_ready, (t + 1) * 4 + n * 2 + p - 1)
                            nc.tensor.matmul(sim_ps[:, p, :], xn_t[:, 1 - j, n * P:(n + 1) * P], folded[:, p, :],
                                             start=True, stop=True).then_inc(sim_done, 1)

            turns(pe, turn)

        @block.scalar
        def _(act):
            act.wait_ge(fold_done, 1)
            nc.scalar.activation(folded[:], sim_ps[:], ACT.Copy).then_inc(fold_ready, 1)

            def turn(t, j, ahead, now, before, last_):
                if before:
                    need(act, y_done, t - 1)
                    for n in range(FILLS):
                        act.wait_ge(d_done, (t - 1) * FILLS + n + 1)
                        nc.scalar.activation(acts[:, n * 2:n * 2 + 2, :], d_ps[:, n % 2],
                                             ACT.Silu if n < UP_BLOCKS // 2 else ACT.Copy).then_inc(d_ready, 1)
                if now:
                    act.wait_ge(gap_ready, t + 1)
                    need(act, spread_ready, t)
                    nc.scalar.activation(ex[:], gap[:], ACT.Exp).then_inc(exp_ready, 1)
                if before:
                    need(act, w_ready, (t - 1) * 2)
                    for f in range(GF):
                        n, k = f // (GF // TB), f % (GF // TB)
                        act.wait_ge(g_done, (t - 1) * GF + f + 1)
                        nc.scalar.activation(
                            g[:, :, n * P:(n + 1) * P].rearrange("p r (q g) -> p g q r", q=Q4)[:, k * BANK_GROUPS:(k + 1) * BANK_GROUPS],
                            g_ps[:, f % 2], ACT.Copy).then_inc(g_ready, 1)
                if ahead:
                    act.wait_ge(xt_done, t + 2)
                    need(act, d_done, t * FILLS)
                    nc.scalar.activation(xn_t[:, 1 - j, :], xt_ps[:, 0:S], ACT.Copy).then_inc(xt_ready, 1)
                    need(act, gap_ready, t + 1)
                    for n in range(TB):
                        for p in range(2):
                            act.wait_ge(sim_done, (t + 1) * 4 + n * 2 + p + 1)
                            nc.scalar.activation(sim[:, p, n], sim_ps[:, p, :].rearrange("p (h k) -> p h k", h=PH),
                                                 ACT.Copy).then_inc(sim_ready, 1)
                if now:
                    if isinstance(t, int) and t == 0:
                        act.wait_ge(const_set, 1)
                    act.wait_ge(spread_ready, t + 1)
                    need(act, g_done, (t - 1) * GF)
                    for n in range(TB):
                        for q in range(Q4):
                            rows = slice(q * PICKS, (q + 1) * PICKS)
                            last = nc.scalar.activation(by_token[rows, j, n, :, q, :],
                                                        spread_t[rows, n].rearrange("p r g -> p g r"), ACT.Copy)
                    last.then_inc(by_token_ready, 1)

            turns(act, turn)

        @block.vector
        def _(dve):
            squares = [P, 2 * TB * PH, TOP, TOP]

            def output(t):
                dve.wait_ge(y_done, t - 1)
                xb = x[:, bass.ds((t - 2) * TB, TB), :]
                nc.vector.tensor_tensor(xb, xb, y_ps[:, 0:TB * D].rearrange("p (t d) -> p t d", t=TB),
                                        ALU.add).then_inc(x_ready, 1)

            def turn(t, j, ahead, now, before, last_):
                if ahead:
                    steps = Steps(dve, norm_steps, t + 1, NORM_STEPS)
                    norm_moments(nc, dve, steps, nb, x, t + 1)
                if now:
                    if isinstance(t, int) and t == 0:
                        dve.wait_ge(first_in, 48)
                    s = Steps(dve, pick_steps, t, PICK_STEPS)
                    for n in range(TB):
                        for p in range(2):
                            dve.wait_ge(sim_ready, t * 4 + n * 2 + p + 1)
                            apart(dve)
                            for h in range(PH):
                                last = nc.vector.max(best[:, p, n * PH + h, :], sim[:, p, n, h, :])
                    s.link(last)
                    apart(dve)
                    for p in range(2):
                        for n in range(TB):
                            for h in range(PH):
                                last = nc.vector.max_index(best_at[:, p, n * PH + h, :], best[:, p, n * PH + h, :], sim[:, p, n, h, :])
                    s.step(last)
                    s.link(nc.vector.tensor_tensor(sums[:], best[:, 0].unsqueeze(3).to_broadcast([P, TB * PH, TOP, TOP]),
                                                   best[:, 1].unsqueeze(2).to_broadcast([P, TB * PH, TOP, TOP]), ALU.add))
                    s.step(nc.vector.tensor_copy(at[:], best_at[:]))
                    for h in range(TB * PH):
                        last = nc.vector.max(top[:, h, :], sums[:, h].rearrange("p i j -> p (i j)"))
                    s.link(last)
                    apart(dve)
                    for h in range(TB * PH):
                        last = nc.vector.max_index(top_at[:, h, :], top[:, h, :], sums[:, h].rearrange("p i j -> p (i j)"))
                    s.step(last)
                    nc.vector.tensor_tensor(gap[:], top[:], top[:, :, 0:1].to_broadcast([P, TB * PH, TOP]),
                                            ALU.subtract).then_inc(gap_ready, 1)
                    s.settle()
                    if last_:
                        output(t)
                    s.step(nc.vector.tensor_scalar(out=rank_at[:, 0], in0=top_at[:], scalar1=3, scalar2=None,
                                                   op0=ALU.logical_shift_right))
                    s.link(nc.vector.tensor_scalar(out=rank_at[:, 1], in0=top_at[:], scalar1=TOP - 1, scalar2=None,
                                                   op0=ALU.bitwise_and))
                    s.link(nc.vector.tensor_copy(rank[:], rank_at[:]))
                    s.link(nc.vector.tensor_tensor(chosen[:], rank[:].rearrange("p a h s -> p (a h) s").unsqueeze(3).to_broadcast(squares),
                                                   iota[:, 0:TOP].unsqueeze(1).unsqueeze(1).to_broadcast(squares), ALU.is_equal))
                    s.link(nc.vector.tensor_tensor(chosen[:], chosen[:],
                                                   at[:].rearrange("p a h s -> p (a h) s").unsqueeze(2).to_broadcast(squares), ALU.mult))
                    s.link(nc.vector.tensor_reduce(pick[:].rearrange("p a h s -> p (a h) s"), chosen[:], AX.X, ALU.add))
                    s.link(nc.vector.tensor_scalar(out=beyond[:], in0=pick[:, 0], scalar1=EX - 0.5, scalar2=PK - 1.0,
                                                   op0=ALU.is_gt, op1=ALU.mult))
                    s.step(nc.vector.tensor_scalar(out=pick[:, 0], in0=pick[:, 0], scalar1=EX - 1.0, scalar2=None, op0=ALU.min))
                    s.link(nc.vector.tensor_tensor(pick[:, 1], pick[:, 1], beyond[:], ALU.max))
                    need(dve, ones_1_ready, t)
                    nc.vector.transpose(y_t[:].rearrange("p n g -> p (n g)"),
                                        pick[:, 1].rearrange("p h s -> p (h s)")).then_inc(y_t_ready, 1)
                    dve.wait_ge(y_t_ready, t + 1)
                    need(dve, g_done, (t - 1) * GF)
                    wide = [P, PICKS, PK]
                    nc.vector.tensor_tensor(ones_y[:, j, 0], y_t[:, 0].unsqueeze(2).to_broadcast(wide),
                                            iota[:].unsqueeze(1).to_broadcast(wide), ALU.is_equal).then_inc(ones_ready, 1)
                    dve.wait_ge(exp_ready, t + 1)
                    s.link(nc.vector.tensor_reduce(total[:], ex[:], AX.X, ALU.add))
                    s.link(nc.vector.reciprocal(total[:], total[:]))
                    s.link(nc.vector.tensor_tensor(weight[:], ex[:], total[:].unsqueeze(2).to_broadcast([P, TB * PH, TOP]), ALU.mult))
                    by_x = [P, TB, EX, PICKS]
                    s.link(nc.vector.tensor_tensor(
                        spread, pick[:, 0].rearrange("p (n h) s -> p n (h s)", n=TB).unsqueeze(2).to_broadcast(by_x),
                        iota[:, 0:EX].unsqueeze(1).unsqueeze(3).to_broadcast(by_x), ALU.is_equal))
                    s.link(nc.vector.tensor_tensor(
                        spread, spread, weight[:].rearrange("p (n h) s -> p n (h s)", n=TB).unsqueeze(2).to_broadcast(by_x),
                        ALU.mult))
                    s.close()
                    need(dve, by_token_ready, t)
                    nc.vector.transpose(spread_t[:].rearrange("p n r g -> p (n r g)"),
                                        spread.rearrange("p n r s -> p (n r s)")).then_inc(spread_ready, 1)
                elif last_:
                    output(t)
                if ahead:
                    need(dve, xt_done, t + 1)
                    norm_apply(nc, dve, steps, nb, x, t + 1, xn)
                if before:
                    dve.wait_ge(d_ready, t * FILLS)
                    nc.vector.tensor_tensor(acts[:, EXPERT_BLOCKS:UP_BLOCKS, :], acts[:, EXPERT_BLOCKS:UP_BLOCKS, :],
                                            acts[:, UP_BLOCKS:DOWN_BLOCKS, :], ALU.mult).then_inc(w_ready, 1)
                    dve.wait_ge(g_ready, t * GF)
                    nc.vector.tensor_tensor(acts[:, 0:EXPERT_BLOCKS, :], acts[:, 0:EXPERT_BLOCKS, :], g[:],
                                            ALU.mult).then_inc(w_ready, 1)

            turns(dve, turn)





def one_head_layer(nc, a, x, ident, later_loads):
    from contextlib import ExitStack
    scale = D ** -0.5
    with ExitStack() as stack:
        mem = Memory(nc, stack, "k3")
        nb = NormBuffers(mem)
        w = mem.sbuf("w", [P, 4, D])
        b_qk = mem.sbuf("b_qk", [P, 2])
        b_vo = mem.sbuf("b_vo", [P, 2, D])
        mask_in = mem.sbuf("mask_in", [1, B, S], U8)
        mask = mem.sbuf("mask", [1, B, S], BF16)
        ones = mem.sbuf("ones", [1, P], BF16)
        ctx_t = mem.sbuf("ctx_t", [P, 2, S])
        xn = mem.sbuf("xn", [P, 2, TB, D])
        xn_t = mem.sbuf("xn_t", [P, 2, S])
        q_t = mem.sbuf("q_t", [P, 2, S])
        k_t = mem.sbuf("k_t", [P, 2, S])
        v = mem.sbuf("v", [P, 2, TB, D])
        neg_max = mem.sbuf("neg_max", [P, 2, TB])
        p = mem.sbuf("p", [P, 2, TB, S])
        total = mem.sbuf("total", [P, 2, TB])
        p_t = mem.sbuf("p_t", [P, TB, S])
        o_t = mem.sbuf("o_t", [P, S])
        recip = mem.sbuf("recip", [P, TB])
        xt_ps = mem.psum("xt_ps", [P, 512])
        qk_ps = mem.psum("qk_ps", [P, 2, S])
        v_ps = mem.psum("v_ps", [P, 512])
        s_ps = mem.psum("s_ps", [P, 2, TB, S])
        pt_ps = mem.psum("pt_ps", [P, TB, S])
        o_ps = mem.psum("o_ps", [P, 512])
        out_ps = mem.psum("out_ps", [P, 512])

        const_in = mem.sem("const_in")
        const_set = mem.sem("const_set")
        ctx_in = [mem.sem(f"ctx_in_{j}") for j in range(2)]
        xt_done = mem.sem("xt_done")
        xt_ready = mem.sem("xt_ready")
        qk_done = mem.sem("qk_done")
        qk_ready = mem.sem("qk_ready")
        v_done = mem.sem("v_done")
        v_ready = mem.sem("v_ready")
        s_done = mem.sem("s_done")
        max_ready = mem.sem("max_ready")
        p_ready = mem.sem("p_ready")
        pt_done = mem.sem("pt_done")
        pt_ready = mem.sem("pt_ready")
        o_done = mem.sem("o_done")
        o_ready = mem.sem("o_ready")
        out_done = mem.sem("out_done")
        x_ready = mem.sem("x_ready")
        norm_steps = mem.sem("norm_steps")
        out_steps = mem.sem("out_steps")
        block = stack.enter_context(nc.Block())

        def need(engine, sem, value):
            if not isinstance(value, int) or value > 0:
                engine.wait_ge(sem, value)

        def turns(engine, turn):
            def straight(t):
                turn(t, t % 2, t + 1 < B, 0 <= t < B, t >= 1)

            for t in range(-1, 2):
                straight(t)
            with engine.Fori(1, B // 2 - 1) as i:
                for j in range(2):
                    turn(i * 2 + j, j, True, True, True)
            for t in range(B - 2, B + 1):
                straight(t)

        @block.sync
        def _(sync):
            for t, n in ((w, "k3_w"), (b_qk, "k3_b_qk"), (b_vo, "k3_b_vo"), (mask_in, "k3_mask")):
                sync.dma_start(t[:], a[n]).then_inc(const_in, 16)

            def load(c, j):
                need(sync, qk_done, c - 1)
                sync.dma_start(ctx_t[:, j, :], a["ctx_t"][:, bass.ds(c, 1), :]).then_inc(ctx_in[j], 16)

            load(0, 0)
            load(1, 1)
            with sync.Fori(1, B // 2) as i:
                for j in range(2):
                    load(i * 2 + j, j)

        @block.gpsimd
        def _(pool):
            norm_power_set(nc, pool, nb)
            with pool.Fori(0, B) as b:
                norm_gpsimd(nc, pool, nb, b)

        @block.tensor
        def _(pe):
            pe.wait_ge(const_in, 64)

            def turn(t, j, ahead, now, before):
                if now:
                    pe.wait_ge(qk_ready, t + 1)
                    need(pe, p_ready, t - 1)
                    if isinstance(t, int) and t == 0:
                        pe.wait_ge(const_set, 2)
                    for qt in range(TB):
                        nc.tensor.matmul(s_ps[:, j, qt, :], q_t[:, j, qt * P:(qt + 1) * P], k_t[:, j, :],
                                         start=qt == 0, stop=False, skip_group_check=True)
                    nc.tensor.matmul(s_ps[:, j], ones[:], mask[:, bass.ds(t, 1), :].to_broadcast([1, TB, S]),
                                     start=False, stop=True, skip_group_check=True).then_inc(s_done, 1)
                if before:
                    pe.wait_ge(p_ready, t)
                    need(pe, pt_ready, t - 1)
                    for kt in range(TB):
                        for qt in range(TB):
                            last = nc.tensor.transpose(pt_ps[:, kt, qt * P:(qt + 1) * P], p[:, 1 - j, qt, kt * P:(kt + 1) * P],
                                                       ident[:])
                    last.then_inc(pt_done, 1)
                if ahead:
                    pe.wait_ge(ctx_in[1 - j], ((t + 1) // 2 if isinstance(t, int) else (t - j) // 2 + j) * 16 + 16)
                    need(pe, qk_ready, t + 1)
                    nc.tensor.matmul(qk_ps[:, 1, :], w[:, 1, :], ctx_t[:, 1 - j, :], start=True, stop=True)
                    pe.wait_ge(nb.ready, t + 2)
                    need(pe, xt_ready, t + 1)
                    for n in range(TB):
                        last = nc.tensor.transpose(xt_ps[:, n * P:(n + 1) * P], xn[:, 1 - j, n, :], ident[:])
                    last.then_inc(xt_done, 1)
                if before:
                    pe.wait_ge(pt_ready, t)
                    pe.wait_ge(v_ready, t)
                    need(pe, o_ready, t - 1)
                    for kt in range(TB):
                        last = nc.tensor.matmul(o_ps[:, 0:S], v[:, 1 - j, kt, :], p_t[:, kt, :], start=kt == 0, stop=kt == 1)
                    last.then_inc(o_done, 1)
                if ahead:
                    need(pe, v_ready, t + 1)
                    for n in range(TB):
                        last = nc.tensor.matmul(v_ps[:, n * D:(n + 1) * D], ctx_t[:, 1 - j, n * P:(n + 1) * P], w[:, 2, :],
                                                start=True, stop=True)
                    last.then_inc(v_done, 1)
                    pe.wait_ge(xt_ready, t + 2)
                    nc.tensor.matmul(qk_ps[:, 0, :], w[:, 0, :], xn_t[:, 1 - j, :], start=True, stop=True).then_inc(qk_done, 1)
                if before:
                    pe.wait_ge(o_ready, t)
                    need(pe, x_ready, t - 1)
                    for qt in range(TB):
                        last = nc.tensor.matmul(out_ps[:, qt * D:(qt + 1) * D], o_t[:, qt * P:(qt + 1) * P], w[:, 3, :],
                                                start=True, stop=True)
                    last.then_inc(out_done, 1)

            turns(pe, turn)

        @block.scalar
        def _(act):
            act.wait_ge(const_in, 64)
            later_loads(act)

            def turn(t, j, ahead, now, before):
                if before:
                    act.wait_ge(pt_done, t)
                    need(act, o_done, t - 1)
                    nc.scalar.activation(p_t[:], pt_ps[:], ACT.Copy).then_inc(pt_ready, 1)
                if ahead:
                    act.wait_ge(xt_done, t + 2)
                    need(act, qk_done, t)
                    nc.scalar.activation(xn_t[:, 1 - j, :], xt_ps[:, 0:S], ACT.Copy).then_inc(xt_ready, 1)
                if before:
                    act.wait_ge(o_done, t)
                    need(act, out_done, t - 1)
                    nc.scalar.activation(o_t[:], o_ps[:, 0:S], ACT.Copy).then_inc(o_ready, 1)
                if now:
                    act.wait_ge(max_ready, t + 1)
                    need(act, pt_done, t - 1)
                    need(act, x_ready, t - 1)
                    for qt in range(TB):
                        last = nc.scalar.activation(p[:, j, qt, :], s_ps[:, j, qt, :], ACT.Exp, bias=neg_max[:, j, qt:qt + 1],
                                                    accum_out=total[:, j, qt:qt + 1])
                    last.then_inc(p_ready, 1)

            turns(act, turn)

        @block.vector
        def _(dve):
            nc.vector.memset(ones[:], 1.0).then_inc(const_set, 1)

            def turn(t, j, ahead, now, before):
                if ahead:
                    steps = Steps(dve, norm_steps, t + 1, NORM_STEPS)
                    norm_moments(nc, dve, steps, nb, x, t + 1)
                if isinstance(t, int) and t < 0:
                    dve.wait_ge(const_in, 64)
                    nc.vector.tensor_scalar(out=mask[:], in0=mask_in[:], scalar1=0.0, scalar2=MASKED,
                                            op0=ALU.is_equal, op1=ALU.mult).then_inc(const_set, 1)
                if now:
                    dve.wait_ge(s_done, t + 1)
                    need(dve, p_ready, t - 1)
                    nc.vector.tensor_reduce(neg_max[:, j, :], s_ps[:, j], AX.X, ALU.max, negate=True).then_inc(max_ready, 1)
                if ahead:
                    need(dve, xt_done, t)
                    norm_apply(nc, dve, steps, nb, x, t + 1, xn[:, 1 - j])
                    dve.wait_ge(v_done, t + 2)
                    need(dve, o_done, t)
                    nc.vector.tensor_tensor(v[:, 1 - j], v_ps[:, 0:TB * D].rearrange("p (t d) -> p t d", t=TB),
                                            b_vo[:, 0:1, :].to_broadcast([P, TB, D]), ALU.add).then_inc(v_ready, 1)
                    dve.wait_ge(qk_done, t + 2)
                    need(dve, s_done, t)
                    nc.vector.tensor_scalar(out=k_t[:, 1 - j, :], in0=qk_ps[:, 1, :], scalar1=b_qk[:, 1:2], scalar2=None, op0=ALU.add)
                    nc.vector.tensor_scalar(out=q_t[:, 1 - j, :], in0=qk_ps[:, 0, :], scalar1=b_qk[:, 0:1], scalar2=scale,
                                            op0=ALU.add, op1=ALU.mult).then_inc(qk_ready, 1)
                if before:
                    out = Steps(dve, out_steps, t - 1, 3)
                    xb = x[:, bass.ds((t - 1) * TB, TB), :]
                    need(dve, x_ready, t - 1)
                    out.step(nc.vector.tensor_tensor(xb, xb, b_vo[:, 1:2, :].to_broadcast([P, TB, D]), ALU.add))
                    dve.wait_ge(p_ready, t)
                    out.link(nc.vector.reciprocal(recip[:], total[:, 1 - j, :]))
                    dve.wait_ge(out_done, t)
                    out.step(nc.vector.scalar_tensor_tensor(out=x[:, bass.ds((t - 1) * TB, 1), :], in0=out_ps[:, 0:D],
                                                            scalar=recip[:, 0:1], in1=x[:, bass.ds((t - 1) * TB, 1), :],
                                                            op0=ALU.mult, op1=ALU.add))
                    nc.vector.scalar_tensor_tensor(out=x[:, bass.ds((t - 1) * TB + 1, 1), :], in0=out_ps[:, D:2 * D],
                                                   scalar=recip[:, 1:2], in1=x[:, bass.ds((t - 1) * TB + 1, 1), :],
                                                   op0=ALU.mult, op1=ALU.add).then_inc(x_ready, 1)
                    out.close()

            turns(dve, turn)



def build(nc, a, out):
    from contextlib import ExitStack
    with ExitStack() as stack:
        mem = Memory(nc, stack, "all")
        x = mem.sbuf("x", [P, NT, D])
        ident = mem.sbuf("ident", [P, P])
        zeros = mem.sbuf("zeros", [P, D])
        slot = mem.sbuf("slot", [P, MIX3.k, NT], U32)
        score = mem.sbuf("score", [P, MIX3.k, NT])
        slots_x = nc.dram_tensor("slots_x", (MOST_SLOTS, D), F32, kind="Internal").ap()
        slots_y = nc.dram_tensor("slots_y", (MOST_SLOTS, D), F32, kind="Internal").ap()
        start_in = mem.sem("start_in")
        zeros_set = mem.sem("zeros_set")
        stored = mem.sem("stored")
        Memory.carried = mem.sem("carried")
        Memory.zeroed = mem.sem("zeroed")
        Memory.scattered = mem.sem("scattered")
        Memory.gathered = [mem.sem(f"gathered_{t}") for t in range(NT)]
        Memory.loaded = {mix.name: mem.sem(f"loaded_{mix.name}") for mix in (MIX0, MIX1, MIX3)}
        Memory.rounds = 0
        Memory.used = []
        with nc.Block() as block:
            @block.sync
            def _(sync):
                sync.dma_start(x[:], a["x"]).then_inc(start_in, 16)
                sync.dma_start(ident[:], a["ident"]).then_inc(start_in, 16)
                sync.wait_ge(zeros_set, 1)
                sync.dma_start(slots_x.rearrange("(n p) d -> p n d", p=P),
                               zeros[:].unsqueeze(1).to_broadcast([P, MOST_SLOTS // P, D])).then_inc(Memory.zeroed, 16)
                sync.wait_ge(start_in, 32)

            @block.vector
            def _(dve):
                nc.vector.memset(zeros[:], 0.0).then_inc(zeros_set, 1)
        with ExitStack() as layer:
            weights = mixture_weights(nc, a, MIX0, layer, slot, score)
            with ExitStack() as inner:
                m = Memory(nc, inner, "l0")
                xn_t = m.sbuf("xn_t", [P, B * S])
                cols = (m.sbuf("g_col", [P, TB, BH]), m.sbuf("e_col", [P, TB, BH]), m.sbuf("neg_g_row", [3, BH * S], BF16))
                mlstm_gates(nc, a, x, ident, xn_t, cols, weights.start_loads)
                mlstm_attention(nc, a, x, xn_t, cols)
            clear_semaphores(nc)
            mixture_layer(nc, a, x, ident, MIX0, weights, slots_x, slots_y)
        clear_semaphores(nc)

        with ExitStack() as layer:
            before, weights = weights, mixture_weights(nc, a, MIX1, layer, slot, score)
            heads_layer(nc, a, x, ident, HEADS1, MIX0, before, slots_y, weights.start_loads)
            clear_semaphores(nc)

            mixture_layer(nc, a, x, ident, MIX1, weights, slots_x, slots_y)
        clear_semaphores(nc)

        heads_layer(nc, a, x, ident, HEADS2, MIX1, weights, slots_y)
        clear_semaphores(nc)

        keyed_layer(nc, a, x, ident)
        clear_semaphores(nc)

        with ExitStack() as layer:
            weights = mixture_weights(nc, a, MIX3, layer, slot, score)
            one_head_layer(nc, a, x, ident, weights.start_loads)
            clear_semaphores(nc)

            mixture_layer(nc, a, x, ident, MIX3, weights, slots_x, slots_y)
        arriving = Arriving(nc, mem, MIX3, weights, slots_y)
        mixture_output(nc, x, out, arriving, stored)


def rows_by_tile(m):
    return m.reshape(NT, P, D).transpose(1, 0, 2)


def laid_out(v):
    g = {n: np.asarray(m) for n, m in v.items()}
    z = {}
    z["x"] = rows_by_tile(g["x"])
    z["ctx_n"] = rows_by_tile(g["ctx_1024"])
    z["ctx_t"] = g["ctx_1024"].transpose(2, 0, 1)
    z["ident"] = np.eye(P, dtype=np.float32)
    w = np.zeros((P, 3, 36), np.float32)
    w[:, :, 0:MH] = g["L0_xattn_w_igate"].reshape(MH, 3, D).transpose(2, 1, 0)
    w[:, :, 32:32 + MH] = g["L0_xattn_w_fgate"].reshape(MH, 3, D).transpose(2, 1, 0)
    z["w_gates"] = w
    z["b_gates"] = np.stack([np.repeat(g["L0_xattn_b_igate"], B), np.repeat(g["L0_xattn_b_fgate"], B)], axis=1)
    s = np.arange(S)
    z["causal"] = np.where(np.arange(P)[:, None] <= s[None, :], 0.0, -1e30).astype(np.float32)
    z["ln_scale"] = np.tile(g["L0_xattn_ln_weight"], (P, 1))
    z["before"] = np.triu(np.ones((P, P), np.float32), 1)
    z["iota_e"] = np.tile(np.arange(E, dtype=np.float32), (P, 1))
    z["keep"] = np.tile((np.arange(NT) > 0).astype(np.float32), (P, E, 1))
    z["tile_starts"] = np.tile(np.arange(NT, dtype=np.float32) * P, (P, 1))
    none = np.zeros(E, np.float32)
    for mix, router, biases, w1, w2 in (
            (MIX0, g["L0_ffn_gate_w"].T, (g["L0_ffn_gate_b"], g["L0_ffn_expert_bias"]), g["L0_ffn_w1"], g["L0_ffn_w2"]),
            (MIX1, g["L1_ffn_router_w"], (g["L1_ffn_router_b"], none), g["L1_ffn_w1"], g["L1_ffn_w2"]),
            (MIX3, g["L3_ffn_Wr"], (g["L3_ffn_br"], none), g["L3_ffn_W1"], g["L3_ffn_W2"])):
        n = mix.name
        z[n + "_router"] = router
        z[n + "_router_b"] = np.tile(np.stack(biases), (P, 1, 1))
        z[n + "_iota_s"] = np.tile(np.arange(mix.tiles, dtype=np.float32), (P, 1))
        z[n + "_w1"] = w1.transpose(1, 0, 2).reshape(P, E * mix.wide)
        z[n + "_w2"] = w2.reshape(E, mix.h // P, P, D).transpose(2, 0, 1, 3).reshape(P, E * mix.h)
    z["f0_b1"], z["f0_b2"] = g["L0_ffn_b1"].reshape(1, -1), g["L0_ffn_b2"].reshape(1, -1)
    z["f3_b1"], z["f3_b2"] = g["L3_ffn_b1"].reshape(1, -1), g["L3_ffn_b2"].reshape(1, -1)

    def slots(w):
        heads = w.reshape(-1, G, HG, HD)
        return np.concatenate([heads] * 3 + [np.zeros_like(heads)], axis=3).reshape(-1, G, P)

    z["ctx_t"] = g["ctx_1024"].transpose(2, 0, 1)
    row = np.arange(P) % SLOT
    low = np.stack([(row >= 2 * HD) & (row < 3 * HD), (row >= HD) & (row < 2 * HD)], axis=1).astype(np.float32)
    ones = ((row >= MAX_ROW) & (row < MAX_ROW + 2)).astype(np.float32)
    nil = np.zeros(D, np.float32)
    for n, q, k, v, o, bq, bk, bv, bo in (
            ("h1", *(g["L1_xattn_W_" + c].T for c in "qkvo"), nil, nil, nil, nil),
            ("h2", *(g["L2_xattn_W" + c].T for c in "qkvo"), *(g["L2_xattn_b" + c] for c in "qkvo"))):
        z[n + "_w_qk"] = np.stack([slots(q), slots(k)], axis=1)
        z[n + "_w_v"], z[n + "_w_o"] = v, o
        z[n + "_b_v"], z[n + "_b_o"] = np.tile(bv, (P, 1)), np.tile(bo, (P, 1))
        b = np.stack([slots(bq[None])[0].T, slots(bk[None])[0].T], axis=1)
        z[n + "_b_low"] = np.where(low[:, :, None] > 0, b, 0.0).astype(np.float32)
        b[:, 1] = np.where(ones[:, None] > 0, np.float32(1.0), b[:, 1])
        z[n + "_b_qk"] = b
        z[n + "_low"] = low
    mask = g["mask_1x1xSxS2_ik0"][0, 0]
    z["h1_mask"] = np.stack([mask.reshape(TB, P, S), mask.T.reshape(TB, P, S)]).transpose(2, 0, 1, 3)



    z["iota"] = np.tile(np.arange(PK, dtype=np.float32), (P, 1))
    z["pk_w_q"] = g["L2_ffn_Wq"].reshape(2 * PH, HALF, D).transpose(1, 0, 2)
    z["pk_keys"] = g["L2_ffn_keys"].transpose(3, 2, 0, 1).reshape(HALF, 2 * PH, PK)
    z["pk_down"] = np.concatenate([g["L2_ffn_down_embed"].reshape(EX, PK, D), g["L2_ffn_Wg"].reshape(MLP_BLOCKS, P, D),
                                   g["L2_ffn_Wu"].reshape(MLP_BLOCKS, P, D)]).transpose(2, 0, 1)
    z["pk_up"] = np.concatenate([g["L2_ffn_up_embed"].reshape(EX, PK, D),
                                 g["L2_ffn_Wd"].T.reshape(MLP_BLOCKS, P, D)]).transpose(1, 0, 2)

    z["k3_w"] = np.stack([g["L3_xattn_W" + c] for c in "qkvo"], axis=1)
    z["k3_b_qk"] = np.stack([g["L3_xattn_bq"], g["L3_xattn_bk"]], axis=1)
    z["k3_b_vo"] = np.tile(np.stack([g["L3_xattn_bv"], g["L3_xattn_bo"]]), (P, 1, 1))
    z["k3_mask"] = g["mask_BxS2_bk0"][None]
    return {n: np.ascontiguousarray(m) for n, m in z.items()}


def kernel(**inputs):
    import concourse.bacc as bacc
    from concourse.bass_utils import run_bass_kernel_spmd

    arrays = laid_out(inputs)
    nc = bacc.Bacc("TRN2", target_bir_lowering=False, num_devices=1)
    a = {n: nc.dram_tensor(f"in_{n}", m.shape, mybir.dt.from_np(m.dtype), kind="ExternalInput").ap()
         for n, m in arrays.items()}
    out = nc.dram_tensor("out_x", (P, NT, D), F32, kind="ExternalOutput").ap()
    build(nc, a, out)
    r = run_bass_kernel_spmd(nc, [{f"in_{n}": m for n, m in arrays.items()}], core_ids=[0])
    return r.results[0]["out_x"].transpose(1, 0, 2).reshape(B, S, D)
```
